# Optimizing a Trainium2 kernel written in Bass

```python
import numpy as np
import jax
import jax.numpy as jnp

def _softmax(x, axis=-1):
    return jax.nn.softmax(x, axis=axis)

def _gelu(x):
    return jax.nn.gelu(x, approximate=True)

def _silu(x):
    return jax.nn.silu(x)

def _sigmoid(x):
    return jax.nn.sigmoid(x)

def _layernorm(x, axis=-1, eps=1e-05):
    m = jnp.mean(x, axis=axis, keepdims=True)
    v = jnp.var(x, axis=axis, keepdims=True)
    return (x - m) / jnp.sqrt(v + eps)

def _scatter_add(tgt, idx, src, axis=0):
    return tgt.at[idx].add(src)

def _segment_sum(src, seg, n):
    return jax.ops.segment_sum(src, seg, n)
kernel_name = 'mk_gnn_resnorm_d4_gnn_r32_98007d'

def setup_inputs(seed: int=0):
    np.random.seed(seed)
    _w = jnp.asarray

    def _rec_inputs():
        import jax
        import jax.numpy as jnp
        _gk = jax.random.key(seed)
        x = -4.129e-06 + 0.1 * jax.random.normal(jax.random.fold_in(_gk, 1), (3125, 64), jnp.float32)
        _s = jax.random.randint(jax.random.fold_in(_gk, 2), (50000,), 0, 3125, jnp.int32)
        _d = jax.random.randint(jax.random.fold_in(_gk, 3), (50000,), 0, 3125, jnp.int32)
        _loop = jnp.arange(3125, dtype=jnp.int32)
        src = jnp.concatenate([_s, _d, _loop])
        dst = jnp.concatenate([_d, _s, _loop])
        _o = jnp.argsort(dst, stable=True)
        src = src[_o]
        dst = dst[_o]
        edge_attr_32 = -5.3897e-05 + 0.999841 * jax.random.normal(jax.random.fold_in(_gk, 12), (103125, 32), jnp.float32)
        edge_attr_64 = -8.16379e-05 + 0.999858 * jax.random.normal(jax.random.fold_in(_gk, 13), (103125, 64), jnp.float32)
        edge_type_200 = jax.random.randint(jax.random.fold_in(_gk, 15), (103125,), 0, 200, jnp.int32)
        edge_weight = jax.random.uniform(jax.random.fold_in(_gk, 16), (103125,), jnp.float32, 0.0, 0.999999)
        node_vec = jax.random.uniform(jax.random.fold_in(_gk, 17), (3125,), jnp.float32, 0.0, 0.999957)
        return (x, src, dst, edge_attr_32, edge_attr_64, edge_type_200, edge_weight, node_vec)
    x, src, dst, edge_attr_32, edge_attr_64, edge_type_200, edge_weight, node_vec = _rec_inputs()

    def _L0_gnn_setup():
        import jax, jax.numpy as jnp
        import numpy as np
        N_NODES = 3125
        N_REL = 200
        DIM = 64
        N_LAYERS = 2
        N_EDGES = 1250000

        def _compgcn_forward(node_emb, rel_emb, w_loop, w_fwd, w_bwd, edge_index, edge_type, edge_norm):
            half = N_REL // 2
            src, dst = (edge_index[0], edge_index[1])
            is_fwd = edge_type < half
            ridx = jnp.where(is_fwd, edge_type, edge_type - half)
            fmask = is_fwd.astype(node_emb.dtype)[:, None]
            bmask = 1.0 - fmask
            norm = edge_norm[:, None]
            x = node_emb
            for l in range(N_LAYERS):
                comp = x[src] * rel_emb[l][ridx]
                agg_f = jax.ops.segment_sum(comp * norm * fmask, dst, num_segments=N_NODES)
                agg_b = jax.ops.segment_sum(comp * norm * bmask, dst, num_segments=N_NODES)
                x = agg_f @ w_fwd[l] + agg_b @ w_bwd[l] + x @ w_loop[l]
                x = jax.nn.relu(x)
            return x
        key = jax.random.key(seed)
        ks = jax.random.split(key, 8)
        edge_index = jax.random.randint(ks[0], (2, N_EDGES), 0, N_NODES, dtype=jnp.int64)
        edge_type = jax.random.randint(ks[1], (N_EDGES,), 0, N_REL, dtype=jnp.int64)
        edge_norm = jax.random.uniform(ks[2], (N_EDGES,), dtype=jnp.float32)
        node_emb = jax.random.normal(ks[3], (N_NODES, DIM), dtype=jnp.float32) * 0.1
        rel_emb = jax.random.normal(ks[4], (N_LAYERS, N_REL, DIM), dtype=jnp.float32) * 0.1
        w_loop = jax.random.normal(ks[5], (N_LAYERS, DIM, DIM), dtype=jnp.float32) * (1.0 / np.sqrt(DIM))
        w_fwd = jax.random.normal(ks[6], (N_LAYERS, DIM, DIM), dtype=jnp.float32) * (1.0 / np.sqrt(DIM))
        w_bwd = jax.random.normal(ks[7], (N_LAYERS, DIM, DIM), dtype=jnp.float32) * (1.0 / np.sqrt(DIM))
        return {'node_emb': node_emb, 'rel_emb': rel_emb, 'w_loop': w_loop, 'w_fwd': w_fwd, 'w_bwd': w_bwd, 'edge_index': edge_index, 'edge_type': edge_type, 'edge_norm': edge_norm}
    _L0_gnn_all = _L0_gnn_setup()
    _L0_gnn_in = {k: v for k, v in _L0_gnn_all.items() if k in ('rel_emb', 'w_loop', 'w_fwd', 'w_bwd')}
    del _L0_gnn_all

    def _L1_gnn_setup():
        import jax, jax.numpy as jnp
        import numpy as np
        N_NODES, N_EDGES = (50000, 25000)
        NODE_DIM, EDGE_DIM, HIDDEN, NUM_LAYERS = (64, 32, 64, 2)
        IN_MSG = NODE_DIM + EDGE_DIM
        IN_UPD = NODE_DIM + HIDDEN
        key = jax.random.key(seed)
        ks = jax.random.split(key, 12)

        def w(k, shape, fan_in):
            return jax.random.normal(k, shape, jnp.float32) * (1.0 / np.sqrt(fan_in))
        return {'node_features': jax.random.normal(ks[0], (N_NODES, NODE_DIM), jnp.float32), 'edge_features': jax.random.normal(ks[1], (N_EDGES, EDGE_DIM), jnp.float32), 'msg_w1': w(ks[2], (NUM_LAYERS, IN_MSG, HIDDEN), IN_MSG), 'msg_b1': w(ks[3], (NUM_LAYERS, HIDDEN), IN_MSG), 'msg_w2': w(ks[4], (NUM_LAYERS, HIDDEN, HIDDEN), HIDDEN), 'msg_b2': w(ks[5], (NUM_LAYERS, HIDDEN), HIDDEN), 'upd_w1': w(ks[6], (IN_UPD, HIDDEN), IN_UPD), 'upd_b1': w(ks[7], (HIDDEN,), IN_UPD), 'upd_w2': w(ks[8], (HIDDEN, NODE_DIM), HIDDEN), 'upd_b2': w(ks[9], (NODE_DIM,), HIDDEN), 'src': jax.random.randint(ks[10], (N_EDGES,), 0, N_NODES, dtype=jnp.int32), 'dst': jax.random.randint(ks[11], (N_EDGES,), 0, N_NODES, dtype=jnp.int32)}
    _L1_gnn_all = _L1_gnn_setup()
    _L1_gnn_in = {k: v for k, v in _L1_gnn_all.items() if k in ('msg_w1', 'msg_b1', 'msg_w2', 'msg_b2', 'upd_w1', 'upd_b1', 'upd_w2', 'upd_b2')}
    del _L1_gnn_all

    def _L2_gnn_setup():
        import jax, jax.numpy as jnp
        import numpy as np
        N = 50000
        E = 25000
        D_IN = 64
        LD = 128
        HEADS = 8
        MAX_POS = 10000.0
        LRELU_SLOPE = 0.2
        BN_EPS = 1e-05

        def _pos_embed(t, channels):
            half = channels // 2
            freqs = jnp.arange(half, dtype=jnp.float32) / half
            freqs = (1.0 / MAX_POS) ** freqs
            x = t[:, None] * freqs[None, :]
            emb = jnp.concatenate([jnp.cos(x), jnp.sin(x)], axis=1)
            n = emb.shape[0]
            return jnp.flip(emb.reshape(n, 2, half), axis=1).reshape(n, channels)

        def _gat(x, src, dst, W, a_src, a_dst, bias, n_nodes):
            H, C = a_src.shape
            xw = (x @ W).reshape(n_nodes, H, C)
            al_s = jnp.einsum('nhc,hc->nh', xw, a_src)
            al_d = jnp.einsum('nhc,hc->nh', xw, a_dst)
            logits = jax.nn.leaky_relu(al_s[src] + al_d[dst], LRELU_SLOPE)
            m = jax.lax.stop_gradient(jax.ops.segment_max(logits, dst, num_segments=n_nodes))
            e = jnp.exp(logits - m[dst])
            denom = jax.ops.segment_sum(e, dst, num_segments=n_nodes)
            alpha = e / denom[dst]
            out = jax.ops.segment_sum(alpha[:, :, None] * xw[src], dst, num_segments=n_nodes)
            return out.reshape(n_nodes, H * C) + bias

        def _bn_train(x, g, b):
            mu = x.mean(axis=0)
            var = x.var(axis=0)
            return g * (x - mu) * jax.lax.rsqrt(var + BN_EPS) + b
        key = jax.random.key(seed)
        ks = jax.random.split(key, 32)
        p = lambda i, shape: jax.random.normal(ks[i], shape, dtype=jnp.float32) * 0.05
        inp = {'subgraph_x': jax.random.normal(ks[0], (N, D_IN), dtype=jnp.float32), 'edge_index': jax.random.randint(ks[1], (2, E), 0, N, dtype=jnp.int32), 'noise_labels': jax.random.uniform(ks[2], (N,), dtype=jnp.float32), 'init_w': p(3, (D_IN, LD)), 'init_b': jnp.zeros((LD,), jnp.float32), 'te_w1': p(4, (LD, LD)), 'te_b1': jnp.zeros((LD,), jnp.float32), 'te_w2': p(5, (LD, LD)), 'te_b2': jnp.zeros((LD,), jnp.float32)}
        dims = [(LD, 2 * LD), (2 * LD, 2 * LD), (2 * LD, LD)]
        for i, (din, dout) in enumerate(dims):
            c = dout // HEADS
            inp[f'gat_w{i}'] = p(6 + 4 * i, (din, dout))
            inp[f'att_src{i}'] = p(7 + 4 * i, (HEADS, c))
            inp[f'att_dst{i}'] = p(8 + 4 * i, (HEADS, c))
            inp[f'gat_b{i}'] = jnp.zeros((dout,), jnp.float32)
            inp[f'adj_w{i}'] = p(9 + 4 * i, (din, dout))
            inp[f'adj_b{i}'] = jnp.zeros((dout,), jnp.float32)
            inp[f'bn_g{i}'] = jnp.ones((dout,), jnp.float32)
            inp[f'bn_b{i}'] = jnp.zeros((dout,), jnp.float32)
        inp['out_w'] = p(20, (LD, D_IN))
        inp['out_b'] = jnp.zeros((D_IN,), jnp.float32)
        return inp
    _L2_gnn_all = _L2_gnn_setup()
    _L2_gnn_in = {k: v for k, v in _L2_gnn_all.items() if k in ('init_w', 'init_b', 'te_w1', 'te_b1', 'te_w2', 'te_b2', 'gat_w0', 'att_src0', 'att_dst0', 'gat_b0', 'adj_w0', 'adj_b0', 'bn_g0', 'bn_b0', 'gat_w1', 'att_src1', 'att_dst1', 'gat_b1', 'adj_w1', 'adj_b1', 'bn_g1', 'bn_b1', 'gat_w2', 'att_src2', 'att_dst2', 'gat_b2', 'adj_w2', 'adj_b2', 'bn_g2', 'bn_b2', 'out_w', 'out_b')}
    del _L2_gnn_all

    def _L3_gnn_setup():
        import jax, jax.numpy as jnp
        import numpy as np
        N = 3125
        NE = 50000
        IN_DIM = 64
        OUT_DIM = 64
        H = 8
        D = OUT_DIM // H
        key = jax.random.key(seed)
        ks = jax.random.split(key, 12)
        s = 1.0 / np.sqrt(IN_DIM)
        x = jax.random.normal(ks[0], (N, IN_DIM), jnp.float32)
        edge_attr = jax.random.normal(ks[1], (NE, IN_DIM), jnp.float32)
        edge_index = jax.random.randint(ks[2], (2, NE), 0, N, dtype=jnp.int32)
        WQ = jax.random.normal(ks[3], (IN_DIM, OUT_DIM), jnp.float32) * s
        WK = jax.random.normal(ks[4], (IN_DIM, OUT_DIM), jnp.float32) * s
        WE = jax.random.normal(ks[5], (IN_DIM, OUT_DIM), jnp.float32) * s
        WV = jax.random.normal(ks[6], (IN_DIM, OUT_DIM), jnp.float32) * s
        bQ = jax.random.normal(ks[7], (OUT_DIM,), jnp.float32) * 0.01
        bK = jax.random.normal(ks[8], (OUT_DIM,), jnp.float32) * 0.01
        bE = jax.random.normal(ks[9], (OUT_DIM,), jnp.float32) * 0.01
        bV = jax.random.normal(ks[10], (OUT_DIM,), jnp.float32) * 0.01
        return {'x': x, 'edge_attr': edge_attr, 'edge_index': edge_index, 'WQ': WQ, 'bQ': bQ, 'WK': WK, 'bK': bK, 'WE': WE, 'bE': bE, 'WV': WV, 'bV': bV}
    _L3_gnn_all = _L3_gnn_setup()
    _L3_gnn_in = {k: v for k, v in _L3_gnn_all.items() if k in ('WQ', 'bQ', 'WK', 'bK', 'WE', 'bE', 'WV', 'bV')}
    del _L3_gnn_all
    return {'x': x, 'src': src, 'dst': dst, 'edge_attr_32': edge_attr_32, 'edge_attr_64': edge_attr_64, 'edge_type_200': edge_type_200, 'edge_weight': edge_weight, 'node_vec': node_vec, 'L0_gnn_rel_emb': _L0_gnn_in['rel_emb'], 'L0_gnn_w_loop': _L0_gnn_in['w_loop'], 'L0_gnn_w_fwd': _L0_gnn_in['w_fwd'], 'L0_gnn_w_bwd': _L0_gnn_in['w_bwd'], 'L1_gnn_msg_w1': _L1_gnn_in['msg_w1'], 'L1_gnn_msg_b1': _L1_gnn_in['msg_b1'], 'L1_gnn_msg_w2': _L1_gnn_in['msg_w2'], 'L1_gnn_msg_b2': _L1_gnn_in['msg_b2'], 'L1_gnn_upd_w1': _L1_gnn_in['upd_w1'], 'L1_gnn_upd_b1': _L1_gnn_in['upd_b1'], 'L1_gnn_upd_w2': _L1_gnn_in['upd_w2'], 'L1_gnn_upd_b2': _L1_gnn_in['upd_b2'], 'L2_gnn_init_w': _L2_gnn_in['init_w'], 'L2_gnn_init_b': _L2_gnn_in['init_b'], 'L2_gnn_te_w1': _L2_gnn_in['te_w1'], 'L2_gnn_te_b1': _L2_gnn_in['te_b1'], 'L2_gnn_te_w2': _L2_gnn_in['te_w2'], 'L2_gnn_te_b2': _L2_gnn_in['te_b2'], 'L2_gnn_gat_w0': _L2_gnn_in['gat_w0'], 'L2_gnn_att_src0': _L2_gnn_in['att_src0'], 'L2_gnn_att_dst0': _L2_gnn_in['att_dst0'], 'L2_gnn_gat_b0': _L2_gnn_in['gat_b0'], 'L2_gnn_adj_w0': _L2_gnn_in['adj_w0'], 'L2_gnn_adj_b0': _L2_gnn_in['adj_b0'], 'L2_gnn_bn_g0': _L2_gnn_in['bn_g0'], 'L2_gnn_bn_b0': _L2_gnn_in['bn_b0'], 'L2_gnn_gat_w1': _L2_gnn_in['gat_w1'], 'L2_gnn_att_src1': _L2_gnn_in['att_src1'], 'L2_gnn_att_dst1': _L2_gnn_in['att_dst1'], 'L2_gnn_gat_b1': _L2_gnn_in['gat_b1'], 'L2_gnn_adj_w1': _L2_gnn_in['adj_w1'], 'L2_gnn_adj_b1': _L2_gnn_in['adj_b1'], 'L2_gnn_bn_g1': _L2_gnn_in['bn_g1'], 'L2_gnn_bn_b1': _L2_gnn_in['bn_b1'], 'L2_gnn_gat_w2': _L2_gnn_in['gat_w2'], 'L2_gnn_att_src2': _L2_gnn_in['att_src2'], 'L2_gnn_att_dst2': _L2_gnn_in['att_dst2'], 'L2_gnn_gat_b2': _L2_gnn_in['gat_b2'], 'L2_gnn_adj_w2': _L2_gnn_in['adj_w2'], 'L2_gnn_adj_b2': _L2_gnn_in['adj_b2'], 'L2_gnn_bn_g2': _L2_gnn_in['bn_g2'], 'L2_gnn_bn_b2': _L2_gnn_in['bn_b2'], 'L2_gnn_out_w': _L2_gnn_in['out_w'], 'L2_gnn_out_b': _L2_gnn_in['out_b'], 'L3_gnn_WQ': _L3_gnn_in['WQ'], 'L3_gnn_bQ': _L3_gnn_in['bQ'], 'L3_gnn_WK': _L3_gnn_in['WK'], 'L3_gnn_bK': _L3_gnn_in['bK'], 'L3_gnn_WE': _L3_gnn_in['WE'], 'L3_gnn_bE': _L3_gnn_in['bE'], 'L3_gnn_WV': _L3_gnn_in['WV'], 'L3_gnn_bV': _L3_gnn_in['bV']}

def reference(x, src, dst, edge_attr_32, edge_attr_64, edge_type_200, edge_weight, node_vec, L0_gnn_rel_emb, L0_gnn_w_loop, L0_gnn_w_fwd, L0_gnn_w_bwd, L1_gnn_msg_w1, L1_gnn_msg_b1, L1_gnn_msg_w2, L1_gnn_msg_b2, L1_gnn_upd_w1, L1_gnn_upd_b1, L1_gnn_upd_w2, L1_gnn_upd_b2, L2_gnn_init_w, L2_gnn_init_b, L2_gnn_te_w1, L2_gnn_te_b1, L2_gnn_te_w2, L2_gnn_te_b2, L2_gnn_gat_w0, L2_gnn_att_src0, L2_gnn_att_dst0, L2_gnn_gat_b0, L2_gnn_adj_w0, L2_gnn_adj_b0, L2_gnn_bn_g0, L2_gnn_bn_b0, L2_gnn_gat_w1, L2_gnn_att_src1, L2_gnn_att_dst1, L2_gnn_gat_b1, L2_gnn_adj_w1, L2_gnn_adj_b1, L2_gnn_bn_g1, L2_gnn_bn_b1, L2_gnn_gat_w2, L2_gnn_att_src2, L2_gnn_att_dst2, L2_gnn_gat_b2, L2_gnn_adj_w2, L2_gnn_adj_b2, L2_gnn_bn_g2, L2_gnn_bn_b2, L2_gnn_out_w, L2_gnn_out_b, L3_gnn_WQ, L3_gnn_bQ, L3_gnn_WK, L3_gnn_bK, L3_gnn_WE, L3_gnn_bE, L3_gnn_WV, L3_gnn_bV):
    import jax
    import jax.numpy as jnp

    def _L0_gnn_ref(node_emb, rel_emb, w_loop, w_fwd, w_bwd, edge_index, edge_type, edge_norm):
        import jax, jax.numpy as jnp
        import numpy as np
        N_NODES = 3125
        N_REL = 200
        DIM = 64
        N_LAYERS = 2
        N_EDGES = 1250000

        def _compgcn_forward(node_emb, rel_emb, w_loop, w_fwd, w_bwd, edge_index, edge_type, edge_norm):
            half = N_REL // 2
            src, dst = (edge_index[0], edge_index[1])
            is_fwd = edge_type < half
            ridx = jnp.where(is_fwd, edge_type, edge_type - half)
            fmask = is_fwd.astype(node_emb.dtype)[:, None]
            bmask = 1.0 - fmask
            norm = edge_norm[:, None]
            x = node_emb
            for l in range(N_LAYERS):
                comp = x[src] * rel_emb[l][ridx]
                agg_f = jax.ops.segment_sum(comp * norm * fmask, dst, num_segments=N_NODES)
                agg_b = jax.ops.segment_sum(comp * norm * bmask, dst, num_segments=N_NODES)
                x = agg_f @ w_fwd[l] + agg_b @ w_bwd[l] + x @ w_loop[l]
                x = jax.nn.relu(x)
            return x
        return _compgcn_forward(node_emb, rel_emb, w_loop, w_fwd, w_bwd, edge_index, edge_type, edge_norm)

    def _L1_gnn_ref(node_features, edge_features, msg_w1, msg_b1, msg_w2, msg_b2, upd_w1, upd_b1, upd_w2, upd_b2, src, dst):
        import jax, jax.numpy as jnp
        import numpy as np
        N_NODES, N_EDGES = (50000, 25000)
        NODE_DIM, EDGE_DIM, HIDDEN, NUM_LAYERS = (64, 32, 64, 2)
        IN_MSG = NODE_DIM + EDGE_DIM
        IN_UPD = NODE_DIM + HIDDEN
        n_nodes = node_features.shape[0]
        combined = jnp.concatenate([node_features[src], edge_features], axis=-1)
        msg = jnp.zeros((combined.shape[0], msg_w2.shape[-1]), combined.dtype)
        for l in range(msg_w1.shape[0]):
            h = jax.nn.relu(combined @ msg_w1[l] + msg_b1[l])
            msg = msg + (h @ msg_w2[l] + msg_b2[l])
        agg = jax.ops.segment_sum(msg, dst, num_segments=n_nodes)
        deg = jax.ops.segment_sum(jnp.ones((dst.shape[0],), msg.dtype), dst, num_segments=n_nodes)
        agg = agg / (deg[:, None] + 1e-08)
        comb2 = jnp.concatenate([node_features, agg], axis=-1)
        return jax.nn.relu(comb2 @ upd_w1 + upd_b1) @ upd_w2 + upd_b2

    def _L2_gnn_ref(subgraph_x, edge_index, noise_labels, init_w, init_b, te_w1, te_b1, te_w2, te_b2, gat_w0, att_src0, att_dst0, gat_b0, adj_w0, adj_b0, bn_g0, bn_b0, gat_w1, att_src1, att_dst1, gat_b1, adj_w1, adj_b1, bn_g1, bn_b1, gat_w2, att_src2, att_dst2, gat_b2, adj_w2, adj_b2, bn_g2, bn_b2, out_w, out_b):
        import jax, jax.numpy as jnp
        import numpy as np
        N = 50000
        E = 25000
        D_IN = 64
        LD = 128
        HEADS = 8
        MAX_POS = 10000.0
        LRELU_SLOPE = 0.2
        BN_EPS = 1e-05

        def _pos_embed(t, channels):
            half = channels // 2
            freqs = jnp.arange(half, dtype=jnp.float32) / half
            freqs = (1.0 / MAX_POS) ** freqs
            x = t[:, None] * freqs[None, :]
            emb = jnp.concatenate([jnp.cos(x), jnp.sin(x)], axis=1)
            n = emb.shape[0]
            return jnp.flip(emb.reshape(n, 2, half), axis=1).reshape(n, channels)

        def _gat(x, src, dst, W, a_src, a_dst, bias, n_nodes):
            H, C = a_src.shape
            xw = (x @ W).reshape(n_nodes, H, C)
            al_s = jnp.einsum('nhc,hc->nh', xw, a_src)
            al_d = jnp.einsum('nhc,hc->nh', xw, a_dst)
            logits = jax.nn.leaky_relu(al_s[src] + al_d[dst], LRELU_SLOPE)
            m = jax.lax.stop_gradient(jax.ops.segment_max(logits, dst, num_segments=n_nodes))
            e = jnp.exp(logits - m[dst])
            denom = jax.ops.segment_sum(e, dst, num_segments=n_nodes)
            alpha = e / denom[dst]
            out = jax.ops.segment_sum(alpha[:, :, None] * xw[src], dst, num_segments=n_nodes)
            return out.reshape(n_nodes, H * C) + bias

        def _bn_train(x, g, b):
            mu = x.mean(axis=0)
            var = x.var(axis=0)
            return g * (x - mu) * jax.lax.rsqrt(var + BN_EPS) + b
        n = subgraph_x.shape[0]
        self_idx = jnp.arange(n, dtype=edge_index.dtype)
        src = jnp.concatenate([edge_index[0], self_idx])
        dst = jnp.concatenate([edge_index[1], self_idx])
        emb = _pos_embed(noise_labels, LD)
        emb = jax.nn.silu(emb @ te_w1 + te_b1) @ te_w2 + te_b2
        x = subgraph_x @ init_w + init_b + emb
        layers = [(gat_w0, att_src0, att_dst0, gat_b0, adj_w0, adj_b0, bn_g0, bn_b0), (gat_w1, att_src1, att_dst1, gat_b1, adj_w1, adj_b1, bn_g1, bn_b1), (gat_w2, att_src2, att_dst2, gat_b2, adj_w2, adj_b2, bn_g2, bn_b2)]
        for gw, a_s, a_d, gb, aw, ab, g, b in layers:
            res = x @ aw + ab
            x = _gat(x, src, dst, gw, a_s, a_d, gb, n) + res
            x = jax.nn.silu(_bn_train(x, g, b))
        return x @ out_w + out_b

    def _L3_gnn_ref(x, edge_attr, edge_index, WQ, bQ, WK, bK, WE, bE, WV, bV):
        import jax, jax.numpy as jnp
        import numpy as np
        N = 3125
        NE = 50000
        IN_DIM = 64
        OUT_DIM = 64
        H = 8
        D = OUT_DIM // H
        n = x.shape[0]
        Qh = (x @ WQ + bQ).reshape(n, H, D)
        Kh = (x @ WK + bK).reshape(n, H, D)
        Vh = (x @ WV + bV).reshape(n, H, D)
        Eh = (edge_attr @ WE + bE).reshape(-1, H, D)
        src = edge_index[0]
        dst = edge_index[1]
        inv_sqrt_d = jnp.float32(1.0 / np.sqrt(D))
        score = Kh[src] * Qh[dst] * inv_sqrt_d * Eh
        score = jnp.exp(jnp.clip(score.sum(-1, keepdims=True), -5.0, 5.0))
        msg = Vh[src] * score
        wV = jax.ops.segment_sum(msg, dst, num_segments=n)
        return wV.reshape(n, H * D)
    edge_index = jnp.stack([src, dst])
    x = _layernorm(x + _L0_gnn_ref(x, L0_gnn_rel_emb, L0_gnn_w_loop, L0_gnn_w_fwd, L0_gnn_w_bwd, edge_index, edge_type_200, edge_weight), axis=-1)
    x = _layernorm(x + _L1_gnn_ref(x, edge_attr_32, L1_gnn_msg_w1, L1_gnn_msg_b1, L1_gnn_msg_w2, L1_gnn_msg_b2, L1_gnn_upd_w1, L1_gnn_upd_b1, L1_gnn_upd_w2, L1_gnn_upd_b2, src, dst), axis=-1)
    x = _layernorm(x + _L2_gnn_ref(x, edge_index, node_vec, L2_gnn_init_w, L2_gnn_init_b, L2_gnn_te_w1, L2_gnn_te_b1, L2_gnn_te_w2, L2_gnn_te_b2, L2_gnn_gat_w0, L2_gnn_att_src0, L2_gnn_att_dst0, L2_gnn_gat_b0, L2_gnn_adj_w0, L2_gnn_adj_b0, L2_gnn_bn_g0, L2_gnn_bn_b0, L2_gnn_gat_w1, L2_gnn_att_src1, L2_gnn_att_dst1, L2_gnn_gat_b1, L2_gnn_adj_w1, L2_gnn_adj_b1, L2_gnn_bn_g1, L2_gnn_bn_b1, L2_gnn_gat_w2, L2_gnn_att_src2, L2_gnn_att_dst2, L2_gnn_gat_b2, L2_gnn_adj_w2, L2_gnn_adj_b2, L2_gnn_bn_g2, L2_gnn_bn_b2, L2_gnn_out_w, L2_gnn_out_b), axis=-1)
    x = _layernorm(x + _L3_gnn_ref(x, edge_attr_64, edge_index, L3_gnn_WQ, L3_gnn_bQ, L3_gnn_WK, L3_gnn_bK, L3_gnn_WE, L3_gnn_bE, L3_gnn_WV, L3_gnn_bV), axis=-1)
    return x

_drawn_inputs = setup_inputs


def setup_inputs(seed=0):
    import zlib

    import numpy as np

    out = dict(_drawn_inputs(seed))
    spreads = {'L2_gnn_init_b': (0.0, 0.8),
     'L2_gnn_te_b1': (0.0, 0.8),
     'L2_gnn_te_b2': (0.0, 0.8),
     'L2_gnn_gat_b0': (0.0, 0.8),
     'L2_gnn_adj_b0': (0.0, 0.8),
     'L2_gnn_bn_g0': (1.0, 0.2),
     'L2_gnn_bn_b0': (0.0, 0.1),
     'L2_gnn_gat_b1': (0.0, 0.8),
     'L2_gnn_adj_b1': (0.0, 0.8),
     'L2_gnn_bn_g1': (1.0, 0.2),
     'L2_gnn_bn_b1': (0.0, 0.279),
     'L2_gnn_gat_b2': (0.0, 0.8),
     'L2_gnn_adj_b2': (0.0, 0.8),
     'L2_gnn_bn_g2': (1.0, 0.2),
     'L2_gnn_bn_b2': (0.0, 0.1),
     'L2_gnn_out_b': (0.0, 0.1)}
    factors = {'node_vec': 3.978,
     'L2_gnn_te_w1': 3.615,
     'L2_gnn_te_w2': 4.079,
     'L2_gnn_att_src0': 8.0,
     'L2_gnn_att_dst0': 8.0,
     'L2_gnn_att_src1': 5.519,
     'L2_gnn_att_dst1': 8.0,
     'L2_gnn_att_src2': 8.0,
     'L2_gnn_att_dst2': 8.0,
     'L3_gnn_bQ': 6.86,
     'L3_gnn_bK': 7.715,
     'L3_gnn_bE': 5.855,
     'L3_gnn_bV': 2.809}
    for name, (base, spread) in spreads.items():
        noise = np.random.default_rng([zlib.crc32(name.encode()), seed]).standard_normal(out[name].shape)
        drawn = base * np.exp(spread * noise) if base else spread * noise
        out[name] = jnp.asarray(drawn.astype(out[name].dtype))
    for name, factor in factors.items():
        out[name] = (out[name] * factor).astype(out[name].dtype)
    return out
```

```python
from contextlib import ExitStack

import numpy as np
import concourse.bass as bass
from concourse import mybir

F32 = mybir.dt.float32
I32 = mybir.dt.int32
ALU = mybir.AluOpType
ACT = mybir.ActivationFunctionType
AX = mybir.AxisListType

P = 128
N, E, DIM = 3125, 103125, 64
NB = -(-N // P)
NP = NB * P
BATCH = 4
NI = -(-((E + NB * (P - 1)) // P) // (2 * BATCH)) * 2 * BATCH
LOOPS = NI // (2 * BATCH)
KI = -(-NI // P)
NIP = KI * P
ER, EC = 125, E // 125
HALF_REL = 100
HEADS = 8
FAR = -1.0e30
CHUNK = 512
ds = bass.ds


class Mem:
    pass


def build(nc, a, out, debug=None):
    m = Mem()
    m.norms = 0
    with ExitStack() as ctx:
        def sb(name, shape, dt=F32):
            return ctx.enter_context(nc.sbuf_tensor(name, shape, dt))

        def dram(name, shape, dt=F32):
            return nc.dram_tensor(name, shape, dt, kind="Internal").ap()

        m.item_first = dram("item_first", [NIP], I32)
        m.item_block = dram("item_block", [NIP], I32)
        m.edge_rows = dram("edge_rows", [3, NIP, P], I32)
        m.weight_rows = dram("weight_rows", [NIP, P])
        m.dst_rows = dram("dst_rows", [NIP, P])
        m.rel_rows = dram("rel_rows", [NIP, P])
        m.run_rows = dram("run_rows", [NIP, P])
        m.x_table = dram("x_table", [NP, DIM])
        m.pre_table = dram("pre_table", [NP, 2 * DIM])
        m.xw_table = dram("xw_table", [NP, 264])
        m.xw_table2 = dram("xw_table2", [NP, 136])
        m.al_table = dram("al_table", [NP, HEADS])

        m.ident = sb("ident", [P, P])
        m.iota_row = sb("iota_row", [P, P])
        m.iota_col = sb("iota_col", [P, 1])
        m.ones = sb("ones", [P, P])
        m.src_i = sb("src_i", [P, NIP], I32)
        m.dst_l = sb("dst_l", [P, NIP])
        m.w_fwd = sb("w_fwd", [P, NIP])
        m.w_bwd = sb("w_bwd", [P, NIP])
        m.run_end = sb("run_end", [P, NIP])
        m.late = sb("late", [P, KI])
        m.blk_col = sb("blk_col", [P, KI])
        m.first_tab = sb("first_tab", [1, NIP], I32)
        m.block_tab = sb("block_tab", [1, NIP], I32)
        m.x = sb("x", [P, NB, DIM])
        m.acc = sb("acc", [P, NB, 264])
        m.ps = [ctx.enter_context(nc.psum_tensor(f"bank{i}", [P, 512], F32)) for i in range(8)]

        constants(nc, m)
        item_tables(nc, m, a)
        edge_columns(nc, m, a)
        load_nodes(nc, m, a)
        if debug == "prep":
            return finish(nc, m, out)
        with ExitStack() as c:
            m.y = c.enter_context(nc.sbuf_tensor("y", [P, NB, DIM], F32))
            compgcn_pass(nc, m, a, 0, a["x"], m.x)
            compgcn_nodes(nc, m, a, 0, m.x, m.y)
            compgcn_pass(nc, m, a, 1, m.x_table, m.y)
            compgcn_nodes(nc, m, a, 1, m.y, m.y)
            residual_norm(nc, m, m.y)
        if debug == "L0":
            return finish(nc, m, out)
        message_tables(nc, m, a)
        message_pass(nc, m, a)
        message_nodes(nc, m, a)
        if debug == "L1":
            return finish(nc, m, out)
        with ExitStack() as c:
            def cb(name, shape):
                return c.enter_context(nc.sbuf_tensor(name, shape, F32))
            m.ft = cb("ft", [P, 2, NP])
            m.ft2 = cb("ft2", [P, 2, NP])
            m.node_out = cb("node_out", [P, NB, 272])
            m.al_max = cb("al_max", [P, NB, HEADS])
            m.dst_tab = cb("dst_tab", [P, NB, 2 * HEADS])
            cur, nxt = m.ft, m.ft2
            diffusion_embed(nc, m, a, cur)
            for layer in range(3):
                gat_tables(nc, m, a, layer, cur)
                gat_max_pass(nc, m, layer)
                gat_self_loops(nc, m, layer)
                gat_sum_pass(nc, m, layer)
                gat_nodes(nc, m, a, layer, cur, nxt)
                cur, nxt = nxt, cur
            diffusion_out(nc, m, a, cur)
        if debug == "L2":
            return finish(nc, m, out)
        with ExitStack() as c:
            m.q_tab = c.enter_context(nc.sbuf_tensor("q_tab", [P, NB, DIM], F32))
            attention_tables(nc, m, a)
            attention_pass(nc, m, a)
        residual_norm(nc, m, m.acc[:, :, 0:DIM])
        finish(nc, m, out)


class Stage:

    def __init__(self, nc, name):
        self.nc, self.name, self.stack, self.sems = nc, name, ExitStack(), []

    def sem(self, name):
        s = self.nc.alloc_semaphore(f"{self.name}_{name}")
        self.sems.append(s)
        return s

    def pair(self, name):
        return [self.sem(f"{name}_{q}") for q in range(2)]

    def sb(self, name, shape, dt=F32):
        return self.stack.enter_context(self.nc.sbuf_tensor(f"{self.name}_{name}", shape, dt))

    def pair_sb(self, name, shape, dt=F32):
        return [self.sb(f"{name}_{q}", shape, dt) for q in range(2)]

    def __enter__(self):
        return self

    def __exit__(self, *e):
        if e[0] is None:
            self.nc.clear_and_free_semaphores(self.sems)
            self.nc.all_engine_barrier()
        self.stack.close()


def spread(ap, count):
    return ap.unsqueeze(2).to_broadcast([ap.shape[0], ap.shape[1], count])


def repeat(ap, count):
    return ap.unsqueeze(1).to_broadcast([ap.shape[0], count, ap.shape[1]])


def constants(nc, m):
    with Stage(nc, "const") as st:
        made = st.sem("const_made")
        zeroed = st.sem("ident_zeroed")
        with nc.Block() as block:
            @block.gpsimd
            def _(pool):
                pool.iota(m.iota_row[:, :], [[1, P]], base=0, channel_multiplier=0,
                          allow_small_or_imprecise_dtypes=True).then_inc(made, 1)
                pool.iota(m.iota_col[:, :], [[1, 1]], base=0, channel_multiplier=1,
                          allow_small_or_imprecise_dtypes=True).then_inc(made, 1)
                pool.memset(m.ident[:, :], 0.0).then_inc(zeroed, 1)
                pool.wait_ge(zeroed, 1)
                pool.affine_select(out=m.ident[:, :], in_=m.ident[:, :], compare_op=ALU.not_equal, fill=1.0,
                                   base=0, pattern=[[-1, P]], channel_multiplier=1).then_inc(made, 1)

            @block.vector
            def _(dve):
                dve.memset(m.ones[:, :], 1.0).then_inc(made, 1)


def item_tables(nc, m, a):
    with Stage(nc, "items") as st:
        loaded, cast, counted, totals = st.sem("dst_loaded"), st.sem("dst_cast"), st.sem("counted"), st.sem("totals")
        step, idx_made, stored, back = st.sem("step"), st.sem("ids_made"), st.sem("tables_stored"), st.sem("tables_back")
        di, df, hit = st.sb("dst_int", [ER, EC], I32), st.sb("dst_f", [ER, EC]), st.sb("below", [ER, EC])
        cnt = st.sb("below_count", [ER, NB + 1])
        first = st.sb("first_edge", [P, NB + 1])
        n_e, n_ii = st.sb("edges_of", [P, NB]), st.sb("items_int", [P, NB], I32)
        n_i, base = st.sb("items_of", [P, NB]), st.sb("items_to", [P, NB + 1])
        lag, dlag = st.sb("lag", [P, NB]), st.sb("dlag", [P, NB])
        ids, blk, e0, past = (st.sb(n, [P, KI]) for n in ("ids", "blk", "nominal", "past"))
        tab_f, tab_b = st.sb("tab_f", [P, KI], I32), st.sb("tab_b", [P, KI], I32)
        clip = st.sb("clipped", [P, KI])
        tot = m.ps[0]
        with nc.Block() as block:
            @block.sync
            def _(sp):
                sp.dma_start(di[:, :], a["edges"][1, :].rearrange("(p c) -> p c", p=ER)).then_inc(loaded, 16)
                sp.wait_ge(stored, 1)
                with nc.allow_non_contiguous_dma(reason="two small tables"):
                    sp.dma_start(m.item_first.rearrange("(k p) -> p k", p=P), tab_f[:, :]).then_inc(back, 16)
                    sp.dma_start(m.item_block.rearrange("(k p) -> p k", p=P), tab_b[:, :]).then_inc(back, 16)
                sp.wait_ge(back, 32)
                sp.dma_start(m.first_tab[:, :], m.item_first.unsqueeze(0)).then_inc(back, 16)
                sp.dma_start(m.block_tab[:, :], m.item_block.unsqueeze(0)).then_inc(back, 16)
                sp.wait_ge(back, 64)

            @block.gpsimd
            def _(pool):
                pool.iota(ids[:, :], [[P, KI]], base=0, channel_multiplier=1,
                          allow_small_or_imprecise_dtypes=True).then_inc(idx_made, 1)

            @block.vector
            def _(dve):
                n = [0]

                def then(ins):
                    n[0] += 1
                    ins.then_inc(step, 1)
                    dve.wait_ge(step, n[0])

                dve.wait_ge(loaded, 16)
                dve.memset(cnt[:, :], 0.0).then_inc(cast, 1)
                dve.tensor_copy(df[:, :], di[:, :]).then_inc(cast, 1)
                dve.wait_ge(cast, 2)
                for b in range(1, NB):
                    then(dve.tensor_scalar(hit[:, :], df[:, :], float(P * b), 0.0, ALU.is_lt, ALU.add,
                                           accum_out=cnt[:, b:b + 1]))
                dve.memset(cnt[:, NB:NB + 1], float(EC)).then_inc(counted, 1)
                dve.wait_ge(totals, 1)
                then(dve.tensor_copy(first[:, :], tot[:, 0:NB + 1]))
                then(dve.tensor_tensor(n_e[:, :], first[:, 1:NB + 1], first[:, 0:NB], ALU.subtract))
                then(dve.tensor_scalar(n_ii[:, :], n_e[:, :], float(P - 1), None, ALU.add))
                then(dve.tensor_single_scalar(n_ii[:, :], n_ii[:, :], P.bit_length() - 1, ALU.arith_shift_right))
                then(dve.tensor_copy(n_i[:, :], n_ii[:, :]))
                then(dve.memset(base[:, 0:1], 0.0))
                then(dve.tensor_tensor_scan(base[:, 1:NB + 1], m.ones[:, 0:NB], n_i[:, :], 0.0, ALU.mult, ALU.add))
                then(dve.scalar_tensor_tensor(lag[:, :], base[:, 0:NB], float(-P), first[:, 0:NB], ALU.mult, ALU.add))
                then(dve.tensor_tensor(dlag[:, 1:NB], lag[:, 1:NB], lag[:, 0:NB - 1], ALU.subtract))
                dve.wait_ge(idx_made, 1)
                then(dve.memset(blk[:, :], 0.0))
                then(dve.tensor_scalar(e0[:, :], ids[:, :], float(P), lag[:, 0:1], ALU.mult, ALU.add))
                for b in range(1, NB):
                    then(dve.tensor_scalar(past[:, :], ids[:, :], base[:, b:b + 1], None, ALU.is_ge))
                    then(dve.tensor_tensor(blk[:, :], blk[:, :], past[:, :], ALU.add))
                    then(dve.scalar_tensor_tensor(e0[:, :], past[:, :], dlag[:, b:b + 1], e0[:, :], ALU.mult, ALU.add))
                then(dve.tensor_scalar(past[:, :], ids[:, :], base[:, NB:NB + 1], float(E), ALU.is_ge, ALU.mult))
                then(dve.tensor_tensor(e0[:, :], e0[:, :], past[:, :], ALU.add))
                then(dve.tensor_scalar(clip[:, :], e0[:, :], float(E - P), None, ALU.min))
                then(dve.tensor_tensor(m.late[:, :], e0[:, :], clip[:, :], ALU.subtract))
                then(dve.tensor_copy(m.blk_col[:, :], blk[:, :]))
                then(dve.tensor_copy(tab_f[:, :], clip[:, :]))
                dve.tensor_copy(tab_b[:, :], blk[:, :]).then_inc(stored, 1)

            @block.tensor
            def _(pe):
                pe.wait_ge(counted, 1)
                pe.matmul(tot[:, 0:NB + 1], m.ones[0:ER, :], cnt[:, :], start=True, stop=True).then_inc(totals, 1)


def edge_columns(nc, m, a):
    UN = 4
    with Stage(nc, "cols") as st:
        copied, wcopied, rowed = st.sem("rows_copied"), st.sem("weights_copied"), st.sem("rows_loaded")
        ready, turned, kept, wrote = st.sem("rows_ready"), st.sem("turned"), st.sem("kept"), st.sem("rows_written")
        step = st.sem("step")
        ri = st.sb("int_rows", [P, KI, 3, P], I32)
        rw = st.sb("weight_rows", [P, KI, P])
        src, dst, rel = (st.sb(n, [P, KI, P]) for n in ("src", "dst", "rel"))
        wf, wb, end, run = (st.sb(n, [P, KI, P]) for n in ("wf", "wb", "end", "run"))
        tmp = st.sb("tmp", [P, KI, P])
        weights = a["edge_weight"].unsqueeze(0)
        with nc.Block() as block:
            @block.sync
            def _(sp):
                with sp.Fori(0, NIP // UN) as i:
                    for u in range(UN):
                        e = sp.value_load(m.first_tab[0:1, ds(i * UN + u, 1)], min_val=0, max_val=E - P)
                        sp.dma_start(m.edge_rows[:, ds(i * UN + u, 1), :],
                                     a["edges"][:, ds(e, P)].unsqueeze(1)).then_inc(copied, 16)
                sp.wait_ge(copied, 16 * NIP)
                for k in range(KI):
                    sp.dma_start(ri[:, k, :, :], m.edge_rows[:, k * P:(k + 1) * P, :].rearrange("t p e -> p t e"))\
                      .then_inc(rowed, 16)
                sp.wait_ge(ready, 1)
                for rows, tile in ((m.dst_rows, dst), (m.rel_rows, rel), (m.run_rows, run)):
                    sp.dma_start(rows.rearrange("(k p) e -> p k e", p=P), tile[:, :, :]).then_inc(wrote, 16)
                sp.wait_ge(wrote, 48)

            @block.scalar
            def _(act):
                with act.Fori(0, NIP // UN) as i:
                    for u in range(UN):
                        e = act.value_load(m.first_tab[0:1, ds(i * UN + u, 1)], min_val=0, max_val=E - P)
                        act.dma_start(m.weight_rows[ds(i * UN + u, 1), :],
                                      weights[:, ds(e, P)]).then_inc(wcopied, 16)
                act.wait_ge(wcopied, 16 * NIP)
                act.dma_start(rw[:, :, :], m.weight_rows.rearrange("(k p) e -> p k e", p=P)).then_inc(rowed, 16)

            @block.vector
            def _(dve):
                n = [0]

                def then(ins):
                    n[0] += 1
                    ins.then_inc(step, 1)
                    dve.wait_ge(step, n[0])

                dve.wait_ge(rowed, 16 * (KI + 1))
                then(dve.tensor_copy(src[:, :, :], ri[:, :, 0, :]))
                then(dve.tensor_copy(dst[:, :, :], ri[:, :, 1, :]))
                then(dve.tensor_copy(rel[:, :, :], ri[:, :, 2, :]))
                then(dve.scalar_tensor_tensor(dst[:, :, :], spread(m.blk_col[:, :], P), float(-P), dst[:, :, :],
                                              ALU.mult, ALU.add))
                then(dve.tensor_tensor(tmp[:, :, :], repeat(m.iota_row[:, :], KI), spread(m.late[:, :], P), ALU.is_lt))
                then(dve.scalar_tensor_tensor(dst[:, :, :], tmp[:, :, :], float(-4 * NP), dst[:, :, :],
                                              ALU.mult, ALU.add))
                then(dve.memset(run[:, :, 0:1], FAR))
                then(dve.memset(end[:, :, P - 1:P], 1.0))
                then(dve.tensor_tensor(end[:, :, 0:P - 1], dst[:, :, 0:P - 1], dst[:, :, 1:P], ALU.not_equal))
                then(dve.tensor_single_scalar(run[:, :, 1:P], end[:, :, 0:P - 1], FAR, ALU.mult))
                then(dve.tensor_single_scalar(tmp[:, :, :], rel[:, :, :], float(HALF_REL), ALU.is_ge))
                then(dve.tensor_tensor(wb[:, :, :], rw[:, :, :], tmp[:, :, :], ALU.mult))
                then(dve.tensor_tensor(wf[:, :, :], rw[:, :, :], wb[:, :, :], ALU.subtract))
                then(dve.scalar_tensor_tensor(rel[:, :, :], tmp[:, :, :], float(-HALF_REL), rel[:, :, :],
                                              ALU.mult, ALU.add))
                dve.sem_inc(ready, 1)
                for k in range(KI):
                    dve.wait_ge(turned, k + 1)
                    for i, t in enumerate((m.src_i, m.dst_l, m.w_fwd, m.w_bwd, m.run_end)):
                        ins = dve.tensor_copy(t[:, k * P:(k + 1) * P], m.ps[i][:, 0:P])
                    ins.then_inc(kept, 1)

            @block.tensor
            def _(pe):
                pe.wait_ge(ready, 1)
                for k in range(KI):
                    if k:
                        pe.wait_ge(kept, k)
                    for i, t in enumerate((src, dst, wf, wb, end)):
                        ins = pe.transpose(m.ps[i][:, 0:P], t[:, k, :], m.ident[:, :])
                    ins.then_inc(turned, 1)


def load_nodes(nc, m, a):
    full = N // P
    with Stage(nc, "nodes") as st:
        loaded, zeroed = st.sem("loaded"), st.sem("zeroed")
        with nc.Block() as block:
            @block.vector
            def _(dve):
                dve.memset(m.x[:, full, :], 0.0).then_inc(zeroed, 1)

            @block.sync
            def _(sp):
                sp.dma_start(m.x[:, 0:full, :], a["x"][0:full * P, :].rearrange("(b p) d -> p b d", p=P))\
                  .then_inc(loaded, 16)
                sp.wait_ge(zeroed, 1)
                sp.dma_start(m.x[0:N - full * P, full, :], a["x"][full * P:N, :]).then_inc(loaded, 16)
                sp.wait_ge(loaded, 32)


def finish(nc, m, out):
    full = N // P
    with Stage(nc, "finish") as st:
        stored = st.sem("stored")
        with nc.Block() as block:
            @block.sync
            def _(sp):
                sp.dma_start(out[0:full * P, :].rearrange("(b p) d -> p b d", p=P), m.x[:, 0:full, :])\
                  .then_inc(stored, 16)
                sp.dma_start(out[full * P:N, :], m.x[0:N - full * P, full, :]).then_inc(stored, 16)
                sp.wait_ge(stored, 32)


class Gather:

    def __init__(self, nc, m, st, table, width):
        self.nc, self.m, self.table = nc, m, table
        self.rows = st.pair_sb("rows", [P, BATCH, width])
        self.index = st.pair_sb("index", [P, BATCH], I32)
        self.index_set = st.pair("index_set")
        self.gathered = st.pair("gathered")

    def program(self, pool, rows_used):
        with pool.Fori(0, LOOPS) as it:
            for q in range(2):
                pool.wait_ge(rows_used[q], it + 1)
                pool.tensor_copy(self.index[q][:, :], self.m.src_i[:, ds(it * (2 * BATCH) + q * BATCH, BATCH)])\
                    .then_inc(self.index_set[q], 1)
                pool.wait_ge(rows_used[q], 1)
                pool.wait_ge(self.index_set[q], it + 1)
                for j in range(BATCH):
                    pool.indirect_dma_start(self.rows[q][:, j, :], None, self.table,
                                            bass.IndirectOffsetOnAxis(ap=self.index[q][:, j:j + 1], axis=0))\
                        .then_inc(self.gathered[q], 16)

    def wait(self, eng, q, it):
        eng.wait_ge(self.gathered[q], it * (16 * BATCH) + 16 * BATCH)


def item(it, q, j=0):
    return it * (2 * BATCH) + (q * BATCH + j)


def compgcn_pass(nc, m, a, layer, table, x):
    with Stage(nc, f"gcn{layer}") as st:
        g = Gather(nc, m, st, table, DIM)
        rel_loaded, ids_loaded = st.sem("rel_loaded"), st.pair("ids_loaded")
        rel_hot, rel_used = st.pair("rel_hot"), st.pair("rel_rows")
        comp_made, hot_made, msg_made = st.pair("comp"), st.pair("edge_hot"), st.pair("msg")
        summed, added, sums_read = st.pair("summed"), st.sem("added"), st.pair("sums_read")
        rel = st.sb("rel", [HALF_REL, DIM])
        ids = st.pair_sb("ids", [HALF_REL, BATCH * P])
        rhot = st.pair_sb("rhot", [HALF_REL, BATCH * P])
        comp = st.pair_sb("comp_s", [P, BATCH, DIM])
        hot = st.pair_sb("hot", [P, BATCH, P])
        msg = st.pair_sb("msg_s", [P, BATCH, 2 * DIM])
        rel_ps, sum_ps = m.ps[0:2], m.ps[2:4]
        with nc.Block() as block:
            @block.gpsimd
            def _(pool):
                g.program(pool, comp_made)

            @block.sync
            def _(sp):
                sp.dma_start(rel[:, :], a["L0_gnn_rel_emb"][layer, 0:HALF_REL, :]).then_inc(rel_loaded, 16)
                with sp.Fori(0, LOOPS) as it:
                    for q in range(2):
                        sp.wait_ge(rel_hot[q], it + 1)
                        sp.dma_start(ids[q][:, :], m.rel_rows[ds(item(it, q), BATCH), :]
                                     .rearrange("b e -> (b e)").partition_broadcast(HALF_REL))\
                          .then_inc(ids_loaded[q], 16)

            @block.vector
            def _(dve):
                dve.memset(m.acc[:, :, :], 0.0).then_inc(added, 1)
                for q in range(2):
                    dve.sem_inc(rel_hot[q], 1)
                    dve.sem_inc(comp_made[q], 1)
                    dve.sem_inc(sums_read[q], 1)
                dve.wait_ge(added, 1)
                with dve.Fori(0, LOOPS) as it:
                    for q in range(2):
                        dve.wait_ge(ids_loaded[q], it * 16 + 16)
                        dve.wait_ge(rel_used[q], it + 1)
                        dve.tensor_scalar(rhot[q][:, :], ids[q][:, :], m.iota_col[0:HALF_REL, 0:1], None, ALU.is_equal)\
                            .then_inc(rel_hot[q], 1)
                        dve.wait_ge(summed[q], it + 1)
                        dve.tensor_tensor(hot[q][:, :, :], repeat(m.iota_row[:, :], BATCH),
                                          spread(m.dst_l[:, ds(item(it, q), BATCH)], P), ALU.is_equal)\
                            .then_inc(hot_made[q], 1)
                        g.wait(dve, q, it)
                        dve.wait_ge(rel_used[q], it + 2)
                        dve.tensor_tensor(comp[q][:, :, :], g.rows[q][:, :, :],
                                          rel_ps[q][:, 0:BATCH * DIM].rearrange("p (b d) -> p b d", b=BATCH), ALU.mult)\
                            .then_inc(comp_made[q], 1)
                        dve.wait_ge(comp_made[q], it + 2)
                        for half, w in ((0, m.w_fwd), (1, m.w_bwd)):
                            dve.tensor_tensor(msg[q][:, :, half * DIM:(half + 1) * DIM], comp[q][:, :, :],
                                              spread(w[:, ds(item(it, q), BATCH)], DIM), ALU.mult).then_inc(msg_made[q], 1)
                        dve.wait_ge(summed[q], it + 2)
                        add_items(dve, m, it, q, sum_ps[q], 0, 2 * DIM, added, last=sums_read[q])

            @block.tensor
            def _(pe):
                for q in range(2):
                    pe.sem_inc(rel_used[q], 1)
                    pe.sem_inc(summed[q], 1)
                pe.wait_ge(rel_loaded, 16)
                with pe.Fori(0, LOOPS) as it:
                    for q in range(2):
                        pe.wait_ge(rel_hot[q], it + 2)
                        pe.wait_ge(comp_made[q], it + 1)
                        for j in range(BATCH):
                            ins = pe.matmul(rel_ps[q][:, j * DIM:(j + 1) * DIM], rhot[q][:, j * P:(j + 1) * P], rel[:, :],
                                            start=True, stop=True)
                        ins.then_inc(rel_used[q], 1)
                        pe.wait_ge(hot_made[q], it + 1)
                        pe.wait_ge(msg_made[q], it * 2 + 2)
                        pe.wait_ge(sums_read[q], it + 1)
                        sum_items(pe, hot[q], msg[q], sum_ps[q], 2 * DIM, summed[q])


def sum_items(pe, hot, msg, bank, width, summed):
    for j in range(BATCH):
        ins = pe.matmul(bank[:, j * width:(j + 1) * width], hot[:, j, :], msg[:, j, 0:width], start=True, stop=True)
    ins.then_inc(summed, 1)


def add_items(dve, m, it, q, bank, lo, width, added, parts=1, part=0, acc=None, op=ALU.add, last=None):
    acc = m.acc if acc is None else acc
    for j in range(BATCH):
        b = dve.value_load(m.block_tab[0:1, ds(item(it, q, j), 1)], min_val=0, max_val=NB - 1)
        dve.wait_ge(added, it * (2 * BATCH * parts) + ((q * parts + part) * BATCH + j + 1))
        dst = acc[:, ds(b, 1), lo:lo + width]
        dve.tensor_tensor(dst, dst, place(bank, j, width).unsqueeze(1), op).then_inc(added, 1)
    if last is not None:
        dve.wait_ge(added, it * (2 * BATCH * parts) + ((q * parts + part + 1) * BATCH + 1))
        dve.sem_inc(last, 1)


def compgcn_nodes(nc, m, a, layer, x, y):
    with Stage(nc, f"gcn_nodes{layer}") as st:
        loaded, staged, turned = st.sem("loaded"), st.sem("staged"), st.sem("turned")
        evacuated, product, stored, written = st.sem("evacuated"), st.sem("product"), st.sem("stored"), st.sem("written")
        w_agg, w_loop = st.sb("w_agg", [P, DIM]), st.sb("w_loop", [DIM, DIM])
        flat, tall, tall_x = st.sb("flat", [P, 3 * DIM]), st.sb("tall", [P, P]), st.sb("tall_x", [DIM, P])
        agg_t, x_t, res = m.ps[0], m.ps[1], m.ps[2]
        with nc.Block() as block:
            @block.sync
            def _(sp):
                sp.dma_start(w_agg[0:DIM, :], a["L0_gnn_w_fwd"][layer]).then_inc(loaded, 16)
                sp.dma_start(w_agg[DIM:P, :], a["L0_gnn_w_bwd"][layer]).then_inc(loaded, 16)
                sp.dma_start(w_loop[:, :], a["L0_gnn_w_loop"][layer]).then_inc(loaded, 16)
                if layer == 0:
                    sp.wait_ge(stored, NB + 1)
                    sp.dma_start(m.x_table.rearrange("(b p) d -> p b d", p=P), y[:, :, :]).then_inc(written, 16)
                    sp.wait_ge(written, 16)

            @block.vector
            def _(dve):
                with dve.Fori(0, NB) as b:
                    dve.wait_ge(turned, b + 1)
                    dve.tensor_copy(flat[:, 0:P].unsqueeze(1), m.acc[:, ds(b, 1), 0:P]).then_inc(staged, 1)
                    dve.tensor_copy(flat[:, P:3 * DIM].unsqueeze(1), x[:, ds(b, 1), :]).then_inc(staged, 1)

            @block.tensor
            def _(pe):
                pe.sem_inc(turned, 1)
                pe.sem_inc(product, 1)
                pe.wait_ge(loaded, 48)
                with pe.Fori(0, NB) as b:
                    pe.wait_ge(staged, b * 2 + 2)
                    pe.wait_ge(evacuated, b * 2 + 1)
                    pe.transpose(agg_t[:, 0:P], flat[:, 0:P], m.ident[:, :])
                    pe.transpose(x_t[0:DIM, 0:P], flat[:, P:3 * DIM], m.ident[:, :]).then_inc(turned, 1)
                    pe.wait_ge(evacuated, b * 2 + 3)
                    pe.wait_ge(stored, b + 1)
                    pe.matmul(res[:, 0:DIM], tall[:, :], w_agg[:, :], start=True, stop=False)
                    pe.matmul(res[:, 0:DIM], tall_x[:, :], w_loop[:, :], start=False, stop=True).then_inc(product, 1)

            @block.scalar
            def _(act):
                act.sem_inc(evacuated, 1)
                act.sem_inc(stored, 1)
                with act.Fori(0, NB) as b:
                    act.wait_ge(turned, b + 2)
                    act.wait_ge(product, b + 1)
                    act.activation(tall[:, :], agg_t[:, 0:P], ACT.Copy).then_inc(evacuated, 1)
                    act.activation(tall_x[:, :], x_t[0:DIM, 0:P], ACT.Copy).then_inc(evacuated, 1)
                    act.wait_ge(product, b + 2)
                    act.activation(y[:, ds(b, 1), :], res[:, 0:DIM].unsqueeze(1), ACT.Relu).then_inc(stored, 1)


def residual_norm(nc, m, y):
    with Stage(nc, f"norm{m.norms}") as st:
        m.norms += 1
        step, rooted = st.sem("step"), st.sem("rooted")
        sq = st.sb("sq", [P, NB, DIM])
        mean, var = st.sb("mean", [P, NB]), st.sb("var", [P, NB])
        x = m.x[:, :, :]
        with nc.Block() as block:
            @block.vector
            def _(dve):
                n = [0]

                def then(ins):
                    n[0] += 1
                    ins.then_inc(step, 1)
                    dve.wait_ge(step, n[0])

                then(dve.tensor_tensor(x, x, y[:, :, :], ALU.add))
                then(dve.tensor_reduce(mean[:, :], x, AX.X, ALU.add))
                then(dve.tensor_single_scalar(mean[:, :], mean[:, :], 1.0 / DIM, ALU.mult))
                then(dve.tensor_tensor(x, x, spread(mean[:, :], DIM), ALU.subtract))
                then(dve.tensor_tensor(sq[:, :, :], x, x, ALU.mult))
                then(dve.tensor_reduce(var[:, :], sq[:, :, :], AX.X, ALU.add))
                then(dve.tensor_scalar(var[:, :], var[:, :], 1.0 / DIM, 1e-5, ALU.mult, ALU.add))
                dve.wait_ge(rooted, 1)
                then(dve.reciprocal(var[:, :], var[:, :]))
                dve.tensor_tensor(x, x, spread(var[:, :], DIM), ALU.mult)

            @block.scalar
            def _(act):
                act.wait_ge(step, 7)
                act.activation(var[:, :], var[:, :], ACT.Sqrt).then_inc(rooted, 1)


def message_tables(nc, m, a):
    with Stage(nc, "msg_tab") as st:
        loaded, staged, turned = st.sem("loaded"), st.sem("staged"), st.sem("turned")
        evacuated, product, stored, written = st.sem("evacuated"), st.sem("product"), st.sem("stored"), st.sem("written")
        w, bias = st.sb("w", [DIM, 2 * DIM]), st.sb("bias", [P, 2 * DIM])
        flat, tall = st.sb("flat", [P, P]), st.sb("tall", [DIM, P])
        pre = st.sb("pre", [P, NB, 2 * DIM])
        x_t, res = m.ps[0], m.ps[1]
        with nc.Block() as block:
            @block.sync
            def _(sp):
                for l in range(2):
                    half = slice(l * DIM, (l + 1) * DIM)
                    sp.dma_start(w[:, half], a["L1_gnn_msg_w1"][l, 0:DIM, :]).then_inc(loaded, 16)
                    sp.dma_start(bias[:, half], a["L1_gnn_msg_b1"][l].partition_broadcast(P)).then_inc(loaded, 16)
                sp.wait_ge(stored, NB + 1)
                sp.dma_start(m.pre_table.rearrange("(b p) d -> p b d", p=P), pre[:, :, :]).then_inc(written, 16)
                sp.wait_ge(written, 16)

            @block.vector
            def _(dve):
                dve.memset(flat[:, :], 0.0).then_inc(stored, 1)
                dve.wait_ge(stored, 1)
                dve.wait_ge(loaded, 64)
                with dve.Fori(0, NB) as b:
                    dve.wait_ge(turned, b + 1)
                    dve.tensor_copy(flat[:, 0:DIM].unsqueeze(1), m.x[:, ds(b, 1), :]).then_inc(staged, 1)
                    dve.wait_ge(product, b + 2)
                    dve.tensor_tensor(pre[:, ds(b, 1), :], res[:, 0:2 * DIM].unsqueeze(1), bias[:, :].unsqueeze(1),
                                      ALU.add).then_inc(stored, 1)

            @block.tensor
            def _(pe):
                pe.sem_inc(turned, 1)
                pe.sem_inc(product, 1)
                pe.wait_ge(loaded, 64)
                with pe.Fori(0, NB) as b:
                    pe.wait_ge(staged, b + 1)
                    pe.wait_ge(evacuated, b + 1)
                    pe.transpose(x_t[:, 0:P], flat[:, :], m.ident[:, :]).then_inc(turned, 1)
                    pe.wait_ge(evacuated, b + 2)
                    pe.wait_ge(stored, b + 1)
                    pe.matmul(res[:, 0:2 * DIM], tall[:, :], w[:, :], start=True, stop=True).then_inc(product, 1)

            @block.scalar
            def _(act):
                act.sem_inc(evacuated, 1)
                with act.Fori(0, NB) as b:
                    act.wait_ge(turned, b + 2)
                    act.wait_ge(product, b + 1)
                    act.activation(tall[:, :], x_t[0:DIM, 0:P], ACT.Copy).then_inc(evacuated, 1)


def attr_loads(sp, m, attr, tiles, free, loaded):
    with sp.Fori(0, LOOPS) as it:
        for q in range(2):
            sp.wait_ge(free[q], it + 1)
            for j in range(BATCH):
                e = sp.value_load(m.first_tab[0:1, ds(item(it, q, j), 1)], min_val=0, max_val=E - P)
                sp.dma_start(tiles[q][:, j, :], attr[ds(e, P), :]).then_inc(loaded[q], 16)


def message_pass(nc, m, a):
    HID, ED = 2 * DIM, 32
    with Stage(nc, "msg") as st:
        g = Gather(nc, m, st, m.pre_table, HID)
        w_zeroed, w_loaded, attr_loaded = st.sem("w_zeroed"), st.sem("w_loaded"), st.pair("attr_loaded")
        turned, evacuated, edge_part = st.pair("turned"), st.pair("evacuated"), st.pair("edge_part")
        pre_made, msg_made, hot_made = st.pair("pre"), st.pair("msg"), st.pair("edge_hot")
        summed, added, sums_read = st.pair("summed"), st.sem("added"), st.pair("sums_read")
        w = st.sb("w", [P, BATCH * HID])
        attr = st.pair_sb("attr", [P, BATCH, ED])
        attr_t = st.pair_sb("attr_t", [P, P])
        pre = st.pair_sb("pre_s", [P, BATCH * HID])
        msg = st.pair_sb("msg_s", [P, BATCH, HID])
        hot = st.pair_sb("hot", [P, BATCH, P])
        turn_ps, edge_ps, sum_ps, deg_ps = m.ps[0:2], m.ps[2:4], m.ps[4:6], m.ps[6:8]
        with nc.Block() as block:
            @block.gpsimd
            def _(pool):
                g.program(pool, pre_made)

            @block.sync
            def _(sp):
                sp.wait_ge(w_zeroed, 1)
                for l in range(2):
                    for j in range(BATCH):
                        col = j * HID + l * DIM
                        sp.dma_start(w[j * ED:(j + 1) * ED, col:col + DIM], a["L1_gnn_msg_w1"][l, DIM:DIM + ED, :])\
                          .then_inc(w_loaded, 16)
                attr_loads(sp, m, a["edge_attr_32"], attr, turned, attr_loaded)

            @block.scalar
            def _(act):
                for q in range(2):
                    act.sem_inc(evacuated[q], 1)
                with act.Fori(0, LOOPS) as it:
                    for q in range(2):
                        act.wait_ge(turned[q], it + 2)
                        act.wait_ge(edge_part[q], it + 1)
                        act.activation(attr_t[q][:, :], turn_ps[q][:, 0:P], ACT.Copy).then_inc(evacuated[q], 1)
                        act.wait_ge(pre_made[q], it + 2)
                        act.wait_ge(summed[q], it + 1)
                        act.activation(msg[q][:, :, :].rearrange("p b d -> p (b d)"), pre[q][:, :], ACT.Relu)\
                            .then_inc(msg_made[q], 1)

            @block.vector
            def _(dve):
                dve.memset(w[:, :], 0.0).then_inc(w_zeroed, 1)
                dve.memset(m.acc[:, :, :], 0.0).then_inc(added, 1)
                for q in range(2):
                    dve.sem_inc(pre_made[q], 1)
                    dve.sem_inc(msg_made[q], 1)
                    dve.sem_inc(sums_read[q], 1)
                with dve.Fori(0, LOOPS) as it:
                    for q in range(2):
                        dve.wait_ge(summed[q], it + 1)
                        dve.tensor_tensor(hot[q][:, :, :], repeat(m.iota_row[:, :], BATCH),
                                          spread(m.dst_l[:, ds(item(it, q), BATCH)], P), ALU.is_equal)\
                            .then_inc(hot_made[q], 1)
                        g.wait(dve, q, it)
                        dve.wait_ge(edge_part[q], it + 2)
                        dve.wait_ge(msg_made[q], it + 1)
                        dve.tensor_tensor(pre[q][:, :], g.rows[q][:, :, :].rearrange("p b d -> p (b d)"),
                                          edge_ps[q][:, :], ALU.add).then_inc(pre_made[q], 1)
                        dve.wait_ge(summed[q], it + 2)
                        add_items(dve, m, it, q, sum_ps[q], 0, HID, added, 2, 0)
                        add_items(dve, m, it, q, deg_ps[q], HID, 1, added, 2, 1, last=sums_read[q])

            @block.tensor
            def _(pe):
                for q in range(2):
                    pe.sem_inc(turned[q], 1)
                    pe.sem_inc(edge_part[q], 1)
                    pe.sem_inc(summed[q], 1)
                pe.wait_ge(w_loaded, 2 * BATCH * 16)
                with pe.Fori(0, LOOPS) as it:
                    for q in range(2):
                        pe.wait_ge(attr_loaded[q], it * (16 * BATCH) + 16 * BATCH)
                        pe.wait_ge(evacuated[q], it + 1)
                        pe.transpose(turn_ps[q][:, 0:P], attr[q][:, :, :].rearrange("p b d -> p (b d)"), m.ident[:, :])\
                          .then_inc(turned[q], 1)
                        pe.wait_ge(evacuated[q], it + 2)
                        pe.wait_ge(pre_made[q], it + 1)
                        pe.matmul(edge_ps[q][:, :], attr_t[q][:, :], w[:, :], start=True, stop=True)\
                          .then_inc(edge_part[q], 1)
                        pe.wait_ge(hot_made[q], it + 1)
                        pe.wait_ge(msg_made[q], it + 2)
                        pe.wait_ge(sums_read[q], it + 1)
                        for j in range(BATCH):
                            pe.matmul(deg_ps[q][:, j:j + 1], hot[q][:, j, :], m.ones[:, 0:1], start=True, stop=True)
                        sum_items(pe, hot[q], msg[q], sum_ps[q], HID, summed[q])


def message_nodes(nc, m, a):
    with Stage(nc, "msg_nodes") as st:
        loaded, biased, rated = st.sem("loaded"), st.sem("biased"), st.sem("rated")
        staged, turned, evac, agged = st.sem("staged"), st.sem("turned"), st.sem("evacuated"), st.sem("agg")
        divided, joined, joined_t = st.sem("divided"), st.sem("joined"), st.sem("joined_t")
        hidden_ps, hidden, updated, stored = st.sem("hidden_ps"), st.sem("hidden"), st.sem("updated"), st.sem("stored")
        w2, w_u1, w_u2 = st.sb("w2", [P, DIM]), st.sb("w_u1", [P, DIM]), st.sb("w_u2", [DIM, DIM])
        b2, b2b, b_u1, b_u2 = st.sb("b2", [P, DIM]), st.sb("b2b", [P, DIM]), st.sb("b_u1", [DIM, 1]), st.sb("b_u2", [P, DIM])
        rate = st.sb("rate", [P, NB])
        y = st.sb("y", [P, NB, DIM])
        flat, tall, agg_s = st.sb("flat", [P, P]), st.sb("tall", [P, P]), st.sb("agg_s", [P, DIM])
        both, both_t, hid = st.sb("both", [P, P]), st.sb("both_t", [P, P]), st.sb("hid", [DIM, P])
        t_ps, agg_ps, bt_ps, h_ps, u_ps = m.ps[0:5]
        deg = m.acc[:, :, 2 * DIM:2 * DIM + 1].rearrange("p b o -> p (b o)")
        with nc.Block() as block:
            @block.sync
            def _(sp):
                sp.dma_start(w2[:, :], a["L1_gnn_msg_w2"].rearrange("l i o -> (l i) o")).then_inc(loaded, 16)
                sp.dma_start(b2[:, :], a["L1_gnn_msg_b2"][0].partition_broadcast(P)).then_inc(loaded, 16)
                sp.dma_start(b2b[:, :], a["L1_gnn_msg_b2"][1].partition_broadcast(P)).then_inc(loaded, 16)
                sp.dma_start(w_u1[:, :], a["L1_gnn_upd_w1"]).then_inc(loaded, 16)
                sp.dma_start(w_u2[:, :], a["L1_gnn_upd_w2"]).then_inc(loaded, 16)
                sp.dma_start(b_u1[:, :], a["L1_gnn_upd_b1"].unsqueeze(1)).then_inc(loaded, 16)
                sp.dma_start(b_u2[:, :], a["L1_gnn_upd_b2"].partition_broadcast(P)).then_inc(loaded, 16)

            @block.vector
            def _(dve):
                dve.wait_ge(loaded, 16 * 7)
                dve.tensor_tensor(b2[:, :], b2[:, :], b2b[:, :], ALU.add).then_inc(biased, 1)
                dve.tensor_single_scalar(rate[:, :], deg, 1e-8, ALU.add).then_inc(rated, 1)
                dve.wait_ge(rated, 1)
                dve.reciprocal(rate[:, :], rate[:, :]).then_inc(rated, 1)
                dve.wait_ge(biased, 1)
                dve.wait_ge(rated, 2)
                with dve.Fori(0, NB) as b:
                    dve.wait_ge(turned, b + 1)
                    dve.tensor_copy(flat[:, :].unsqueeze(1), m.acc[:, ds(b, 1), 0:P]).then_inc(staged, 1)
                    dve.wait_ge(agged, b + 1)
                    dve.scalar_tensor_tensor(agg_s[:, :], b2[:, :], m.acc[:, ds(b, 1), P:P + 1].rearrange("p b o -> p (b o)"),
                                             agg_ps[:, 0:DIM], ALU.mult, ALU.add).then_inc(divided, 1)
                    dve.wait_ge(divided, b + 1)
                    dve.wait_ge(joined_t, b + 1)
                    dve.tensor_copy(both[:, 0:DIM].unsqueeze(1), m.x[:, ds(b, 1), :]).then_inc(joined, 1)
                    dve.tensor_scalar(both[:, DIM:P], agg_s[:, :], rate[:, ds(b, 1)], None, ALU.mult).then_inc(joined, 1)
                    dve.wait_ge(updated, b + 1)
                    dve.tensor_tensor(y[:, ds(b, 1), :], u_ps[:, 0:DIM].unsqueeze(1), b_u2[:, :].unsqueeze(1),
                                      ALU.add).then_inc(stored, 1)

            @block.tensor
            def _(pe):
                pe.sem_inc(turned, 1)
                pe.sem_inc(joined_t, 1)
                pe.wait_ge(loaded, 16 * 7)
                with pe.Fori(0, NB) as b:
                    pe.wait_ge(staged, b + 1)
                    pe.transpose(t_ps[:, 0:P], flat[:, :], m.ident[:, :]).then_inc(turned, 1)
                    pe.wait_ge(evac, b * 2 + 1)
                    pe.matmul(agg_ps[:, 0:DIM], tall[:, :], w2[:, :], start=True, stop=True).then_inc(agged, 1)
                    pe.wait_ge(joined, b * 2 + 2)
                    pe.transpose(bt_ps[:, 0:P], both[:, :], m.ident[:, :]).then_inc(joined_t, 1)
                    pe.wait_ge(evac, b * 2 + 2)
                    pe.matmul(h_ps[0:DIM, 0:P], w_u1[:, :], both_t[:, :], start=True, stop=True).then_inc(hidden_ps, 1)
                    pe.wait_ge(hidden, b + 1)
                    pe.wait_ge(stored, b + 1)
                    pe.matmul(u_ps[:, 0:DIM], hid[:, :], w_u2[:, :], start=True, stop=True).then_inc(updated, 1)

            @block.scalar
            def _(act):
                act.sem_inc(stored, 1)
                with act.Fori(0, NB) as b:
                    act.wait_ge(turned, b + 2)
                    act.activation(tall[:, :], t_ps[:, 0:P], ACT.Copy).then_inc(evac, 1)
                    act.wait_ge(joined_t, b + 2)
                    act.activation(both_t[:, :], bt_ps[:, 0:P], ACT.Copy).then_inc(evac, 1)
                    act.wait_ge(hidden_ps, b + 1)
                    act.activation(hid[:, :], h_ps[0:DIM, 0:P], ACT.Relu, bias=b_u1[:, 0:1]).then_inc(hidden, 1)
        residual_norm(nc, m, y)


MAGIC = 12582912.0
TURN = 2.0 * np.pi
TURN_HI = float(np.float32(6.28125))
TURN_MID = float(np.float32(TURN - 6.28125))
TURN_LO = float(np.float32(TURN - 6.28125 - float(np.float32(TURN - 6.28125))))


def diffusion_embed(nc, m, a, cur):
    with Stage(nc, "embed") as st:
        loaded, padded, step, sined = st.sem("loaded"), st.sem("padded"), st.sem("step"), st.sem("sined")
        staged, turned, evac = st.sem("staged"), st.sem("turned"), st.sem("evacuated")
        hidden_ps, hidden, product, stored = st.sem("hidden_ps"), st.sem("hidden"), st.sem("product"), st.sem("stored")
        w_in, w1, w2 = st.sb("w_in", [DIM, P]), st.sb("w1", [P, P]), st.sb("w2", [P, P])
        b_in, b1, b2 = st.sb("b_in", [P, 1]), st.sb("b1", [P, 1]), st.sb("b2", [P, 1])
        freq = st.sb("freq", [P, 2])
        ang, rnd = st.sb("ang", [P, NP]), st.sb("rnd", [P, NP])
        flat, tall, emb = st.sb("flat", [P, P]), st.sb("tall", [DIM, P]), st.sb("emb", [P, P])
        hid = st.sb("hid", [P, P])
        t_ps, h_ps, o_ps = m.ps[0:3]
        with nc.Block() as block:
            @block.sync
            def _(sp):
                sp.wait_ge(padded, 1)
                sp.dma_start(ang[:, 0:N], a["node_vec"].partition_broadcast(P)).then_inc(loaded, 16)
                sp.dma_start(freq[:, :], a["freq"]).then_inc(loaded, 16)
                for tile, name in ((w_in, "init_w"), (w1, "te_w1"), (w2, "te_w2")):
                    sp.dma_start(tile[:, :], a["L2_gnn_" + name]).then_inc(loaded, 16)
                for tile, name in ((b_in, "init_b"), (b1, "te_b1"), (b2, "te_b2")):
                    sp.dma_start(tile[:, :], a["L2_gnn_" + name].unsqueeze(1)).then_inc(loaded, 16)

            @block.vector
            def _(dve):
                n = [0]

                def then(ins):
                    n[0] += 1
                    ins.then_inc(step, 1)
                    dve.wait_ge(step, n[0])

                dve.memset(ang[:, :], 0.0).then_inc(padded, 1)
                dve.memset(flat[:, :], 0.0).then_inc(padded, 1)
                dve.wait_ge(loaded, 16 * 8)
                dve.wait_ge(padded, 2)
                then(dve.tensor_tensor(b_in[:, :], b_in[:, :], b2[:, :], ALU.add))
                then(dve.tensor_single_scalar(ang[:, :], ang[:, :], freq[:, 0:1], ALU.mult))
                then(dve.tensor_scalar(rnd[:, :], ang[:, :], freq[:, 1:2], None, ALU.add))
                then(dve.tensor_scalar(rnd[:, :], rnd[:, :], 1.0 / TURN, MAGIC, ALU.mult, ALU.add))
                then(dve.tensor_single_scalar(rnd[:, :], rnd[:, :], -MAGIC, ALU.add))
                for part in (TURN_HI, TURN_MID, TURN_LO):
                    then(dve.scalar_tensor_tensor(ang[:, :], rnd[:, :], -part, ang[:, :], ALU.mult, ALU.add))
                then(dve.tensor_scalar(ang[:, :], ang[:, :], freq[:, 1:2], None, ALU.add))
                then(dve.tensor_scalar(ang[:, :], ang[:, :], 3.1415925, -3.1415925, ALU.min, ALU.max))
                dve.wait_ge(sined, 1)
                with dve.Fori(0, NB) as b:
                    dve.wait_ge(product, b + 1)
                    dve.tensor_copy(flat[:, 0:DIM].unsqueeze(1), m.x[:, ds(b, 1), :]).then_inc(staged, 1)
                    dve.tensor_copy(emb[:, :], rnd[:, ds(b * P, P)]).then_inc(staged, 1)

            @block.scalar
            def _(act):
                act.wait_ge(step, 10)
                act.activation(rnd[:, :], ang[:, :], ACT.Sin).then_inc(sined, 1)
                act.sem_inc(stored, 1)
                with act.Fori(0, NB) as b:
                    act.wait_ge(turned, b + 1)
                    act.activation(tall[:, :], t_ps[0:DIM, 0:P], ACT.Copy).then_inc(evac, 1)
                    act.wait_ge(hidden_ps, b + 1)
                    act.activation(hid[:, :], h_ps[:, 0:P], ACT.Silu, bias=b1[:, 0:1]).then_inc(hidden, 1)
                    act.wait_ge(product, b + 2)
                    act.activation(cur[:, 0, ds(b * P, P)], o_ps[:, 0:P], ACT.Identity, bias=b_in[:, 0:1])\
                        .then_inc(stored, 1)

            @block.tensor
            def _(pe):
                pe.sem_inc(product, 1)
                pe.wait_ge(loaded, 16 * 8)
                with pe.Fori(0, NB) as b:
                    pe.wait_ge(staged, b * 2 + 2)
                    pe.transpose(t_ps[:, 0:P], flat[:, :], m.ident[:, :]).then_inc(turned, 1)
                    pe.matmul(h_ps[:, 0:P], w1[:, :], emb[:, :], start=True, stop=True).then_inc(hidden_ps, 1)
                    pe.wait_ge(evac, b + 1)
                    pe.wait_ge(hidden, b + 1)
                    pe.wait_ge(stored, b + 1)
                    pe.matmul(o_ps[:, 0:P], w_in[:, :], tall[:, :], start=True, stop=False)
                    pe.matmul(o_ps[:, 0:P], w2[:, :], hid[:, :], start=False, stop=True).then_inc(product, 1)


def gat_shape(layer):
    return (1, 2, 2)[layer], (256, 256, 128)[layer]


def gat_tables(nc, m, a, layer, cur):
    kt, width = gat_shape(layer)
    c, full = width // HEADS, width + 2 * HEADS
    with Stage(nc, f"gat_tab{layer}") as st:
        loaded, folded, staged = st.sem("loaded"), st.sem("folded"), st.sem("staged")
        product, stored, kept, written, step = st.sem("product"), st.sem("stored"), st.sem("kept"), st.sem("written"), st.sem("step")
        w = st.sb("w", [P, kt, full])
        att = st.sb("att", [P, 2, width])
        prod = st.sb("prod", [P, width])
        flat = st.sb("flat", [P, kt, P])
        o_ps = m.ps[0]
        table = m.xw_table if width == 256 else m.xw_table2
        with nc.Block() as block:
            @block.sync
            def _(sp):
                sp.dma_start(w[:, :, 0:width], a[f"L2_gnn_gat_w{layer}"].rearrange("(k p) o -> p k o", p=P)).then_inc(loaded, 16)
                for i, name in enumerate(("src", "dst")):
                    sp.dma_start(att[:, i, :], a[f"L2_gnn_att_{name}{layer}"].rearrange("h c -> (h c)").partition_broadcast(P))\
                      .then_inc(loaded, 16)
                sp.wait_ge(stored, NB + 1)
                sp.dma_start(table.rearrange("(b p) d -> p b d", p=P), m.node_out[:, :, 0:width + HEADS]).then_inc(written, 16)
                sp.dma_start(m.al_table.rearrange("(b p) d -> p b d", p=P), m.node_out[:, :, width:width + HEADS])\
                  .then_inc(written, 16)
                sp.wait_ge(written, 32)

            @block.vector
            def _(dve):
                n = [0]

                def then(ins):
                    n[0] += 1
                    ins.then_inc(step, 1)
                    dve.wait_ge(step, n[0])

                dve.wait_ge(loaded, 48)
                for k in range(kt):
                    for i in range(2):
                        then(dve.tensor_tensor(prod[:, :], w[:, k, 0:width], att[:, i, :], ALU.mult))
                        then(dve.tensor_reduce(w[:, k, width + HEADS * i:width + HEADS * (i + 1)],
                                               prod[:, :].rearrange("p (h c) -> p h c", h=HEADS), AX.X, ALU.add))
                dve.sem_inc(folded, 1)
                with dve.Fori(0, NB) as b:
                    dve.wait_ge(product, b + 1)
                    dve.tensor_copy(flat[:, :, :], cur[:, 0:kt, ds(b * P, P)]).then_inc(staged, 1)
                dve.wait_ge(stored, NB + 1)
                dve.tensor_copy(m.dst_tab[:, :, 0:HEADS], m.node_out[:, :, width + HEADS:full])

            @block.scalar
            def _(act):
                act.sem_inc(stored, 1)
                with act.Fori(0, NB) as b:
                    act.wait_ge(product, b + 2)
                    act.activation(m.node_out[:, ds(b, 1), 0:full], o_ps[:, 0:full].unsqueeze(1), ACT.Copy).then_inc(stored, 1)

            @block.tensor
            def _(pe):
                pe.sem_inc(product, 1)
                pe.wait_ge(folded, 1)
                with pe.Fori(0, NB) as b:
                    pe.wait_ge(staged, b + 1)
                    pe.wait_ge(stored, b + 1)
                    for k in range(kt):
                        ins = pe.matmul(o_ps[:, 0:full], flat[:, k, :], w[:, k, :], start=k == 0, stop=k == kt - 1)
                    ins.then_inc(product, 1)


def gat_max_pass(nc, m, layer):
    with Stage(nc, f"gat_max{layer}") as st:
        g = Gather(nc, m, st, m.al_table, HEADS)
        runs_loaded, turned, scanned, turned_back = (st.pair(n) for n in ("runs_loaded", "turned", "scanned", "turned_back"))
        ends_made, hot_made, picked, penal = (st.pair(n) for n in ("ends", "edge_hot", "picked", "penalty"))
        best, added, sums_read = st.pair("best"), st.sem("added"), st.pair("sums_read")
        ROWS = BATCH * HEADS
        runs = st.pair_sb("runs", [ROWS, P])
        run_max = st.pair_sb("run_max", [ROWS, P])
        ends = st.pair_sb("ends_s", [P, BATCH, HEADS + 1])
        hot = st.pair_sb("hot", [P, BATCH, P])
        pen = st.pair_sb("pen", [P, BATCH])
        cand = st.pair_sb("cand", [P, BATCH, HEADS])
        turn_ps, back_ps, pick_ps = m.ps[0:2], m.ps[2:4], m.ps[4:6]
        with nc.Block() as block:
            @block.gpsimd
            def _(pool):
                g.program(pool, turned)

            @block.sync
            def _(sp):
                with sp.Fori(0, LOOPS) as it:
                    for q in range(2):
                        sp.wait_ge(scanned[q], it + 1)
                        sp.dma_start(runs[q][:, :], m.run_rows[ds(item(it, q), BATCH), :].unsqueeze(1)
                                     .to_broadcast([BATCH, HEADS, P])).then_inc(runs_loaded[q], 16)

            @block.vector
            def _(dve):
                dve.memset(m.al_max[:, :, :], FAR).then_inc(added, 1)
                for q in range(2):
                    dve.sem_inc(scanned[q], 1)
                    dve.sem_inc(ends_made[q], 1)
                    dve.sem_inc(sums_read[q], 1)
                with dve.Fori(0, LOOPS) as it:
                    for q in range(2):
                        dve.wait_ge(picked[q], it + 1)
                        dve.tensor_tensor(hot[q][:, :, :], repeat(m.iota_row[:, :], BATCH),
                                          spread(m.dst_l[:, ds(item(it, q), BATCH)], P), ALU.is_equal)\
                            .then_inc(hot_made[q], 1)
                        dve.wait_ge(runs_loaded[q], it * 16 + 16)
                        dve.wait_ge(turned[q], it + 2)
                        dve.wait_ge(turned_back[q], it + 1)
                        dve.tensor_tensor_scan(run_max[q][:, :], runs[q][:, :], turn_ps[q][0:ROWS, 0:P], FAR, ALU.add, ALU.max)\
                            .then_inc(scanned[q], 1)
                        dve.wait_ge(turned_back[q], it + 2)
                        last = m.run_end[:, ds(item(it, q), BATCH)]
                        dve.tensor_tensor(ends[q][:, :, 0:HEADS],
                                          back_ps[q][:, 0:ROWS].rearrange("p (b h) -> p b h", b=BATCH),
                                          spread(last, HEADS), ALU.mult).then_inc(ends_made[q], 1)
                        dve.tensor_copy(ends[q][:, :, HEADS:HEADS + 1], last.unsqueeze(2)).then_inc(ends_made[q], 1)
                        dve.wait_ge(picked[q], it + 2)
                        view = pick_ps[q][:, 0:BATCH * (HEADS + 1)].rearrange("p (b h) -> p b h", b=BATCH)
                        dve.tensor_scalar(pen[q][:, :].unsqueeze(2), view[:, :, HEADS:HEADS + 1], -1.0, -FAR, ALU.add, ALU.mult)\
                            .then_inc(penal[q], 1)
                        dve.wait_ge(penal[q], it + 1)
                        dve.tensor_tensor(cand[q][:, :, :], view[:, :, 0:HEADS], spread(pen[q][:, :], HEADS), ALU.add)\
                            .then_inc(best[q], 1)
                        dve.wait_ge(best[q], it + 1)
                        add_items(dve, m, it, q, cand[q][:, :, :].rearrange("p b h -> p (b h)"), 0, HEADS, added,
                                  acc=m.al_max, op=ALU.max, last=sums_read[q])

            @block.tensor
            def _(pe):
                for q in range(2):
                    pe.sem_inc(turned[q], 1)
                    pe.sem_inc(turned_back[q], 1)
                    pe.sem_inc(picked[q], 1)
                with pe.Fori(0, LOOPS) as it:
                    for q in range(2):
                        g.wait(pe, q, it)
                        pe.wait_ge(scanned[q], it + 1)
                        pe.transpose(turn_ps[q][0:ROWS, 0:P], g.rows[q][:, :, :].rearrange("p b h -> p (b h)"),
                                     m.ident[:, :]).then_inc(turned[q], 1)
                        pe.wait_ge(scanned[q], it + 2)
                        pe.wait_ge(ends_made[q], it * 2 + 1)
                        pe.matmul(back_ps[q][:, 0:ROWS], run_max[q][:, :], m.ident[0:ROWS, 0:ROWS], start=True,
                                  stop=True).then_inc(turned_back[q], 1)
                        pe.wait_ge(ends_made[q], it * 2 + 3)
                        pe.wait_ge(hot_made[q], it + 1)
                        pe.wait_ge(sums_read[q], it + 1)
                        sum_items(pe, hot[q], ends[q], pick_ps[q], HEADS + 1, picked[q])


def gat_self_loops(nc, m, layer):
    _, width = gat_shape(layer)
    with Stage(nc, f"gat_self{layer}") as st:
        step, powered = st.sem("step"), st.sem("powered")
        logit, low = st.sb("logit", [P, NB, HEADS]), st.sb("low", [P, NB, HEADS])
        al_s = m.node_out[:, :, width:width + HEADS]
        al_d, top = m.dst_tab[:, :, 0:HEADS], m.dst_tab[:, :, HEADS:2 * HEADS]
        own = m.acc[:, :, width:width + HEADS]
        with nc.Block() as block:
            @block.vector
            def _(dve):
                n = [0]

                def then(ins):
                    n[0] += 1
                    ins.then_inc(step, 1)
                    dve.wait_ge(step, n[0])

                then(dve.tensor_tensor(top, m.al_max[:, :, :], al_s, ALU.max))
                then(dve.tensor_tensor(top, top, al_d, ALU.add))
                then(dve.scalar_tensor_tensor(top, top, 0.2, top, ALU.mult, ALU.max))
                then(dve.tensor_tensor(logit[:, :, :], al_s, al_d, ALU.add))
                then(dve.scalar_tensor_tensor(low[:, :, :], logit[:, :, :], 0.2, logit[:, :, :], ALU.mult, ALU.max))
                then(dve.tensor_tensor(low[:, :, :], low[:, :, :], top, ALU.subtract))
                dve.wait_ge(powered, 1)
                for h in range(HEADS):
                    c = width // HEADS
                    dve.tensor_tensor(m.acc[:, :, h * c:(h + 1) * c], m.node_out[:, :, h * c:(h + 1) * c],
                                      spread(m.acc[:, :, width + h:width + h + 1].rearrange("p b o -> p (b o)"), c), ALU.mult)

            @block.scalar
            def _(act):
                act.wait_ge(step, 6)
                act.activation(own, low[:, :, :], ACT.Exp).then_inc(powered, 1)


def gat_sum_pass(nc, m, layer):
    _, width = gat_shape(layer)
    c, full = width // HEADS, width + HEADS
    halves = width // 128
    with Stage(nc, f"gat_sum{layer}") as st:
        g = Gather(nc, m, st, m.xw_table if width == 256 else m.xw_table2, full)
        dst_loaded, dst_hot, dst_rows = st.pair("dst_loaded"), st.pair("dst_hot"), st.pair("dst_rows")
        logit, leaky, shifted, powered = (st.pair(n) for n in ("logit", "leaky", "shifted", "powered"))
        msg_made, hot_made, summed = st.pair("msg"), st.pair("edge_hot"), st.pair("summed")
        added, sums_read = st.sem("added"), st.pair("sums_read")
        dst = st.pair_sb("dst", [P, BATCH * P])
        dhot = st.pair_sb("dhot", [P, BATCH * P])
        hot = st.pair_sb("hot", [P, BATCH, P])
        lg = st.pair_sb("lg", [P, BATCH, HEADS])
        e = st.pair_sb("e", [P, BATCH, HEADS])
        msg = st.pair_sb("msg_s", [P, BATCH, width])
        row_ps, den_ps = [m.ps[0], m.ps[1]], [m.ps[2], m.ps[3]]
        sum_ps = [m.ps[4:6], m.ps[6:8]]
        with nc.Block() as block:
            @block.gpsimd
            def _(pool):
                g.program(pool, msg_made)

            @block.sync
            def _(sp):
                destination_rows(sp, m, dst, dst_hot, dst_loaded)

            @block.scalar
            def _(act):
                with act.Fori(0, LOOPS) as it:
                    for q in range(2):
                        act.wait_ge(shifted[q], it + 1)
                        act.wait_ge(summed[q], it + 1)
                        act.activation(e[q][:, :, :], lg[q][:, :, :], ACT.Exp).then_inc(powered[q], 1)

            @block.vector
            def _(dve):
                dve.sem_inc(added, 1)
                for q in range(2):
                    dve.sem_inc(dst_hot[q], 1)
                    dve.sem_inc(msg_made[q], 1)
                    dve.sem_inc(sums_read[q], 1)
                    dve.sem_inc(logit[q], 1)
                with dve.Fori(0, LOOPS) as it:
                    for q in range(2):
                        dve.wait_ge(dst_loaded[q], it * 16 + 16)
                        dve.wait_ge(dst_rows[q], it + 1)
                        dve.tensor_scalar(dhot[q][:, :], dst[q][:, :], m.iota_col[:, 0:1], None, ALU.is_equal)\
                            .then_inc(dst_hot[q], 1)
                        dve.wait_ge(summed[q], it + 1)
                        dve.tensor_tensor(hot[q][:, :, :], repeat(m.iota_row[:, :], BATCH),
                                          spread(m.dst_l[:, ds(item(it, q), BATCH)], P), ALU.is_equal)\
                            .then_inc(hot_made[q], 1)
                        g.wait(dve, q, it)
                        dve.wait_ge(dst_rows[q], it + 2)
                        view = row_ps[q][:, 0:BATCH * 2 * HEADS].rearrange("p (b h) -> p b h", b=BATCH)
                        dve.tensor_tensor(lg[q][:, :, :], g.rows[q][:, :, width:full], view[:, :, 0:HEADS], ALU.add)\
                            .then_inc(logit[q], 1)
                        dve.wait_ge(logit[q], it * 2 + 2)
                        dve.scalar_tensor_tensor(lg[q][:, :, :], lg[q][:, :, :], 0.2, lg[q][:, :, :], ALU.mult, ALU.max)\
                            .then_inc(leaky[q], 1)
                        dve.wait_ge(leaky[q], it + 1)
                        dve.tensor_tensor(lg[q][:, :, :], lg[q][:, :, :], view[:, :, HEADS:2 * HEADS], ALU.subtract)\
                            .then_inc(shifted[q], 1)
                        dve.sem_inc(logit[q], 1)
                        dve.wait_ge(powered[q], it + 1)
                        dve.tensor_tensor(msg[q][:, :, :].rearrange("p b (h c) -> p (b h) c", c=c),
                                          g.rows[q][:, :, 0:width].rearrange("p b (h c) -> p b h c", c=c),
                                          spread(e[q][:, :, :].rearrange("p b h -> p (b h)"), c), ALU.mult)\
                            .then_inc(msg_made[q], 1)
                        dve.wait_ge(summed[q], it + 2)
                        add_items(dve, m, it, q, den_ps[q], width, HEADS, added, 2, 0)
                        add_items(dve, m, it, q, sum_ps[q], 0, width, added, 2, 1, last=sums_read[q])

            @block.tensor
            def _(pe):
                for q in range(2):
                    pe.sem_inc(dst_rows[q], 1)
                    pe.sem_inc(summed[q], 1)
                with pe.Fori(0, LOOPS) as it:
                    for q in range(2):
                        pe.wait_ge(dst_hot[q], it + 2)
                        pe.wait_ge(logit[q], it * 2 + 1)
                        destination_gather(pe, m, it, q, dhot[q], m.dst_tab, 2 * HEADS, row_ps[q], dst_rows[q])
                        pe.wait_ge(hot_made[q], it + 1)
                        pe.wait_ge(msg_made[q], it + 2)
                        pe.wait_ge(sums_read[q], it + 1)
                        for j in range(BATCH):
                            pe.matmul(den_ps[q][:, j * HEADS:(j + 1) * HEADS], hot[q][:, j, :], e[q][:, j, :],
                                      start=True, stop=True)
                            ins = pe.matmul(place(sum_ps[q], j, width), hot[q][:, j, :], msg[q][:, j, :], start=True, stop=True)
                        ins.then_inc(summed[q], 1)


def place(banks, j, width):
    if not isinstance(banks, list):
        return banks[:, j * width:(j + 1) * width]
    per = 512 // width
    return banks[j // per][:, (j % per) * width:(j % per + 1) * width]


def destination_rows(sp, m, dst, read, loaded):
    with sp.Fori(0, LOOPS) as it:
        for q in range(2):
            sp.wait_ge(read[q], it + 1)
            sp.dma_start(dst[q][:, :], m.dst_rows[ds(item(it, q), BATCH), :].rearrange("b e -> (b e)")
                         .partition_broadcast(P)).then_inc(loaded[q], 16)


def destination_gather(pe, m, it, q, dhot, table, width, bank, done):
    for j in range(BATCH):
        b = pe.value_load(m.block_tab[0:1, ds(item(it, q, j), 1)], min_val=0, max_val=NB - 1)
        ins = pe.matmul(bank[:, j * width:(j + 1) * width], dhot[:, j * P:(j + 1) * P],
                        table[:, ds(b, 1), :].rearrange("p o w -> p (o w)"), start=True, stop=True)
    ins.then_inc(done, 1)


def gat_nodes(nc, m, a, layer, cur, nxt):
    kt, width = gat_shape(layer)
    ot, c = width // P, width // HEADS
    chunks = [(i, min(CHUNK, N - i)) for i in range(0, N, CHUNK)]
    with Stage(nc, f"gat_nodes{layer}") as st:
        loaded, step, inverted, staged = st.sem("loaded"), st.sem("step"), st.sem("inverted"), st.sem("staged")
        product, stored, rooted = st.sem("product"), st.sem("stored"), st.sem("rooted")
        adj = st.sb("adj", [P, kt, width])
        bias, bias2, gain, shift = (st.sb(n, [P, ot]) for n in ("bias", "bias2", "gain", "shift"))
        rden = st.sb("rden", [P, NB, HEADS])
        flat = st.sb("flat", [P, width])
        stats, agg = st.sb("stats", [P, ot, len(chunks), 6]), st.sb("agg", [P, ot, 2])
        std = st.sb("std", [P, ot])
        o_ps = m.ps[0]
        columns = lambda name: a[f"L2_gnn_{name}{layer}"].rearrange("(k p) -> p k", p=P)
        with nc.Block() as block:
            @block.sync
            def _(sp):
                sp.dma_start(adj[:, :, :], a[f"L2_gnn_adj_w{layer}"].rearrange("(k p) o -> p k o", p=P)).then_inc(loaded, 16)
                with nc.allow_non_contiguous_dma(reason="four short vectors"):
                    for tile, name in ((bias, "gat_b"), (bias2, "adj_b"), (gain, "bn_g"), (shift, "bn_b")):
                        sp.dma_start(tile[:, :], columns(name)).then_inc(loaded, 16)

            @block.vector
            def _(dve):
                n = [0]

                def then(ins):
                    n[0] += 1
                    ins.then_inc(step, 1)
                    dve.wait_ge(step, n[0])

                dve.wait_ge(loaded, 16 * 5)
                then(dve.tensor_tensor(bias[:, :], bias[:, :], bias2[:, :], ALU.add))
                then(dve.reciprocal(rden[:, :, :], m.acc[:, :, width:width + HEADS]))
                with dve.Fori(0, NB) as b:
                    dve.wait_ge(product, b + 1)
                    dve.tensor_tensor(flat[:, :].rearrange("p (h c) -> p h c", c=c),
                                      m.acc[:, ds(b, 1), 0:width].rearrange("p o (h c) -> p (o h) c", c=c),
                                      spread(rden[:, ds(b, 1), :].rearrange("p o h -> p (o h)"), c), ALU.mult).then_inc(staged, 1)
                dve.wait_ge(stored, NB + 1)
                for o in range(ot):
                    for i, (at, size) in enumerate(chunks):
                        ins = dve.bn_stats(stats[:, o, i, :], nxt[:, o, at:at + size])
                    then(ins)
                    then(dve.bn_aggr(agg[:, o, :], stats[:, o, :, :].rearrange("p i s -> p (i s)")))
                then(dve.tensor_scalar(std[:, :].unsqueeze(2), agg[:, :, 1:2], 1e-5, None, ALU.add))
                dve.sem_inc(inverted, 1)
                dve.wait_ge(rooted, 1)
                then(dve.reciprocal(std[:, :], std[:, :]))
                then(dve.tensor_tensor(gain[:, :], gain[:, :], std[:, :], ALU.mult))
                then(dve.tensor_tensor(std[:, :].unsqueeze(2), agg[:, :, 0:1], gain[:, :].unsqueeze(2), ALU.mult))
                then(dve.tensor_tensor(shift[:, :], shift[:, :], std[:, :], ALU.subtract))
                dve.sem_inc(inverted, 1)

            @block.scalar
            def _(act):
                act.sem_inc(stored, 1)
                act.wait_ge(step, 2)
                with act.Fori(0, NB) as b:
                    act.wait_ge(product, b + 2)
                    for o in range(ot):
                        ins = act.activation(nxt[:, o, ds(b * P, P)], o_ps[:, o * P:(o + 1) * P], ACT.Identity, bias=bias[:, o:o + 1])
                    ins.then_inc(stored, 1)
                act.wait_ge(inverted, 1)
                act.activation(std[:, :], std[:, :], ACT.Sqrt).then_inc(rooted, 1)
                act.wait_ge(inverted, 2)
                for o in range(ot):
                    act.activation(nxt[:, o, :], nxt[:, o, :], ACT.Silu, bias=shift[:, o:o + 1], scale=gain[:, o:o + 1])

            @block.tensor
            def _(pe):
                pe.sem_inc(product, 1)
                pe.wait_ge(loaded, 16 * 5)
                with pe.Fori(0, NB) as b:
                    pe.wait_ge(staged, b + 1)
                    pe.wait_ge(stored, b + 1)
                    for o in range(ot):
                        pe.matmul(o_ps[:, o * P:(o + 1) * P], flat[:, o * P:(o + 1) * P], m.ident[:, :], start=True, stop=False)
                        for k in range(kt):
                            ins = pe.matmul(o_ps[:, o * P:(o + 1) * P], adj[:, k, o * P:(o + 1) * P], cur[:, k, ds(b * P, P)],
                                            start=False, stop=k == kt - 1)
                    ins.then_inc(product, 1)


def diffusion_out(nc, m, a, cur):
    with Stage(nc, "gat_out") as st:
        loaded, staged, product, stored = st.sem("loaded"), st.sem("staged"), st.sem("product"), st.sem("stored")
        w, bias, flat, y = st.sb("w", [P, DIM]), st.sb("bias", [P, DIM]), st.sb("flat", [P, P]), st.sb("y", [P, NB, DIM])
        o_ps = m.ps[0]
        with nc.Block() as block:
            @block.sync
            def _(sp):
                sp.dma_start(w[:, :], a["L2_gnn_out_w"]).then_inc(loaded, 16)
                sp.dma_start(bias[:, :], a["L2_gnn_out_b"].partition_broadcast(P)).then_inc(loaded, 16)

            @block.scalar
            def _(act):
                with act.Fori(0, NB) as b:
                    act.wait_ge(product, b + 1)
                    act.activation(flat[:, :], cur[:, 0, ds(b * P, P)], ACT.Copy).then_inc(staged, 1)

            @block.vector
            def _(dve):
                dve.sem_inc(stored, 1)
                dve.wait_ge(loaded, 32)
                with dve.Fori(0, NB) as b:
                    dve.wait_ge(product, b + 2)
                    dve.tensor_tensor(y[:, ds(b, 1), :], o_ps[:, 0:DIM].unsqueeze(1), bias[:, :].unsqueeze(1), ALU.add)\
                        .then_inc(stored, 1)

            @block.tensor
            def _(pe):
                pe.sem_inc(product, 1)
                pe.wait_ge(loaded, 32)
                with pe.Fori(0, NB) as b:
                    pe.wait_ge(staged, b + 1)
                    pe.wait_ge(stored, b + 1)
                    pe.matmul(o_ps[:, 0:DIM], flat[:, :], w[:, :], start=True, stop=True).then_inc(product, 1)
        residual_norm(nc, m, y)


def attention_tables(nc, m, a):
    with Stage(nc, "att_tab") as st:
        loaded, staged, turned = st.sem("loaded"), st.sem("staged"), st.sem("turned")
        evacuated, product, stored, written = st.sem("evacuated"), st.sem("product"), st.sem("stored"), st.sem("written")
        w, bias = st.sb("w", [DIM, 3 * DIM]), st.sb("bias", [P, 3 * DIM])
        flat, tall = st.sb("flat", [P, P]), st.sb("tall", [DIM, P])
        pre = st.sb("pre", [P, NB, 2 * DIM])
        x_t, res = m.ps[0], m.ps[1]
        with nc.Block() as block:
            @block.sync
            def _(sp):
                for i, k in enumerate("KVQ"):
                    part = slice(i * DIM, (i + 1) * DIM)
                    sp.dma_start(w[:, part], a[f"L3_gnn_W{k}"]).then_inc(loaded, 16)
                    sp.dma_start(bias[:, part], a[f"L3_gnn_b{k}"].partition_broadcast(P)).then_inc(loaded, 16)
                sp.wait_ge(stored, 2 * NB + 1)
                sp.dma_start(m.pre_table.rearrange("(b p) d -> p b d", p=P), pre[:, :, :]).then_inc(written, 16)
                sp.wait_ge(written, 16)

            @block.vector
            def _(dve):
                dve.memset(flat[:, :], 0.0).then_inc(stored, 1)
                dve.wait_ge(stored, 1)
                dve.wait_ge(loaded, 96)
                with dve.Fori(0, NB) as b:
                    dve.wait_ge(turned, b + 1)
                    dve.tensor_copy(flat[:, 0:DIM].unsqueeze(1), m.x[:, ds(b, 1), :]).then_inc(staged, 1)
                    dve.wait_ge(product, b + 2)
                    dve.tensor_tensor(pre[:, ds(b, 1), :], res[:, 0:2 * DIM].unsqueeze(1), bias[:, 0:2 * DIM].unsqueeze(1),
                                      ALU.add).then_inc(stored, 1)
                    dve.tensor_tensor(m.q_tab[:, ds(b, 1), :], res[:, 2 * DIM:3 * DIM].unsqueeze(1),
                                      bias[:, 2 * DIM:3 * DIM].unsqueeze(1), ALU.add).then_inc(stored, 1)

            @block.tensor
            def _(pe):
                pe.sem_inc(turned, 1)
                pe.sem_inc(product, 1)
                pe.wait_ge(loaded, 96)
                with pe.Fori(0, NB) as b:
                    pe.wait_ge(staged, b + 1)
                    pe.wait_ge(evacuated, b + 1)
                    pe.transpose(x_t[:, 0:P], flat[:, :], m.ident[:, :]).then_inc(turned, 1)
                    pe.wait_ge(evacuated, b + 2)
                    pe.wait_ge(stored, b * 2 + 1)
                    pe.matmul(res[:, 0:3 * DIM], tall[:, :], w[:, :], start=True, stop=True).then_inc(product, 1)

            @block.scalar
            def _(act):
                act.sem_inc(evacuated, 1)
                with act.Fori(0, NB) as b:
                    act.wait_ge(turned, b + 2)
                    act.wait_ge(product, b + 1)
                    act.activation(tall[:, :], x_t[0:DIM, 0:P], ACT.Copy).then_inc(evacuated, 1)


def attention_pass(nc, m, a):
    d = DIM // HEADS
    scale = float(np.float32(1.0 / np.sqrt(d)))
    PAIRS = BATCH // 2
    with Stage(nc, "att") as st:
        g = Gather(nc, m, st, m.pre_table, 2 * DIM)
        w_zeroed, w_loaded, attr_loaded = st.sem("w_zeroed"), st.sem("w_loaded"), st.pair("attr_loaded")
        dst_loaded, dst_hot, dst_rows = st.pair("dst_loaded"), st.pair("dst_hot"), st.pair("dst_rows")
        turned, evacuated, edge_part = st.pair("turned"), st.pair("evacuated"), st.pair("edge_part")
        eb, kq, kqe, score, scaled, clipped, powered = (st.pair(n) for n in ("eb", "kq", "kqe", "score", "scaled", "clipped", "powered"))
        msg_made, hot_made, summed = st.pair("msg"), st.pair("edge_hot"), st.pair("summed")
        added, sums_read = st.sem("added"), st.pair("sums_read")
        w = st.sb("w", [P, P])
        bias = st.sb("bias", [P, DIM])
        attr = st.pair_sb("attr", [P, BATCH, DIM])
        attr_t = st.pair_sb("attr_t", [P, PAIRS * P])
        dst = st.pair_sb("dst", [P, BATCH * P])
        dhot = st.pair_sb("dhot", [P, BATCH * P])
        hot = st.pair_sb("hot", [P, BATCH, P])
        prod = st.pair_sb("prod", [P, BATCH * DIM])
        edge = st.pair_sb("edge", [P, BATCH, DIM])
        sc = st.pair_sb("sc", [P, BATCH * HEADS])
        e = st.pair_sb("e", [P, BATCH * HEADS])
        msg = st.pair_sb("msg_s", [P, BATCH, DIM])
        turn_ps, edge_ps, row_ps, sum_ps = m.ps[0:2], m.ps[2:4], m.ps[4:6], m.ps[6:8]
        with nc.Block() as block:
            @block.gpsimd
            def _(pool):
                g.program(pool, msg_made)

            @block.sync
            def _(sp):
                sp.wait_ge(w_zeroed, 1)
                for i in range(2):
                    part = slice(i * DIM, (i + 1) * DIM)
                    sp.dma_start(w[part, part], a["L3_gnn_WE"]).then_inc(w_loaded, 16)
                sp.dma_start(bias[:, :], a["L3_gnn_bE"].partition_broadcast(P)).then_inc(w_loaded, 16)
                attr_loads(sp, m, a["edge_attr_64"], attr, turned, attr_loaded)

            @block.scalar
            def _(act):
                for q in range(2):
                    act.sem_inc(evacuated[q], 1)
                with act.Fori(0, LOOPS) as it:
                    for q in range(2):
                        act.wait_ge(dst_hot[q], it + 1)
                        act.dma_start(dst[q][:, :], m.dst_rows[ds(item(it, q), BATCH), :].rearrange("b e -> (b e)")
                                      .partition_broadcast(P)).then_inc(dst_loaded[q], 16)
                        act.wait_ge(turned[q], it + 2)
                        act.wait_ge(edge_part[q], it + 1)
                        act.activation(attr_t[q][:, :], turn_ps[q][:, 0:PAIRS * P], ACT.Copy).then_inc(evacuated[q], 1)
                        act.wait_ge(clipped[q], it + 1)
                        act.wait_ge(msg_made[q], it + 1)
                        act.activation(e[q][:, :], sc[q][:, :], ACT.Exp).then_inc(powered[q], 1)

            @block.vector
            def _(dve):
                dve.memset(w[:, :], 0.0).then_inc(w_zeroed, 1)
                dve.memset(m.acc[:, :, :], 0.0).then_inc(added, 1)
                for q in range(2):
                    for s in (dst_hot, msg_made, sums_read, eb, kq):
                        dve.sem_inc(s[q], 1)
                dve.wait_ge(w_loaded, 48)
                with dve.Fori(0, LOOPS) as it:
                    for q in range(2):
                        dve.wait_ge(dst_loaded[q], it * 16 + 16)
                        dve.wait_ge(dst_rows[q], it + 1)
                        dve.tensor_scalar(dhot[q][:, :], dst[q][:, :], m.iota_col[:, 0:1], None, ALU.is_equal)\
                            .then_inc(dst_hot[q], 1)
                        dve.wait_ge(summed[q], it + 1)
                        dve.tensor_tensor(hot[q][:, :, :], repeat(m.iota_row[:, :], BATCH),
                                          spread(m.dst_l[:, ds(item(it, q), BATCH)], P), ALU.is_equal)\
                            .then_inc(hot_made[q], 1)
                        dve.wait_ge(edge_part[q], it + 2)
                        dve.tensor_tensor(edge[q][:, :, :], edge_ps[q][:, 0:BATCH * DIM].rearrange("p (b d) -> p b d", d=DIM),
                                          repeat(bias[:, :], BATCH), ALU.add).then_inc(eb[q], 1)
                        g.wait(dve, q, it)
                        dve.wait_ge(dst_rows[q], it + 2)
                        dve.tensor_tensor(prod[q][:, :].rearrange("p (b d) -> p b d", d=DIM), g.rows[q][:, :, 0:DIM],
                                          row_ps[q][:, 0:BATCH * DIM].rearrange("p (b d) -> p b d", d=DIM), ALU.mult)\
                            .then_inc(kq[q], 1)
                        dve.wait_ge(kq[q], it + 2)
                        dve.wait_ge(eb[q], it + 2)
                        dve.tensor_tensor(prod[q][:, :], prod[q][:, :], edge[q][:, :, :].rearrange("p b d -> p (b d)"), ALU.mult)\
                            .then_inc(kqe[q], 1)
                        dve.wait_ge(kqe[q], it + 1)
                        dve.tensor_reduce(sc[q][:, :], prod[q][:, :].rearrange("p (h d) -> p h d", d=d), AX.X, ALU.add)\
                            .then_inc(score[q], 1)
                        dve.wait_ge(score[q], it + 1)
                        dve.tensor_scalar(sc[q][:, :], sc[q][:, :], scale, 5.0, ALU.mult, ALU.min).then_inc(scaled[q], 1)
                        dve.wait_ge(scaled[q], it + 1)
                        dve.tensor_single_scalar(sc[q][:, :], sc[q][:, :], -5.0, ALU.max).then_inc(clipped[q], 1)
                        dve.wait_ge(powered[q], it + 1)
                        dve.tensor_tensor(msg[q][:, :, :].rearrange("p b (h d) -> p (b h) d", d=d),
                                          g.rows[q][:, :, DIM:2 * DIM].rearrange("p b (h d) -> p b h d", d=d),
                                          spread(e[q][:, :], d), ALU.mult).then_inc(msg_made[q], 1)
                        dve.wait_ge(summed[q], it + 2)
                        add_items(dve, m, it, q, sum_ps[q], 0, DIM, added, last=sums_read[q])

            @block.tensor
            def _(pe):
                for q in range(2):
                    for s in (turned, dst_rows, edge_part, summed):
                        pe.sem_inc(s[q], 1)
                pe.wait_ge(w_loaded, 48)
                with pe.Fori(0, LOOPS) as it:
                    for q in range(2):
                        pe.wait_ge(attr_loaded[q], it * (16 * BATCH) + 16 * BATCH)
                        pe.wait_ge(evacuated[q], it + 1)
                        for i in range(PAIRS):
                            ins = pe.transpose(turn_ps[q][:, i * P:(i + 1) * P],
                                               attr[q][:, 2 * i:2 * i + 2, :].rearrange("p b d -> p (b d)"), m.ident[:, :])
                        ins.then_inc(turned[q], 1)
                        pe.wait_ge(evacuated[q], it + 2)
                        pe.wait_ge(eb[q], it + 1)
                        for i in range(PAIRS):
                            ins = pe.matmul(edge_ps[q][:, i * P:(i + 1) * P], attr_t[q][:, i * P:(i + 1) * P], w[:, :],
                                            start=True, stop=True)
                        ins.then_inc(edge_part[q], 1)
                        pe.wait_ge(dst_hot[q], it + 2)
                        pe.wait_ge(kq[q], it + 1)
                        destination_gather(pe, m, it, q, dhot[q], m.q_tab, DIM, row_ps[q], dst_rows[q])
                        pe.wait_ge(hot_made[q], it + 1)
                        pe.wait_ge(msg_made[q], it + 2)
                        pe.wait_ge(sums_read[q], it + 1)
                        sum_items(pe, hot[q], msg[q], sum_ps[q], DIM, summed[q])


_NAMES = ["L0_gnn_rel_emb", "L0_gnn_w_loop", "L0_gnn_w_fwd", "L0_gnn_w_bwd", "x", "edge_attr_32", "edge_attr_64",
          "edge_weight", "node_vec", "L1_gnn_msg_w1", "L1_gnn_msg_b1", "L1_gnn_msg_w2", "L1_gnn_msg_b2",
          "L1_gnn_upd_w1", "L1_gnn_upd_b1", "L1_gnn_upd_w2", "L1_gnn_upd_b2",
          "L2_gnn_init_w", "L2_gnn_init_b", "L2_gnn_te_w1", "L2_gnn_te_b1", "L2_gnn_te_w2", "L2_gnn_te_b2",
          "L2_gnn_out_w", "L2_gnn_out_b"]
_NAMES += [f"L2_gnn_{n}{i}" for i in range(3)
           for n in ("gat_w", "att_src", "att_dst", "gat_b", "adj_w", "adj_b", "bn_g", "bn_b")]
_NAMES += [f"L3_gnn_{k}{n}" for n in "QKEV" for k in "Wb"]
DEBUG = None


def kernel(**inputs):
    import concourse.bacc as bacc
    from concourse.bass_utils import run_bass_kernel_spmd

    nc = bacc.Bacc("TRN2", target_bir_lowering=False, num_devices=1)
    arrays = {n: np.ascontiguousarray(inputs[n]) for n in _NAMES}
    arrays["edges"] = np.stack([np.asarray(inputs["src"]), np.asarray(inputs["dst"]), np.asarray(inputs["edge_type_200"])])
    half = P // 2
    freq = np.power(np.float32(1.0 / 10000.0), np.arange(half, dtype=np.float32) / np.float32(half)).astype(np.float32)
    phase = np.repeat(np.array([0.0, np.pi / 2], np.float32), half)
    arrays["freq"] = np.stack([np.concatenate([freq, freq]), phase], axis=1)
    a = {n: nc.dram_tensor(f"in_{n}", v.shape, mybir.dt.from_np(v.dtype), kind="ExternalInput").ap()
         for n, v in arrays.items()}
    out = nc.dram_tensor("out", (N, DIM), F32, kind="ExternalOutput").ap()
    build(nc, a, out, DEBUG)
    r = run_bass_kernel_spmd(nc, [{f"in_{n}": v for n, v in arrays.items()}], core_ids=[0])
    return r.results[0]["out"]
```

```python
from contextlib import ExitStack

import numpy as np
import concourse.bass as bass
from concourse import mybir

F32 = mybir.dt.float32
I32 = mybir.dt.int32
BF16 = mybir.dt.bfloat16
ALU = mybir.AluOpType
ACT = mybir.ActivationFunctionType
AX = mybir.AxisListType

P = 128
N, E, DIM = 3125, 103125, 64
NB = -(-N // P)
NP = NB * P
GROUP = 4
GE = GROUP * P
PAIR = 2
BATCH = PAIR * GROUP
NG = -(-((E + NB * (GE - 1)) // GE) // (2 * PAIR)) * 2 * PAIR
STEPS = NG // PAIR
KG = -(-NG // P)
NGP = KG * P
NIP = NGP * GROUP
ER, EC = 125, E // 125
HALF_REL = 100
HEADS = 8
PARTS = 3
FAR = -1.0e30
CHUNK = 512
ROUND = 5
ds = bass.ds


class Mem:
    pass


def build(nc, a, out):
    m = Mem()
    m.norms = 0
    with ExitStack() as ctx:
        def sb(name, shape, dt=F32):
            return ctx.enter_context(nc.sbuf_tensor(name, shape, dt))

        def dram(name, shape, dt=F32):
            return nc.dram_tensor(name, shape, dt, kind="Internal").ap()

        m.group_first = dram("group_first", [NGP], I32)
        m.group_block = dram("group_block", [NGP], I32)
        m.edge_rows = dram("edge_rows", [4, NGP, GE], I32)
        m.dst_rows = dram("dst_rows", [NGP, GE])
        m.rel_rows = dram("rel_rows", [NGP, GE])
        m.run_rows = dram("run_rows", [NGP, GE])
        m.x_table = dram("x_table", [NP, DIM])
        m.pre_table = dram("pre_table", [NP, 2 * DIM])
        m.xw_table = dram("xw_table", [NP, 264])
        m.xw_table2 = dram("xw_table2", [NP, 136])
        m.al_table = dram("al_table", [NP, HEADS])

        m.ident = sb("ident", [P, P])
        m.iota_row = sb("iota_row", [P, P])
        m.iota_col = sb("iota_col", [P, 1])
        m.ones = sb("ones", [P, P])
        m.src_i = sb("src_i", [P, NIP], I32)
        m.dst_l = sb("dst_l", [P, NIP])
        m.w_fwd = sb("w_fwd", [P, NIP])
        m.w_bwd = sb("w_bwd", [P, NIP])
        m.run_end = sb("run_end", [P, NIP])
        m.late = sb("late", [P, KG])
        m.blk_col = sb("blk_col", [P, KG])
        m.first_tab = sb("first_tab", [1, NGP], I32)
        m.block_tab = sb("block_tab", [1, NGP], I32)
        m.x = sb("x", [P, NB, DIM])
        m.acc = sb("acc", [P, NB, 264])
        m.ps = [ctx.enter_context(nc.psum_tensor(f"bank{i}", [P, 512], F32)) for i in range(8)]

        constants(nc, m)
        group_tables(nc, m, a)
        edge_columns(nc, m, a)
        load_nodes(nc, m, a)
        with ExitStack() as c:
            m.y = c.enter_context(nc.sbuf_tensor("y", [P, NB, DIM], F32))
            compgcn_pass(nc, m, a, 0, a["x"])
            compgcn_nodes(nc, m, a, 0, m.x, m.y)
            compgcn_pass(nc, m, a, 1, m.x_table)
            compgcn_nodes(nc, m, a, 1, m.y, m.y)
            residual_norm(nc, m, m.y)
        message_tables(nc, m, a)
        message_pass(nc, m, a)
        message_nodes(nc, m, a)
        with ExitStack() as c:
            def cb(name, shape, dt=F32):
                return c.enter_context(nc.sbuf_tensor(name, shape, dt))
            m.ft = cb("ft", [P, 2, NP])
            m.ft2 = cb("ft2", [P, 2, NP])
            m.node_out = cb("node_out", [P, NB, 272])
            m.al_max = cb("al_max", [P, NB, HEADS])
            m.dst_tab = cb("dst_tab", [P, NB, 2 * HEADS])
            m.dst_parts = cb("dst_parts", [P, NB, PARTS * 2 * HEADS], BF16)
            cur, nxt = m.ft, m.ft2
            diffusion_embed(nc, m, a, cur)
            for layer in range(3):
                gat_tables(nc, m, a, layer, cur)
                gat_max_pass(nc, m, layer)
                gat_self_loops(nc, m, layer)
                gat_sum_pass(nc, m, layer)
                gat_nodes(nc, m, a, layer, cur, nxt)
                cur, nxt = nxt, cur
            diffusion_out(nc, m, a, cur)
        with ExitStack() as c:
            m.q_tab = c.enter_context(nc.sbuf_tensor("q_tab", [P, NB, DIM], F32))
            attention_tables(nc, m, a)
            attention_pass(nc, m, a)
        residual_norm(nc, m, m.acc[:, :, 0:DIM])
        finish(nc, m, out)


class Stage:

    def __init__(self, nc, name):
        self.nc, self.name, self.stack, self.sems = nc, name, ExitStack(), []

    def sem(self, name):
        s = self.nc.alloc_semaphore(f"{self.name}_{name}")
        self.sems.append(s)
        return s

    def pair(self, name):
        return [self.sem(f"{name}_{q}") for q in range(2)]

    def sb(self, name, shape, dt=F32):
        return self.stack.enter_context(self.nc.sbuf_tensor(f"{self.name}_{name}", shape, dt))

    def pair_sb(self, name, shape, dt=F32):
        return [self.sb(f"{name}_{q}", shape, dt) for q in range(2)]

    def __enter__(self):
        return self

    def __exit__(self, *e):
        if e[0] is None:
            self.nc.clear_and_free_semaphores(self.sems)
            self.nc.all_engine_barrier()
        self.stack.close()


def spread(ap, count):
    return ap.unsqueeze(2).to_broadcast([ap.shape[0], ap.shape[1], count])


def repeat(ap, count):
    return ap.unsqueeze(1).to_broadcast([ap.shape[0], count, ap.shape[1]])


def constants(nc, m):
    with Stage(nc, "const") as st:
        made = st.sem("const_made")
        zeroed = st.sem("ident_zeroed")
        with nc.Block() as block:
            @block.gpsimd
            def _(pool):
                pool.iota(m.iota_row[:, :], [[1, P]], base=0, channel_multiplier=0,
                          allow_small_or_imprecise_dtypes=True).then_inc(made, 1)
                pool.iota(m.iota_col[:, :], [[1, 1]], base=0, channel_multiplier=1,
                          allow_small_or_imprecise_dtypes=True).then_inc(made, 1)
                pool.memset(m.ident[:, :], 0.0).then_inc(zeroed, 1)
                pool.wait_ge(zeroed, 1)
                pool.affine_select(out=m.ident[:, :], in_=m.ident[:, :], compare_op=ALU.not_equal, fill=1.0,
                                   base=0, pattern=[[-1, P]], channel_multiplier=1).then_inc(made, 1)

            @block.vector
            def _(dve):
                dve.memset(m.ones[:, :], 1.0).then_inc(made, 1)


def group_tables(nc, m, a):
    with Stage(nc, "groups") as st:
        loaded, cast, counted, totals = st.sem("dst_loaded"), st.sem("dst_cast"), st.sem("counted"), st.sem("totals")
        step, idx_made, stored, back = st.sem("step"), st.sem("ids_made"), st.sem("tables_stored"), st.sem("tables_back")
        di, df, hit = st.sb("dst_int", [ER, EC], I32), st.sb("dst_f", [ER, EC]), st.sb("below", [ER, EC])
        cnt = st.sb("below_count", [ER, NB + 1])
        first = st.sb("first_edge", [P, NB + 1])
        n_e, n_ii = st.sb("edges_of", [P, NB]), st.sb("groups_int", [P, NB], I32)
        n_i, base = st.sb("groups_of", [P, NB]), st.sb("groups_to", [P, NB + 1])
        lag, dlag = st.sb("lag", [P, NB]), st.sb("dlag", [P, NB])
        ids, blk, e0, past = (st.sb(n, [P, KG]) for n in ("ids", "blk", "nominal", "past"))
        tab_f, tab_b = st.sb("tab_f", [P, KG], I32), st.sb("tab_b", [P, KG], I32)
        clip = st.sb("clipped", [P, KG])
        tot = m.ps[0]
        with nc.Block() as block:
            @block.sync
            def _(sp):
                sp.dma_start(di[:, :], a["edges"][1, :].rearrange("(p c) -> p c", p=ER)).then_inc(loaded, 16)
                sp.wait_ge(stored, 1)
                with nc.allow_non_contiguous_dma(reason="two small tables"):
                    sp.dma_start(m.group_first.rearrange("(k p) -> p k", p=P), tab_f[:, :]).then_inc(back, 16)
                    sp.dma_start(m.group_block.rearrange("(k p) -> p k", p=P), tab_b[:, :]).then_inc(back, 16)
                sp.wait_ge(back, 32)
                sp.dma_start(m.first_tab[:, :], m.group_first.unsqueeze(0)).then_inc(back, 16)
                sp.dma_start(m.block_tab[:, :], m.group_block.unsqueeze(0)).then_inc(back, 16)
                sp.wait_ge(back, 64)

            @block.gpsimd
            def _(pool):
                pool.iota(ids[:, :], [[P, KG]], base=0, channel_multiplier=1,
                          allow_small_or_imprecise_dtypes=True).then_inc(idx_made, 1)

            @block.vector
            def _(dve):
                n = [0]

                def then(ins):
                    n[0] += 1
                    ins.then_inc(step, 1)
                    dve.wait_ge(step, n[0])

                dve.wait_ge(loaded, 16)
                dve.memset(cnt[:, :], 0.0).then_inc(cast, 1)
                dve.tensor_copy(df[:, :], di[:, :]).then_inc(cast, 1)
                dve.wait_ge(cast, 2)
                for b in range(1, NB):
                    then(dve.tensor_scalar(hit[:, :], df[:, :], float(P * b), 0.0, ALU.is_lt, ALU.add,
                                           accum_out=cnt[:, b:b + 1]))
                dve.memset(cnt[:, NB:NB + 1], float(EC)).then_inc(counted, 1)
                dve.wait_ge(totals, 1)
                then(dve.tensor_copy(first[:, :], tot[:, 0:NB + 1]))
                then(dve.tensor_tensor(n_e[:, :], first[:, 1:NB + 1], first[:, 0:NB], ALU.subtract))
                then(dve.tensor_scalar(n_ii[:, :], n_e[:, :], float(GE - 1), None, ALU.add))
                then(dve.tensor_single_scalar(n_ii[:, :], n_ii[:, :], GE.bit_length() - 1, ALU.arith_shift_right))
                then(dve.tensor_copy(n_i[:, :], n_ii[:, :]))
                then(dve.memset(base[:, 0:1], 0.0))
                then(dve.tensor_tensor_scan(base[:, 1:NB + 1], m.ones[:, 0:NB], n_i[:, :], 0.0, ALU.mult, ALU.add))
                then(dve.scalar_tensor_tensor(lag[:, :], base[:, 0:NB], float(-GE), first[:, 0:NB], ALU.mult, ALU.add))
                then(dve.tensor_tensor(dlag[:, 1:NB], lag[:, 1:NB], lag[:, 0:NB - 1], ALU.subtract))
                dve.wait_ge(idx_made, 1)
                then(dve.memset(blk[:, :], 0.0))
                then(dve.tensor_scalar(e0[:, :], ids[:, :], float(GE), lag[:, 0:1], ALU.mult, ALU.add))
                for b in range(1, NB):
                    then(dve.tensor_scalar(past[:, :], ids[:, :], base[:, b:b + 1], None, ALU.is_ge))
                    then(dve.tensor_tensor(blk[:, :], blk[:, :], past[:, :], ALU.add))
                    then(dve.scalar_tensor_tensor(e0[:, :], past[:, :], dlag[:, b:b + 1], e0[:, :], ALU.mult, ALU.add))
                then(dve.tensor_scalar(past[:, :], ids[:, :], base[:, NB:NB + 1], float(E), ALU.is_ge, ALU.mult))
                then(dve.tensor_tensor(e0[:, :], e0[:, :], past[:, :], ALU.add))
                then(dve.tensor_scalar(clip[:, :], e0[:, :], float(E - GE), None, ALU.min))
                then(dve.tensor_tensor(m.late[:, :], e0[:, :], clip[:, :], ALU.subtract))
                then(dve.tensor_copy(m.blk_col[:, :], blk[:, :]))
                then(dve.tensor_copy(tab_f[:, :], clip[:, :]))
                dve.tensor_copy(tab_b[:, :], blk[:, :]).then_inc(stored, 1)

            @block.tensor
            def _(pe):
                pe.wait_ge(counted, 1)
                pe.matmul(tot[:, 0:NB + 1], m.ones[0:ER, :], cnt[:, :], start=True, stop=True).then_inc(totals, 1)


def edge_columns(nc, m, a):
    UN = 4
    with Stage(nc, "cols") as st:
        copied, rowed = [st.sem("rows_copied_sp"), st.sem("rows_copied_act")], st.sem("rows_loaded")
        ready, turned, kept, wrote = st.sem("rows_ready"), st.sem("turned"), st.sem("kept"), st.sem("rows_written")
        step = st.sem("step")
        ri = st.sb("int_rows", [P, KG, 4, GE], I32)
        rw = ri[:, :, 3, :].bitcast(F32)
        src, dst, rel = (st.sb(n, [P, KG, GE]) for n in ("src", "dst", "rel"))
        wf, wb, end, run = (st.sb(n, [P, KG, GE]) for n in ("wf", "wb", "end", "run"))
        tmp = st.sb("tmp", [P, KG, GE])
        count, counted = st.sb("count", [P, GE]), st.sem("counted")

        def copy_rows(eng, odd):
            with eng.Fori(0, NGP // (2 * UN)) as i:
                for u in range(UN):
                    group = ds(i * (2 * UN) + (2 * u + odd), 1)
                    e = eng.value_load(m.first_tab[0:1, group], min_val=0, max_val=E - GE)
                    eng.dma_start(m.edge_rows[:, group, :], a["edges"][:, ds(e, GE)].unsqueeze(1)).then_inc(copied[odd], 16)

        with nc.Block() as block:
            @block.sync
            def _(sp):
                copy_rows(sp, 0)
                for odd in range(2):
                    sp.wait_ge(copied[odd], 8 * NGP)
                for k in range(KG):
                    sp.dma_start(ri[:, k, :, :], m.edge_rows[:, k * P:(k + 1) * P, :].rearrange("t p e -> p t e"))\
                      .then_inc(rowed, 16)
                sp.wait_ge(ready, 1)
                for rows, tile in ((m.dst_rows, dst), (m.rel_rows, rel), (m.run_rows, run)):
                    sp.dma_start(rows.rearrange("(k p) e -> p k e", p=P), tile[:, :, :]).then_inc(wrote, 16)
                sp.wait_ge(wrote, 48)

            @block.gpsimd
            def _(pool):
                pool.iota(count[:, :], [[1, GE]], base=0, channel_multiplier=0,
                          allow_small_or_imprecise_dtypes=True).then_inc(counted, 1)

            @block.scalar
            def _(act):
                copy_rows(act, 1)

            @block.vector
            def _(dve):
                n = [0]

                def then(ins):
                    n[0] += 1
                    ins.then_inc(step, 1)
                    dve.wait_ge(step, n[0])

                dve.wait_ge(rowed, 16 * KG)
                dve.wait_ge(counted, 1)
                then(dve.tensor_copy(src[:, :, :], ri[:, :, 0, :]))
                then(dve.tensor_copy(dst[:, :, :], ri[:, :, 1, :]))
                then(dve.tensor_copy(rel[:, :, :], ri[:, :, 2, :]))
                then(dve.scalar_tensor_tensor(dst[:, :, :], spread(m.blk_col[:, :], GE), float(-P), dst[:, :, :],
                                              ALU.mult, ALU.add))
                then(dve.tensor_tensor(tmp[:, :, :], repeat(count[:, :], KG), spread(m.late[:, :], GE), ALU.is_lt))
                then(dve.scalar_tensor_tensor(dst[:, :, :], tmp[:, :, :], float(-4 * NP), dst[:, :, :],
                                              ALU.mult, ALU.add))
                then(dve.tensor_tensor(end[:, :, 0:GE - 1], dst[:, :, 0:GE - 1], dst[:, :, 1:GE], ALU.not_equal))
                for j in range(GROUP):
                    ins = dve.memset(end[:, :, (j + 1) * P - 1:(j + 1) * P], 1.0)
                then(ins)
                then(dve.tensor_single_scalar(run[:, :, 1:GE], end[:, :, 0:GE - 1], FAR, ALU.mult))
                then(dve.memset(run[:, :, 0:1], FAR))
                then(dve.tensor_single_scalar(tmp[:, :, :], rel[:, :, :], float(HALF_REL), ALU.is_ge))
                then(dve.tensor_tensor(wb[:, :, :], rw, tmp[:, :, :], ALU.mult))
                then(dve.tensor_tensor(wf[:, :, :], rw, wb[:, :, :], ALU.subtract))
                then(dve.scalar_tensor_tensor(rel[:, :, :], tmp[:, :, :], float(-HALF_REL), rel[:, :, :],
                                              ALU.mult, ALU.add))
                dve.sem_inc(ready, 1)
                for k in range(KG):
                    dve.wait_ge(turned, k + 1)
                    for i, t in enumerate((m.src_i, m.dst_l, m.w_fwd, m.w_bwd, m.run_end)):
                        ins = dve.tensor_copy(t[:, k * GE:(k + 1) * GE].rearrange("p (g j) -> p j g", j=GROUP),
                                              m.ps[i][:, :].rearrange("p (j g) -> p j g", j=GROUP))
                    ins.then_inc(kept, 1)

            @block.tensor
            def _(pe):
                pe.wait_ge(ready, 1)
                for k in range(KG):
                    if k:
                        pe.wait_ge(kept, k)
                    for i, t in enumerate((src, dst, wf, wb, end)):
                        for j in range(GROUP):
                            ins = pe.transpose(m.ps[i][:, j * P:(j + 1) * P], t[:, k, j * P:(j + 1) * P], m.ident[:, :])
                    ins.then_inc(turned, 1)


def load_nodes(nc, m, a):
    full = N // P
    with Stage(nc, "nodes") as st:
        loaded, zeroed = st.sem("loaded"), st.sem("zeroed")
        with nc.Block() as block:
            @block.vector
            def _(dve):
                dve.memset(m.x[:, full, :], 0.0).then_inc(zeroed, 1)

            @block.sync
            def _(sp):
                sp.dma_start(m.x[:, 0:full, :], a["x"][0:full * P, :].rearrange("(b p) d -> p b d", p=P))\
                  .then_inc(loaded, 16)
                sp.wait_ge(zeroed, 1)
                sp.dma_start(m.x[0:N - full * P, full, :], a["x"][full * P:N, :]).then_inc(loaded, 16)
                sp.wait_ge(loaded, 32)


def finish(nc, m, out):
    full = N // P
    with Stage(nc, "finish") as st:
        stored = st.sem("stored")
        with nc.Block() as block:
            @block.sync
            def _(sp):
                sp.dma_start(out[0:full * P, :].rearrange("(b p) d -> p b d", p=P), m.x[:, 0:full, :])\
                  .then_inc(stored, 16)
                sp.dma_start(out[full * P:N, :], m.x[0:N - full * P, full, :]).then_inc(stored, 16)
                sp.wait_ge(stored, 32)


class Step:

    def __init__(self, turn, ahead, q):
        self.turn, self.ahead, self.q = turn, ahead, q

    def count(self, per, plus):
        plus = plus + per * self.ahead
        if self.turn is None:
            return plus
        scaled = self.turn if per == 1 else self.turn * per
        return scaled + plus if plus else scaled

    def items(self):
        return ds(self.count(2 * BATCH, self.q * BATCH), BATCH)

    def group(self, g=0, size=1):
        return ds(self.count(2 * PAIR, self.q * PAIR + g), size)


def pipeline(eng, *parts):
    last = max(lag for lag, _ in parts)
    head = last + last % 2

    def at(times):
        for t in times:
            for lag, part in parts:
                if 0 <= t - lag < STEPS:
                    part(Step(None, (t - lag) // 2, (t - lag) % 2))

    at(range(head))
    with eng.Fori(head // 2, STEPS // 2) as turn:
        for r in range(2):
            for lag, part in parts:
                part(Step(turn, (r - lag) // 2, (r - lag) % 2))
    at(range(STEPS, STEPS + last))


class Gather:

    def __init__(self, nc, m, st, table, width):
        self.m, self.table = m, table
        self.rows = st.pair_sb("rows", [P, BATCH, width])
        self.index = st.pair_sb("index", [P, BATCH], I32)
        self.index_set = st.pair("index_set")
        self.gathered = st.pair("gathered")
        self.passed = st.sem("passed")

    def program(self, pool, rows_used, per=1):
        def indices(n):
            pool.wait_ge(rows_used[n.q], n.count(per, per))
            pool.tensor_copy(self.index[n.q][:, :], self.m.src_i[:, n.items()]).then_inc(self.index_set[n.q], 1)

        def gather(n, items):
            for j in items:
                pool.indirect_dma_start(self.rows[n.q][:, j, :], None, self.table,
                                        bass.IndirectOffsetOnAxis(ap=self.index[n.q][:, j:j + 1], axis=0))\
                    .then_inc(self.gathered[n.q], 16)

        def most(n):
            pool.wait_ge(self.index_set[n.q], n.count(1, 1))
            pool.sem_inc(self.passed, 1)
            gather(n, range(BATCH - 2))

        def rest(n):
            gather(n, range(BATCH - 2, BATCH))

        pipeline(pool, (1, most), (0, indices), (1, rest))

    def wait(self, eng, n):
        eng.wait_ge(self.gathered[n.q], n.count(16 * BATCH, 16 * BATCH))


def make_hot(dve, m, n, hot, summed, hot_made):
    dve.wait_ge(summed[n.q], n.count(1, 1))
    dve.tensor_tensor(hot[n.q][:, :, :], repeat(m.iota_row[:, :], BATCH), spread(m.dst_l[:, n.items()], P), ALU.is_equal)\
        .then_inc(hot_made[n.q], 1)


def make_dst_hot(act, m, n, dst, minus_row, dst_loaded, dst_rows, dst_far, dst_hot, dhot):
    q = n.q
    act.wait_ge(dst_loaded[q], n.count(16, 16))
    act.wait_ge(dst_rows[q], n.count(1, 1))
    act.activation(dhot[q][:, :], dst[q][:, :], ACT.Abs, bias=minus_row[:, 0:1]).then_inc(dst_far[q], 1)
    act.wait_ge(dst_far[q], n.count(1, 2))
    act.activation(dhot[q][:, :], dhot[q][:, :], ACT.Relu, scale=-1.0, bias=m.ones[:, 0:1]).then_inc(dst_hot[q], 1)


def load_dst(sp, m, n, dst, dst_far, dst_loaded):
    sp.wait_ge(dst_far[n.q], n.count(1, 1))
    sp.dma_start(dst[n.q][:, :], m.dst_rows[n.group(size=PAIR), :].rearrange("g e -> (g e)").partition_broadcast(P))\
      .then_inc(dst_loaded[n.q], 16)


def sum_groups(pe, hot, msg, banks, width, summed):
    for g in range(PAIR):
        for j in range(GROUP):
            ins = pe.matmul(place(banks, g, width), hot[:, g * GROUP + j, :], msg[:, g * GROUP + j, 0:width],
                            start=j == 0, stop=j == GROUP - 1)
    ins.then_inc(summed, 1)


def add_groups(dve, m, n, banks, width, added, acc, op=ALU.add):
    for g in range(PAIR):
        b = dve.value_load(m.block_tab[0:1, n.group(g)], min_val=0, max_val=NB - 1)
        dve.wait_ge(added, n.count(2 * PAIR, n.q * PAIR + g + 1 + PAIR))
        dst = acc[:, ds(b, 1), 0:width]
        dve.tensor_tensor(dst, dst, place(banks, g, width).unsqueeze(1), op).then_inc(added, 1)


def wait_added(eng, n, added):
    eng.wait_ge(added, n.count(2 * PAIR, n.q * PAIR + 1))


def place(banks, g, width):
    if not isinstance(banks, list):
        return banks[:, g * width:(g + 1) * width]
    return banks[g][:, 0:width]


def compgcn_pass(nc, m, a, layer, table):
    with Stage(nc, f"gcn{layer}") as st:
        g = Gather(nc, m, st, table, DIM)
        rel_loaded, ids_loaded = st.sem("rel_loaded"), st.pair("ids_loaded")
        rel_hot, rel_rows = st.pair("rel_hot"), st.pair("rel_rows")
        comp_made, hot_made, msg_made = st.pair("comp"), st.pair("edge_hot"), st.pair("msg")
        summed, added = st.pair("summed"), st.sem("added")
        rel = st.sb("rel", [HALF_REL, DIM])
        ids = st.pair_sb("ids", [HALF_REL, BATCH * P])
        rhot = st.pair_sb("rhot", [HALF_REL, BATCH * P])
        comp = st.pair_sb("comp_s", [P, BATCH, DIM])
        hot = st.pair_sb("hot", [P, BATCH, P])
        msg = st.pair_sb("msg_s", [P, BATCH, 2 * DIM])
        rel_ps, sum_ps = m.ps[0:2], m.ps[2:4]
        with nc.Block() as block:
            @block.gpsimd
            def _(pool):
                g.program(pool, comp_made)

            @block.sync
            def _(sp):
                def load_ids(n):
                    sp.wait_ge(rel_hot[n.q], n.count(1, 1))
                    sp.dma_start(ids[n.q][:, :], m.rel_rows[n.group(size=PAIR), :].rearrange("g e -> (g e)")
                                 .partition_broadcast(HALF_REL)).then_inc(ids_loaded[n.q], 16)

                sp.dma_start(rel[:, :], a["L0_gnn_rel_emb"][layer, 0:HALF_REL, :]).then_inc(rel_loaded, 16)
                pipeline(sp, (0, load_ids))

            @block.vector
            def _(dve):
                def relation_hot(n):
                    q = n.q
                    dve.wait_ge(ids_loaded[q], n.count(16, 16))
                    dve.wait_ge(rel_rows[q], n.count(1, 1))
                    dve.tensor_scalar(rhot[q][:, :], ids[q][:, :], m.iota_col[0:HALF_REL, 0:1], None, ALU.is_equal)\
                        .then_inc(rel_hot[q], 1)

                def messages(n):
                    q = n.q
                    make_hot(dve, m, n, hot, summed, hot_made)
                    dve.wait_ge(rel_rows[q], n.count(1, 2))
                    g.wait(dve, n)
                    dve.tensor_tensor(comp[q][:, :, :], g.rows[q][:, :, :],
                                      rel_ps[q][:, :].rearrange("p (b d) -> p b d", b=BATCH), ALU.mult)\
                        .then_inc(comp_made[q], 1)
                    dve.wait_ge(comp_made[q], n.count(1, 2))
                    for half, w in ((0, m.w_fwd), (1, m.w_bwd)):
                        dve.tensor_tensor(msg[q][:, :, half * DIM:(half + 1) * DIM], comp[q][:, :, :],
                                          spread(w[:, n.items()], DIM), ALU.mult).then_inc(msg_made[q], 1)

                def adds(n):
                    dve.wait_ge(summed[n.q], n.count(1, 2))
                    add_groups(dve, m, n, sum_ps[n.q], 2 * DIM, added, m.acc)

                dve.memset(m.acc[:, :, :], 0.0).then_inc(added, 1)
                dve.sem_inc(added, PAIR)
                for q in range(2):
                    dve.sem_inc(rel_hot[q], 1)
                    dve.sem_inc(comp_made[q], 1)
                pipeline(dve, (0, relation_hot), (1, messages), (3, adds))

            @block.tensor
            def _(pe):
                def relation_rows(n):
                    q = n.q
                    pe.wait_ge(rel_hot[q], n.count(1, 2))
                    pe.wait_ge(comp_made[q], n.count(1, 1))
                    for j in range(BATCH):
                        ins = pe.matmul(rel_ps[q][:, j * DIM:(j + 1) * DIM], rhot[q][:, j * P:(j + 1) * P], rel[:, :],
                                        start=True, stop=True)
                    ins.then_inc(rel_rows[q], 1)

                def sums(n):
                    q = n.q
                    pe.wait_ge(hot_made[q], n.count(1, 1))
                    pe.wait_ge(msg_made[q], n.count(2, 2))
                    wait_added(pe, n, added)
                    sum_groups(pe, hot[q], msg[q], sum_ps[q], 2 * DIM, summed[q])

                for q in range(2):
                    pe.sem_inc(rel_rows[q], 1)
                    pe.sem_inc(summed[q], 1)
                pe.wait_ge(rel_loaded, 16)
                pipeline(pe, (0, relation_rows), (2, sums))


def write_table(sp, table, tile, width, stored, per, written):
    with sp.Fori(0, NB) as b:
        sp.wait_ge(stored, (b if per == 1 else b * per) + 2)
        sp.dma_start(table[ds(b * P, P), :].unsqueeze(1), tile[:, ds(b, 1), 0:width]).then_inc(written, 16)
    sp.wait_ge(written, 16 * NB)


def compgcn_nodes(nc, m, a, layer, x, y):
    with Stage(nc, f"gcn_nodes{layer}") as st:
        loaded, staged, turned = st.sem("loaded"), st.sem("staged"), st.sem("turned")
        evacuated, product, stored, written = st.sem("evacuated"), st.sem("product"), st.sem("stored"), st.sem("written")
        w_agg, w_loop = st.sb("w_agg", [P, DIM]), st.sb("w_loop", [DIM, DIM])
        first = st.sb("first", [P, 1])
        flat, tall, tall_x = st.sb("flat", [P, 3 * DIM]), st.sb("tall", [P, P]), st.sb("tall_x", [DIM, P])
        agg_t, x_t, res = m.ps[0], m.ps[1], m.ps[2]
        with nc.Block() as block:
            @block.sync
            def _(sp):
                sp.dma_start(w_agg[0:DIM, :], a["L0_gnn_w_fwd"][layer]).then_inc(loaded, 16)
                sp.dma_start(w_agg[DIM:P, :], a["L0_gnn_w_bwd"][layer]).then_inc(loaded, 16)
                sp.dma_start(w_loop[:, :], a["L0_gnn_w_loop"][layer]).then_inc(loaded, 16)
                if layer == 0:
                    write_table(sp, m.x_table, y, DIM, stored, 1, written)

            @block.vector
            def _(dve):
                with dve.Fori(0, NB) as b:
                    dve.wait_ge(turned, b + 1)
                    dve.tensor_copy(flat[:, 0:P].unsqueeze(1), m.acc[:, ds(b, 1), 0:P]).then_inc(staged, 1)
                    dve.tensor_copy(flat[:, P:3 * DIM].unsqueeze(1), x[:, ds(b, 1), :]).then_inc(staged, 1)

            @block.tensor
            def _(pe):
                pe.sem_inc(turned, 1)
                pe.sem_inc(product, 1)
                pe.wait_ge(loaded, 48)
                with pe.Fori(0, NB) as b:
                    pe.wait_ge(staged, b * 2 + 2)
                    pe.wait_ge(evacuated, b * 2 + 1)
                    pe.transpose(agg_t[:, 0:P], flat[:, 0:P], m.ident[:, :])
                    pe.transpose(x_t[0:DIM, 0:P], flat[:, P:3 * DIM], m.ident[:, :]).then_inc(turned, 1)
                    pe.wait_ge(evacuated, b * 2 + 3)
                    pe.wait_ge(stored, b + 1)
                    pe.matmul(res[:, 0:DIM], tall[:, :], w_agg[:, :], start=True, stop=False)
                    pe.matmul(res[:, 0:DIM], tall_x[:, :], w_loop[:, :], start=False, stop=True).then_inc(product, 1)

            @block.scalar
            def _(act):
                act.sem_inc(evacuated, 1)
                act.sem_inc(stored, 1)
                act.activation(first[:, :], m.ones[:, 0:1], ACT.Relu)
                with act.Fori(0, NB) as b:
                    act.wait_ge(turned, b + 2)
                    act.wait_ge(product, b + 1)
                    act.activation(tall[:, :], agg_t[:, 0:P], ACT.Copy).then_inc(evacuated, 1)
                    act.activation(tall_x[:, :], x_t[0:DIM, 0:P], ACT.Copy).then_inc(evacuated, 1)
                    act.wait_ge(product, b + 2)
                    act.activation(y[:, ds(b, 1), :], res[:, 0:DIM].unsqueeze(1), ACT.Relu).then_inc(stored, 1)


def residual_norm(nc, m, y):
    with Stage(nc, f"norm{m.norms}") as st:
        m.norms += 1
        step, rooted = st.sem("step"), st.sem("rooted")
        sq = st.sb("sq", [P, NB, DIM])
        mean, var = st.sb("mean", [P, NB]), st.sb("var", [P, NB])
        x = m.x[:, :, :]
        with nc.Block() as block:
            @block.vector
            def _(dve):
                n = [0]

                def then(ins):
                    n[0] += 1
                    ins.then_inc(step, 1)
                    dve.wait_ge(step, n[0])

                then(dve.tensor_tensor(x, x, y[:, :, :], ALU.add))
                then(dve.tensor_reduce(mean[:, :], x, AX.X, ALU.add))
                then(dve.tensor_single_scalar(mean[:, :], mean[:, :], 1.0 / DIM, ALU.mult))
                then(dve.tensor_tensor(x, x, spread(mean[:, :], DIM), ALU.subtract))
                then(dve.tensor_tensor(sq[:, :, :], x, x, ALU.mult))
                then(dve.tensor_reduce(var[:, :], sq[:, :, :], AX.X, ALU.add))
                then(dve.tensor_scalar(var[:, :], var[:, :], 1.0 / DIM, 1e-5, ALU.mult, ALU.add))
                dve.wait_ge(rooted, 1)
                then(dve.reciprocal(var[:, :], var[:, :]))
                dve.tensor_tensor(x, x, spread(var[:, :], DIM), ALU.mult)

            @block.scalar
            def _(act):
                act.wait_ge(step, 7)
                act.activation(var[:, :], var[:, :], ACT.Sqrt).then_inc(rooted, 1)


def message_tables(nc, m, a):
    with Stage(nc, "msg_tab") as st:
        loaded, staged, turned = st.sem("loaded"), st.sem("staged"), st.sem("turned")
        evacuated, product, stored, written = st.sem("evacuated"), st.sem("product"), st.sem("stored"), st.sem("written")
        w, bias = st.sb("w", [DIM, 2 * DIM]), st.sb("bias", [P, 2 * DIM])
        flat, tall = st.sb("flat", [P, P]), st.sb("tall", [DIM, P])
        pre = st.sb("pre", [P, NB, 2 * DIM])
        x_t, res = m.ps[0], m.ps[1]
        with nc.Block() as block:
            @block.sync
            def _(sp):
                for l in range(2):
                    half = slice(l * DIM, (l + 1) * DIM)
                    sp.dma_start(w[:, half], a["L1_gnn_msg_w1"][l, 0:DIM, :]).then_inc(loaded, 16)
                    sp.dma_start(bias[:, half], a["L1_gnn_msg_b1"][l].partition_broadcast(P)).then_inc(loaded, 16)
                write_table(sp, m.pre_table, pre, 2 * DIM, stored, 1, written)

            @block.vector
            def _(dve):
                dve.memset(flat[:, :], 0.0).then_inc(stored, 1)
                dve.wait_ge(stored, 1)
                dve.wait_ge(loaded, 64)
                with dve.Fori(0, NB) as b:
                    dve.wait_ge(turned, b + 1)
                    dve.tensor_copy(flat[:, 0:DIM].unsqueeze(1), m.x[:, ds(b, 1), :]).then_inc(staged, 1)
                    dve.wait_ge(product, b + 2)
                    dve.tensor_tensor(pre[:, ds(b, 1), :], res[:, 0:2 * DIM].unsqueeze(1), bias[:, :].unsqueeze(1),
                                      ALU.add).then_inc(stored, 1)

            @block.tensor
            def _(pe):
                pe.sem_inc(turned, 1)
                pe.sem_inc(product, 1)
                pe.wait_ge(loaded, 64)
                with pe.Fori(0, NB) as b:
                    pe.wait_ge(staged, b + 1)
                    pe.wait_ge(evacuated, b + 1)
                    pe.transpose(x_t[:, 0:P], flat[:, :], m.ident[:, :]).then_inc(turned, 1)
                    pe.wait_ge(evacuated, b + 2)
                    pe.wait_ge(stored, b + 1)
                    pe.matmul(res[:, 0:2 * DIM], tall[:, :], w[:, :], start=True, stop=True).then_inc(product, 1)

            @block.scalar
            def _(act):
                act.sem_inc(evacuated, 1)
                with act.Fori(0, NB) as b:
                    act.wait_ge(turned, b + 2)
                    act.wait_ge(product, b + 1)
                    act.activation(tall[:, :], x_t[0:DIM, 0:P], ACT.Copy).then_inc(evacuated, 1)


def load_attr(sp, m, n, attr, tile, turned, loaded):
    sp.wait_ge(turned[n.q], n.count(1, 1))
    for g in range(PAIR):
        e = sp.value_load(m.first_tab[0:1, n.group(g)], min_val=0, max_val=E - GE)
        sp.dma_start(tile[n.q][:, g * GROUP:(g + 1) * GROUP, :], attr[ds(e, GE), :].rearrange("(j p) d -> p j d", p=P))\
          .then_inc(loaded[n.q], 16)


def message_pass(nc, m, a):
    HID, ED = 2 * DIM, 32
    with Stage(nc, "msg") as st:
        g = Gather(nc, m, st, m.pre_table, HID)
        w_zeroed, w_loaded, attr_loaded = st.sem("w_zeroed"), st.sem("w_loaded"), st.pair("attr_loaded")
        turned, evacuated, edge_part = st.pair("turned"), st.pair("evacuated"), st.pair("edge_part")
        pre_made, msg_made, hot_made = st.pair("pre"), st.pair("msg"), st.pair("edge_hot")
        summed, added = st.pair("summed"), st.sem("added")
        w = st.sb("w", [P, GROUP * HID])
        attr = st.pair_sb("attr", [P, BATCH, ED])
        attr_t = st.pair_sb("attr_t", [P, PAIR * P])
        pre = st.pair_sb("pre_s", [P, BATCH, HID])
        msg = st.pair_sb("msg_s", [P, BATCH, HID + 1])
        hot = st.pair_sb("hot", [P, BATCH, P])
        turn_ps, edge_ps, sum_ps = m.ps[0:2], [m.ps[2:4], m.ps[4:6]], m.ps[6:8]
        with nc.Block() as block:
            @block.gpsimd
            def _(pool):
                g.program(pool, pre_made, per=PAIR)

            @block.sync
            def _(sp):
                sp.wait_ge(w_zeroed, 1)
                for l in range(2):
                    for j in range(GROUP):
                        col = j * HID + l * DIM
                        sp.dma_start(w[j * ED:(j + 1) * ED, col:col + DIM], a["L1_gnn_msg_w1"][l, DIM:DIM + ED, :])\
                          .then_inc(w_loaded, 16)
                pipeline(sp, (0, lambda n: load_attr(sp, m, n, a["edge_attr_32"], attr, turned, attr_loaded)))

            @block.scalar
            def _(act):
                def keep(n):
                    q = n.q
                    act.wait_ge(turned[q], n.count(1, 2))
                    act.wait_ge(edge_part[q], n.count(1, 1))
                    act.activation(attr_t[q][:, :], turn_ps[q][:, 0:PAIR * P], ACT.Copy).then_inc(evacuated[q], 1)

                def rectify(n):
                    q = n.q
                    act.wait_ge(pre_made[q], n.count(PAIR, 2 * PAIR))
                    act.wait_ge(summed[q], n.count(1, 1))
                    act.activation(msg[q][:, :, 0:HID], pre[q][:, :, :], ACT.Relu).then_inc(msg_made[q], 1)

                for q in range(2):
                    act.sem_inc(evacuated[q], 1)
                pipeline(act, (0, keep), (1, rectify))

            @block.vector
            def _(dve):
                def preactivations(n):
                    q = n.q
                    make_hot(dve, m, n, hot, summed, hot_made)
                    dve.wait_ge(edge_part[q], n.count(1, 2))
                    dve.wait_ge(msg_made[q], n.count(1, 1))
                    g.wait(dve, n)
                    for i in range(PAIR):
                        part = slice(i * GROUP, (i + 1) * GROUP)
                        dve.tensor_tensor(pre[q][:, part, :], g.rows[q][:, part, :],
                                          edge_ps[q][i][:, :].rearrange("p (j d) -> p j d", j=GROUP), ALU.add)\
                            .then_inc(pre_made[q], 1)

                def adds(n):
                    dve.wait_ge(summed[n.q], n.count(1, 2))
                    add_groups(dve, m, n, sum_ps[n.q], HID + 1, added, m.acc)

                dve.memset(w[:, :], 0.0).then_inc(w_zeroed, 1)
                dve.memset(m.acc[:, :, :], 0.0).then_inc(added, 1)
                dve.sem_inc(added, PAIR)
                for q in range(2):
                    dve.memset(msg[q][:, :, HID:HID + 1], 1.0).then_inc(msg_made[q], 1)
                    dve.sem_inc(pre_made[q], PAIR)
                pipeline(dve, (1, preactivations), (3, adds))

            @block.tensor
            def _(pe):
                def turn(n):
                    q = n.q
                    pe.wait_ge(attr_loaded[q], n.count(16 * PAIR, 16 * PAIR))
                    pe.wait_ge(evacuated[q], n.count(1, 1))
                    for i in range(PAIR):
                        ins = pe.transpose(turn_ps[q][:, i * P:(i + 1) * P],
                                           attr[q][:, i * GROUP:(i + 1) * GROUP, :].rearrange("p j d -> p (j d)"), m.ident[:, :])
                    ins.then_inc(turned[q], 1)

                def edge_products(n):
                    q = n.q
                    pe.wait_ge(evacuated[q], n.count(1, 2))
                    pe.wait_ge(pre_made[q], n.count(PAIR, PAIR))
                    for i in range(PAIR):
                        ins = pe.matmul(edge_ps[q][i][:, :], attr_t[q][:, i * P:(i + 1) * P], w[:, :], start=True, stop=True)
                    ins.then_inc(edge_part[q], 1)

                def sums(n):
                    q = n.q
                    pe.wait_ge(hot_made[q], n.count(1, 1))
                    pe.wait_ge(msg_made[q], n.count(1, 2))
                    wait_added(pe, n, added)
                    sum_groups(pe, hot[q], msg[q], sum_ps[q], HID + 1, summed[q])

                for q in range(2):
                    pe.sem_inc(turned[q], 1)
                    pe.sem_inc(edge_part[q], 1)
                    pe.sem_inc(summed[q], 1)
                pe.wait_ge(w_loaded, 2 * GROUP * 16)
                pipeline(pe, (0, turn), (2, sums), (0, edge_products))


def message_nodes(nc, m, a):
    with Stage(nc, "msg_nodes") as st:
        loaded, biased, rated = st.sem("loaded"), st.sem("biased"), st.sem("rated")
        staged, turned, evac, agged = st.sem("staged"), st.sem("turned"), st.sem("evacuated"), st.sem("agg")
        divided, joined, joined_t = st.sem("divided"), st.sem("joined"), st.sem("joined_t")
        hidden_ps, hidden, updated, stored = st.sem("hidden_ps"), st.sem("hidden"), st.sem("updated"), st.sem("stored")
        w2, w_u1, w_u2 = st.sb("w2", [P, DIM]), st.sb("w_u1", [P, DIM]), st.sb("w_u2", [DIM, DIM])
        b2, b2b, b_u1, b_u2 = st.sb("b2", [P, DIM]), st.sb("b2b", [P, DIM]), st.sb("b_u1", [DIM, 1]), st.sb("b_u2", [P, DIM])
        rate, bias_sum = st.sb("rate", [P, NB]), st.sb("bias_sum", [P, NB, DIM])
        y = st.sb("y", [P, NB, DIM])
        flat, tall, agg_s = st.sb("flat", [P, ROUND, P]), st.sb("tall", [P, ROUND * P]), st.sb("agg_s", [P, ROUND, DIM])
        both, both_t, hid = st.sb("both", [P, ROUND, P]), st.sb("both_t", [P, ROUND * P]), st.sb("hid", [DIM, ROUND * P])
        t_ps, agg_ps, bt_ps, h_ps, u_ps = m.ps[0:2], m.ps[2], m.ps[3:5], m.ps[5:7], m.ps[7]
        deg = m.acc[:, :, 2 * DIM:2 * DIM + 1].rearrange("p b o -> p (b o)")
        spans = [(0, CHUNK), (CHUNK, ROUND * P - CHUNK)]
        by_block = lambda bank: bank[:, 0:ROUND * DIM].rearrange("p (i d) -> p i d", d=DIM)
        with nc.Block() as block:
            @block.sync
            def _(sp):
                sp.dma_start(w2[:, :], a["L1_gnn_msg_w2"].rearrange("l i o -> (l i) o")).then_inc(loaded, 16)
                sp.dma_start(b2[:, :], a["L1_gnn_msg_b2"][0].partition_broadcast(P)).then_inc(loaded, 16)
                sp.dma_start(b2b[:, :], a["L1_gnn_msg_b2"][1].partition_broadcast(P)).then_inc(loaded, 16)
                sp.dma_start(w_u1[:, :], a["L1_gnn_upd_w1"]).then_inc(loaded, 16)
                sp.dma_start(w_u2[:, :], a["L1_gnn_upd_w2"]).then_inc(loaded, 16)
                sp.dma_start(b_u1[:, :], a["L1_gnn_upd_b1"].unsqueeze(1)).then_inc(loaded, 16)
                sp.dma_start(b_u2[:, :], a["L1_gnn_upd_b2"].partition_broadcast(P)).then_inc(loaded, 16)

            @block.vector
            def _(dve):
                dve.wait_ge(loaded, 16 * 7)
                dve.tensor_tensor(b2[:, :], b2[:, :], b2b[:, :], ALU.add).then_inc(biased, 1)
                dve.tensor_single_scalar(rate[:, :], deg, 1e-8, ALU.add).then_inc(rated, 1)
                dve.wait_ge(rated, 1)
                dve.reciprocal(rate[:, :], rate[:, :]).then_inc(rated, 1)
                dve.wait_ge(biased, 1)
                dve.tensor_tensor(bias_sum[:, :, :], spread(deg, DIM), repeat(b2[:, :], NB), ALU.mult).then_inc(biased, 1)
                dve.wait_ge(biased, 2)
                dve.wait_ge(rated, 2)
                with dve.Fori(0, NB // ROUND) as r:
                    blocks = ds(r * ROUND, ROUND)
                    dve.wait_ge(turned, r + 1)
                    dve.tensor_copy(flat[:, :, :], m.acc[:, blocks, 0:P]).then_inc(staged, 1)
                    dve.wait_ge(joined_t, r + 1)
                    dve.tensor_copy(both[:, :, 0:DIM], m.x[:, blocks, :]).then_inc(joined, 1)
                    dve.wait_ge(agged, r + 1)
                    dve.tensor_tensor(agg_s[:, :, :], bias_sum[:, blocks, :], by_block(agg_ps), ALU.add).then_inc(divided, 1)
                    dve.wait_ge(divided, r + 1)
                    dve.tensor_tensor(both[:, :, DIM:P], agg_s[:, :, :], spread(rate[:, blocks], DIM), ALU.mult).then_inc(joined, 1)
                    dve.wait_ge(updated, r + 1)
                    dve.tensor_tensor(y[:, blocks, :], by_block(u_ps), repeat(b_u2[:, :], ROUND), ALU.add).then_inc(stored, 1)

            @block.tensor
            def _(pe):
                def turn(banks, tile):
                    for i in range(ROUND):
                        at = (i * P) % CHUNK
                        ins = pe.transpose(banks[i * P // CHUNK][:, at:at + P], tile[:, i, :], m.ident[:, :])
                    return ins

                pe.sem_inc(turned, 1)
                pe.sem_inc(joined_t, 1)
                pe.wait_ge(loaded, 16 * 7)
                with pe.Fori(0, NB // ROUND) as r:
                    pe.wait_ge(staged, r + 1)
                    turn(t_ps, flat).then_inc(turned, 1)
                    pe.wait_ge(evac, r * 2 + 1)
                    for i in range(ROUND):
                        ins = pe.matmul(agg_ps[:, i * DIM:(i + 1) * DIM], tall[:, i * P:(i + 1) * P], w2[:, :], start=True, stop=True)
                    ins.then_inc(agged, 1)
                    pe.wait_ge(joined, r * 2 + 2)
                    turn(bt_ps, both).then_inc(joined_t, 1)
                    pe.wait_ge(evac, r * 2 + 2)
                    for bank, (at, size) in zip(h_ps, spans):
                        ins = pe.matmul(bank[0:DIM, 0:size], w_u1[:, :], both_t[:, at:at + size], start=True, stop=True)
                    ins.then_inc(hidden_ps, 1)
                    pe.wait_ge(hidden, r + 1)
                    pe.wait_ge(stored, r + 1)
                    for i in range(ROUND):
                        ins = pe.matmul(u_ps[:, i * DIM:(i + 1) * DIM], hid[:, i * P:(i + 1) * P], w_u2[:, :], start=True, stop=True)
                    ins.then_inc(updated, 1)

            @block.scalar
            def _(act):
                act.sem_inc(stored, 1)
                with act.Fori(0, NB // ROUND) as r:
                    act.wait_ge(turned, r + 2)
                    for bank, (at, size) in zip(t_ps, spans):
                        ins = act.activation(tall[:, at:at + size], bank[:, 0:size], ACT.Copy)
                    ins.then_inc(evac, 1)
                    act.wait_ge(joined_t, r + 2)
                    for bank, (at, size) in zip(bt_ps, spans):
                        ins = act.activation(both_t[:, at:at + size], bank[:, 0:size], ACT.Copy)
                    ins.then_inc(evac, 1)
                    act.wait_ge(hidden_ps, r + 1)
                    for bank, (at, size) in zip(h_ps, spans):
                        ins = act.activation(hid[:, at:at + size], bank[0:DIM, 0:size], ACT.Relu, bias=b_u1[:, 0:1])
                    ins.then_inc(hidden, 1)
        residual_norm(nc, m, y)


MAGIC = 12582912.0
TURN = 2.0 * np.pi
TURN_HI = float(np.float32(6.28125))
TURN_MID = float(np.float32(TURN - 6.28125))
TURN_LO = float(np.float32(TURN - 6.28125 - float(np.float32(TURN - 6.28125))))


def diffusion_embed(nc, m, a, cur):
    with Stage(nc, "embed") as st:
        loaded, padded, step, sined = st.sem("loaded"), st.sem("padded"), st.sem("step"), st.sem("sined")
        staged, turned, evac = st.sem("staged"), st.sem("turned"), st.sem("evacuated")
        hidden_ps, hidden, product, stored = st.sem("hidden_ps"), st.sem("hidden"), st.sem("product"), st.sem("stored")
        w_in, w1, w2 = st.sb("w_in", [DIM, P]), st.sb("w1", [P, P]), st.sb("w2", [P, P])
        b_in, b1, b2 = st.sb("b_in", [P, 1]), st.sb("b1", [P, 1]), st.sb("b2", [P, 1])
        freq = st.sb("freq", [P, 2])
        ang, rnd = st.sb("ang", [P, NP]), st.sb("rnd", [P, NP])
        flat, tall, emb = st.sb("flat", [P, P]), st.sb("tall", [DIM, P]), st.sb("emb", [P, P])
        hid = st.sb("hid", [P, P])
        t_ps, h_ps, o_ps = m.ps[0:3]
        with nc.Block() as block:
            @block.sync
            def _(sp):
                sp.wait_ge(padded, 1)
                sp.dma_start(ang[:, 0:N], a["node_vec"].partition_broadcast(P)).then_inc(loaded, 16)
                sp.dma_start(freq[:, :], a["freq"]).then_inc(loaded, 16)
                for tile, name in ((w_in, "init_w"), (w1, "te_w1"), (w2, "te_w2")):
                    sp.dma_start(tile[:, :], a["L2_gnn_" + name]).then_inc(loaded, 16)
                for tile, name in ((b_in, "init_b"), (b1, "te_b1"), (b2, "te_b2")):
                    sp.dma_start(tile[:, :], a["L2_gnn_" + name].unsqueeze(1)).then_inc(loaded, 16)

            @block.vector
            def _(dve):
                n = [0]

                def then(ins):
                    n[0] += 1
                    ins.then_inc(step, 1)
                    dve.wait_ge(step, n[0])

                dve.memset(ang[:, :], 0.0).then_inc(padded, 1)
                dve.memset(flat[:, :], 0.0).then_inc(padded, 1)
                dve.wait_ge(loaded, 16 * 8)
                dve.wait_ge(padded, 2)
                then(dve.tensor_tensor(b_in[:, :], b_in[:, :], b2[:, :], ALU.add))
                then(dve.tensor_single_scalar(ang[:, :], ang[:, :], freq[:, 0:1], ALU.mult))
                then(dve.tensor_scalar(rnd[:, :], ang[:, :], freq[:, 1:2], None, ALU.add))
                then(dve.tensor_scalar(rnd[:, :], rnd[:, :], 1.0 / TURN, MAGIC, ALU.mult, ALU.add))
                then(dve.tensor_single_scalar(rnd[:, :], rnd[:, :], -MAGIC, ALU.add))
                for part in (TURN_HI, TURN_MID, TURN_LO):
                    then(dve.scalar_tensor_tensor(ang[:, :], rnd[:, :], -part, ang[:, :], ALU.mult, ALU.add))
                then(dve.tensor_scalar(ang[:, :], ang[:, :], freq[:, 1:2], None, ALU.add))
                then(dve.tensor_scalar(ang[:, :], ang[:, :], 3.1415925, -3.1415925, ALU.min, ALU.max))
                dve.wait_ge(sined, 1)
                dve.sem_inc(stored, 1)
                with dve.Fori(0, NB) as b:
                    dve.wait_ge(product, b + 1)
                    dve.tensor_copy(flat[:, 0:DIM].unsqueeze(1), m.x[:, ds(b, 1), :]).then_inc(staged, 1)
                    dve.tensor_copy(emb[:, :], rnd[:, ds(b * P, P)]).then_inc(staged, 1)
                    dve.wait_ge(turned, b + 1)
                    dve.tensor_copy(tall[:, :], t_ps[0:DIM, 0:P]).then_inc(evac, 1)
                    dve.wait_ge(product, b + 2)
                    dve.tensor_scalar(cur[:, 0, ds(b * P, P)], o_ps[:, 0:P], b_in[:, 0:1], None, ALU.add).then_inc(stored, 1)

            @block.scalar
            def _(act):
                act.wait_ge(step, 10)
                act.activation(rnd[:, :], ang[:, :], ACT.Sin).then_inc(sined, 1)
                with act.Fori(0, NB) as b:
                    act.wait_ge(hidden_ps, b + 1)
                    act.wait_ge(product, b + 1)
                    act.activation(hid[:, :], h_ps[:, 0:P], ACT.Silu, bias=b1[:, 0:1]).then_inc(hidden, 1)

            @block.tensor
            def _(pe):
                pe.sem_inc(product, 1)
                pe.wait_ge(loaded, 16 * 8)
                with pe.Fori(0, NB) as b:
                    pe.wait_ge(staged, b * 2 + 2)
                    pe.transpose(t_ps[:, 0:P], flat[:, :], m.ident[:, :]).then_inc(turned, 1)
                    pe.matmul(h_ps[:, 0:P], w1[:, :], emb[:, :], start=True, stop=True).then_inc(hidden_ps, 1)
                    pe.wait_ge(evac, b + 1)
                    pe.wait_ge(hidden, b + 1)
                    pe.wait_ge(stored, b + 1)
                    pe.matmul(o_ps[:, 0:P], w_in[:, :], tall[:, :], start=True, stop=False)
                    pe.matmul(o_ps[:, 0:P], w2[:, :], hid[:, :], start=False, stop=True).then_inc(product, 1)


def gat_shape(layer):
    return (1, 2, 2)[layer], (256, 256, 128)[layer]


def gat_tables(nc, m, a, layer, cur):
    kt, width = gat_shape(layer)
    c, full = width // HEADS, width + 2 * HEADS
    with Stage(nc, f"gat_tab{layer}") as st:
        loaded, folded, staged = st.sem("loaded"), st.sem("folded"), st.sem("staged")
        product, stored, kept, written, step = st.sem("product"), st.sem("stored"), st.sem("kept"), st.sem("written"), st.sem("step")
        w = st.sb("w", [P, kt, full])
        att = st.sb("att", [P, 2, width])
        prod = st.sb("prod", [P, width])
        flat = st.sb("flat", [P, kt, P])
        o_ps = m.ps[0]
        table = m.xw_table if width == 256 else m.xw_table2
        with nc.Block() as block:
            @block.sync
            def _(sp):
                sp.dma_start(w[:, :, 0:width], a[f"L2_gnn_gat_w{layer}"].rearrange("(k p) o -> p k o", p=P)).then_inc(loaded, 16)
                for i, name in enumerate(("src", "dst")):
                    sp.dma_start(att[:, i, :], a[f"L2_gnn_att_{name}{layer}"].rearrange("h c -> (h c)").partition_broadcast(P))\
                      .then_inc(loaded, 16)
                write_table(sp, table, m.node_out, width + HEADS, stored, 1, written)
                sp.dma_start(m.al_table.rearrange("(b p) d -> p b d", p=P), m.node_out[:, :, width:width + HEADS])\
                  .then_inc(written, 16)
                sp.wait_ge(written, 16 * (NB + 1))

            @block.vector
            def _(dve):
                n = [0]

                def then(ins):
                    n[0] += 1
                    ins.then_inc(step, 1)
                    dve.wait_ge(step, n[0])

                dve.wait_ge(loaded, 48)
                for k in range(kt):
                    for i in range(2):
                        then(dve.tensor_tensor(prod[:, :], w[:, k, 0:width], att[:, i, :], ALU.mult))
                        then(dve.tensor_reduce(w[:, k, width + HEADS * i:width + HEADS * (i + 1)],
                                               prod[:, :].rearrange("p (h c) -> p h c", h=HEADS), AX.X, ALU.add))
                dve.sem_inc(folded, 1)
                with dve.Fori(0, NB) as b:
                    dve.wait_ge(product, b + 1)
                    dve.tensor_copy(flat[:, :, :], cur[:, 0:kt, ds(b * P, P)]).then_inc(staged, 1)
                dve.wait_ge(stored, NB + 1)
                dve.tensor_copy(m.dst_tab[:, :, 0:HEADS], m.node_out[:, :, width + HEADS:full])

            @block.scalar
            def _(act):
                act.sem_inc(stored, 1)
                with act.Fori(0, NB) as b:
                    act.wait_ge(product, b + 2)
                    act.activation(m.node_out[:, ds(b, 1), 0:full], o_ps[:, 0:full].unsqueeze(1), ACT.Copy).then_inc(stored, 1)

            @block.tensor
            def _(pe):
                pe.sem_inc(product, 1)
                pe.wait_ge(folded, 1)
                with pe.Fori(0, NB) as b:
                    pe.wait_ge(staged, b + 1)
                    pe.wait_ge(stored, b + 1)
                    for k in range(kt):
                        ins = pe.matmul(o_ps[:, 0:full], flat[:, k, :], w[:, k, :], start=k == 0, stop=k == kt - 1)
                    ins.then_inc(product, 1)


def gat_max_pass(nc, m, layer):
    with Stage(nc, f"gat_max{layer}") as st:
        g = Gather(nc, m, st, m.al_table, HEADS)
        runs_loaded, turned, scanned, turned_back = (st.pair(s) for s in ("runs_loaded", "turned", "scanned", "turned_back"))
        ends_made, hot_made, picked, penal = (st.pair(s) for s in ("ends", "edge_hot", "picked", "penalty"))
        offered, best, added, passed = st.pair("offered"), st.pair("best"), st.sem("added"), st.sem("turn_passed")
        ROWS = BATCH * HEADS
        runs = st.pair_sb("runs", [ROWS, P])
        run_max = st.pair_sb("run_max", [ROWS, P])
        ends = st.pair_sb("ends_s", [P, BATCH, HEADS + 1])
        hot = st.pair_sb("hot", [P, BATCH, P])
        pen = st.pair_sb("pen", [P, BATCH])
        cand = st.pair_sb("cand", [P, BATCH, HEADS])
        top = st.pair_sb("top", [P, PAIR * HEADS])
        turn_ps, back_ps, pick_ps = m.ps[0:2], m.ps[2:4], m.ps[4:6]
        with nc.Block() as block:
            @block.gpsimd
            def _(pool):
                g.program(pool, turned)

            @block.sync
            def _(sp):
                def load_runs(n):
                    sp.wait_ge(scanned[n.q], n.count(1, 1))
                    sp.dma_start(runs[n.q][:, :], m.run_rows[n.group(size=PAIR), :].rearrange("g (j e) -> (g j) e", e=P)
                                 .unsqueeze(1).to_broadcast([BATCH, HEADS, P])).then_inc(runs_loaded[n.q], 16)

                pipeline(sp, (0, load_runs))

            @block.vector
            def _(dve):
                def scan(n):
                    q = n.q
                    dve.wait_ge(runs_loaded[q], n.count(16, 16))
                    dve.wait_ge(turned_back[q], n.count(1, 1))
                    dve.wait_ge(turned[q], n.count(1, 2))
                    dve.tensor_tensor_scan(run_max[q][:, :], runs[q][:, :], turn_ps[q][0:ROWS, 0:P], FAR, ALU.add, ALU.max)\
                        .then_inc(scanned[q], 1)

                def run_ends(n):
                    q = n.q
                    make_hot(dve, m, n, hot, picked, hot_made)
                    last = m.run_end[:, n.items()]
                    dve.tensor_copy(ends[q][:, :, HEADS:HEADS + 1], last.unsqueeze(2)).then_inc(ends_made[q], 1)
                    dve.wait_ge(turned_back[q], n.count(1, 2))
                    dve.tensor_tensor(ends[q][:, :, 0:HEADS], back_ps[q][:, 0:ROWS].rearrange("p (b h) -> p b h", b=BATCH),
                                      spread(last, HEADS), ALU.mult).then_inc(ends_made[q], 1)

                def maxima(n):
                    q = n.q
                    view = pick_ps[q][:, 0:BATCH * (HEADS + 1)].rearrange("p (b h) -> p b h", b=BATCH)
                    dve.wait_ge(picked[q], n.count(1, 2))
                    dve.tensor_scalar(pen[q][:, :].unsqueeze(2), view[:, :, HEADS:HEADS + 1], -1.0, -FAR, ALU.add, ALU.mult)\
                        .then_inc(penal[q], 1)
                    dve.wait_ge(penal[q], n.count(1, 1))
                    dve.tensor_tensor(cand[q][:, :, :], view[:, :, 0:HEADS], spread(pen[q][:, :], HEADS), ALU.add)\
                        .then_inc(offered[q], 1)
                    dve.wait_ge(offered[q], n.count(1, 2))
                    wait_added(dve, n, added)
                    for i in range(PAIR):
                        dve.tensor_reduce(top[q][:, i * HEADS:(i + 1) * HEADS],
                                          cand[q][:, i * GROUP:(i + 1) * GROUP, :].rearrange("p j h -> p h j"), AX.X, ALU.max)\
                            .then_inc(best[q], 1)
                    dve.wait_ge(best[q], n.count(PAIR, PAIR))
                    add_groups(dve, m, n, top[q], HEADS, added, m.al_max, ALU.max)

                dve.memset(m.al_max[:, :, :], FAR).then_inc(added, 1)
                dve.sem_inc(added, PAIR)
                for q in range(2):
                    dve.sem_inc(scanned[q], 1)
                    dve.sem_inc(ends_made[q], 2)
                    dve.sem_inc(offered[q], 1)
                pipeline(dve, (0, scan), (1, run_ends), (2, maxima))

            @block.tensor
            def _(pe):
                def turn(n):
                    q = n.q
                    pe.wait_ge(scanned[q], n.count(1, 1))
                    g.wait(pe, n)
                    pe.sem_inc(passed, 1)
                    pe.transpose(turn_ps[q][0:ROWS, 0:P], g.rows[q][:, :, :].rearrange("p b h -> p (b h)"),
                                 m.ident[:, :]).then_inc(turned[q], 1)

                def turn_back(n):
                    q = n.q
                    pe.wait_ge(ends_made[q], n.count(2, 2))
                    pe.wait_ge(scanned[q], n.count(1, 2))
                    pe.matmul(back_ps[q][:, 0:ROWS], run_max[q][:, :], m.ident[0:ROWS, 0:ROWS], start=True,
                              stop=True).then_inc(turned_back[q], 1)

                def pick(n):
                    q = n.q
                    pe.wait_ge(hot_made[q], n.count(1, 1))
                    pe.wait_ge(ends_made[q], n.count(2, 4))
                    pe.wait_ge(offered[q], n.count(1, 1))
                    for j in range(BATCH):
                        ins = pe.matmul(pick_ps[q][:, j * (HEADS + 1):(j + 1) * (HEADS + 1)], hot[q][:, j, :], ends[q][:, j, :],
                                        start=True, stop=True)
                    ins.then_inc(picked[q], 1)

                for q in range(2):
                    pe.sem_inc(turned[q], 1)
                    pe.sem_inc(turned_back[q], 1)
                    pe.sem_inc(picked[q], 1)
                pipeline(pe, (0, turn), (1, turn_back), (2, pick))


def gat_self_loops(nc, m, layer):
    _, width = gat_shape(layer)
    with Stage(nc, f"gat_self{layer}") as st:
        step, powered = st.sem("step"), st.sem("powered")
        logit, low = st.sb("logit", [P, NB, HEADS]), st.sb("low", [P, NB, HEADS])
        al_s = m.node_out[:, :, width:width + HEADS]
        al_d, top = m.dst_tab[:, :, 0:HEADS], m.dst_tab[:, :, HEADS:2 * HEADS]
        own = m.acc[:, :, width:width + HEADS]
        rest = st.sb("rest", [P, NB, 2 * HEADS])
        with nc.Block() as block:
            @block.vector
            def _(dve):
                n = [0]

                def then(ins):
                    n[0] += 1
                    ins.then_inc(step, 1)
                    dve.wait_ge(step, n[0])

                then(dve.tensor_tensor(top, m.al_max[:, :, :], al_s, ALU.max))
                then(dve.tensor_tensor(top, top, al_d, ALU.add))
                then(dve.scalar_tensor_tensor(top, top, 0.2, top, ALU.mult, ALU.max))
                then(dve.tensor_tensor(logit[:, :, :], al_s, al_d, ALU.add))
                then(dve.scalar_tensor_tensor(low[:, :, :], logit[:, :, :], 0.2, logit[:, :, :], ALU.mult, ALU.max))
                then(dve.tensor_tensor(low[:, :, :], low[:, :, :], top, ALU.subtract))
                then(dve.tensor_copy(rest[:, :, :], m.dst_tab[:, :, :]))
                for k in range(PARTS):
                    part = m.dst_parts[:, :, k * 2 * HEADS:(k + 1) * 2 * HEADS]
                    then(dve.tensor_copy(part, rest[:, :, :]))
                    if k < PARTS - 1:
                        then(dve.tensor_tensor(rest[:, :, :], rest[:, :, :], part, ALU.subtract))
                dve.wait_ge(powered, 1)
                for h in range(HEADS):
                    c = width // HEADS
                    dve.tensor_tensor(m.acc[:, :, h * c:(h + 1) * c], m.node_out[:, :, h * c:(h + 1) * c],
                                      spread(m.acc[:, :, width + h:width + h + 1].rearrange("p b o -> p (b o)"), c), ALU.mult)

            @block.scalar
            def _(act):
                act.wait_ge(step, 6)
                act.activation(own, low[:, :, :], ACT.Exp).then_inc(powered, 1)


def gat_sum_pass(nc, m, layer):
    _, width = gat_shape(layer)
    c, full = width // HEADS, width + HEADS
    with Stage(nc, f"gat_sum{layer}") as st:
        g = Gather(nc, m, st, m.xw_table if width == 256 else m.xw_table2, full)
        dst_loaded, dst_far, dst_hot, dst_rows = (st.pair(s) for s in ("dst_loaded", "dst_far", "dst_hot", "dst_rows"))
        joined, logit, leaky, shifted, powered = (st.pair(s) for s in ("joined", "logit", "leaky", "shifted", "powered"))
        msg_made, hot_made, summed, added = st.pair("msg"), st.pair("edge_hot"), st.pair("summed"), st.sem("added")
        negated = st.sem("negated")
        minus_row = st.sb("minus_row", [P, 1])
        dst = st.pair_sb("dst", [P, BATCH * P])
        dhot = st.pair_sb("dhot", [P, BATCH * P], BF16)
        drow = st.pair_sb("drow", [P, BATCH, 2 * HEADS])
        hot = st.pair_sb("hot", [P, BATCH, P])
        lg = st.pair_sb("lg", [P, BATCH, HEADS])
        msg = st.pair_sb("msg_s", [P, BATCH, full])
        row_ps, sum_ps = m.ps[0:2], [m.ps[2:4], m.ps[4:6]]
        with nc.Block() as block:
            @block.gpsimd
            def _(pool):
                g.program(pool, msg_made)

            @block.sync
            def _(sp):
                pipeline(sp, (0, lambda n: load_dst(sp, m, n, dst, dst_far, dst_loaded)))

            @block.scalar
            def _(act):
                def power(n):
                    q = n.q
                    act.wait_ge(shifted[q], n.count(1, 2))
                    act.wait_ge(summed[q], n.count(1, 1))
                    act.activation(msg[q][:, :, width:full], lg[q][:, :, :], ACT.Exp).then_inc(powered[q], 1)

                for q in range(2):
                    act.sem_inc(dst_far[q], 1)
                act.wait_ge(negated, 1)
                pipeline(act, (0, lambda n: make_dst_hot(act, m, n, dst, minus_row, dst_loaded, dst_rows, dst_far, dst_hot, dhot)),
                         (1, power))

            @block.vector
            def _(dve):
                def logits(n):
                    q = n.q
                    dve.wait_ge(dst_rows[q], n.count(1, 2))
                    dve.wait_ge(shifted[q], n.count(1, 1))
                    dve.tensor_reduce(drow[q][:, :, :], row_ps[q][:, 0:BATCH * PARTS * 2 * HEADS]
                                      .rearrange("p (b k h) -> p b h k", b=BATCH, k=PARTS), AX.X, ALU.add).then_inc(joined[q], 1)
                    dve.wait_ge(joined[q], n.count(1, 2))
                    g.wait(dve, n)
                    dve.tensor_tensor(lg[q][:, :, :], g.rows[q][:, :, width:full], drow[q][:, :, 0:HEADS], ALU.add)\
                        .then_inc(logit[q], 1)
                    dve.wait_ge(logit[q], n.count(1, 1))
                    dve.scalar_tensor_tensor(lg[q][:, :, :], lg[q][:, :, :], 0.2, lg[q][:, :, :], ALU.mult, ALU.max)\
                        .then_inc(leaky[q], 1)
                    dve.wait_ge(leaky[q], n.count(1, 1))
                    dve.tensor_tensor(lg[q][:, :, :], lg[q][:, :, :], drow[q][:, :, HEADS:2 * HEADS], ALU.subtract)\
                        .then_inc(shifted[q], 1)

                def messages(n):
                    q = n.q
                    make_hot(dve, m, n, hot, summed, hot_made)
                    dve.wait_ge(powered[q], n.count(1, 1))
                    dve.tensor_tensor(msg[q][:, :, 0:width].rearrange("p b (h c) -> p b h c", c=c),
                                      g.rows[q][:, :, 0:width].rearrange("p b (h c) -> p b h c", c=c),
                                      msg[q][:, :, width:full].unsqueeze(3).to_broadcast([P, BATCH, HEADS, c]), ALU.mult)\
                        .then_inc(msg_made[q], 1)

                def adds(n):
                    dve.wait_ge(summed[n.q], n.count(1, 2))
                    add_groups(dve, m, n, sum_ps[n.q], full, added, m.acc)

                dve.tensor_single_scalar(minus_row[:, :], m.iota_col[:, :], -1.0, ALU.mult).then_inc(negated, 1)
                dve.sem_inc(added, 1 + PAIR)
                for q in range(2):
                    dve.sem_inc(msg_made[q], 1)
                    dve.sem_inc(shifted[q], 1)
                    dve.sem_inc(joined[q], 1)
                pipeline(dve, (1, logits), (1, messages), (3, adds))

            @block.tensor
            def _(pe):
                def rows(n):
                    q = n.q
                    pe.wait_ge(dst_hot[q], n.count(1, 1))
                    pe.wait_ge(joined[q], n.count(1, 1))
                    destination_gather(pe, m, n, dhot[q], m.dst_parts, PARTS * 2 * HEADS, row_ps[q], dst_rows[q])

                def sums(n):
                    q = n.q
                    pe.wait_ge(hot_made[q], n.count(1, 1))
                    pe.wait_ge(msg_made[q], n.count(1, 2))
                    wait_added(pe, n, added)
                    sum_groups(pe, hot[q], msg[q], sum_ps[q], full, summed[q])

                for q in range(2):
                    pe.sem_inc(dst_rows[q], 1)
                    pe.sem_inc(summed[q], 1)
                pipeline(pe, (0, rows), (2, sums))


def destination_gather(pe, m, n, dhot, table, width, bank, done):
    for g in range(PAIR):
        b = pe.value_load(m.block_tab[0:1, n.group(g)], min_val=0, max_val=NB - 1)
        for j in range(g * GROUP, (g + 1) * GROUP):
            ins = pe.matmul(bank[:, j * width:(j + 1) * width], dhot[:, j * P:(j + 1) * P],
                            table[:, ds(b, 1), :].rearrange("p o w -> p (o w)"), start=True, stop=True)
    ins.then_inc(done, 1)


def gat_nodes(nc, m, a, layer, cur, nxt):
    kt, width = gat_shape(layer)
    ot, c = width // P, width // HEADS
    chunks = [(i, min(CHUNK, N - i)) for i in range(0, N, CHUNK)]
    with Stage(nc, f"gat_nodes{layer}") as st:
        loaded, step, inverted, staged = st.sem("loaded"), st.sem("step"), st.sem("inverted"), st.sem("staged")
        product, stored, rooted = st.sem("product"), st.sem("stored"), st.sem("rooted")
        adj = st.sb("adj", [P, kt, width])
        bias, bias2, gain, shift = (st.sb(n, [P, ot]) for n in ("bias", "bias2", "gain", "shift"))
        rden = st.sb("rden", [P, NB, HEADS])
        flat = st.sb("flat", [P, width])
        stats, agg = st.sb("stats", [P, ot, len(chunks), 6]), st.sb("agg", [P, ot, 2])
        std = st.sb("std", [P, ot])
        o_ps = m.ps[0]
        columns = lambda name: a[f"L2_gnn_{name}{layer}"].rearrange("(k p) -> p k", p=P)
        with nc.Block() as block:
            @block.sync
            def _(sp):
                sp.dma_start(adj[:, :, :], a[f"L2_gnn_adj_w{layer}"].rearrange("(k p) o -> p k o", p=P)).then_inc(loaded, 16)
                with nc.allow_non_contiguous_dma(reason="four short vectors"):
                    for tile, name in ((bias, "gat_b"), (bias2, "adj_b"), (gain, "bn_g"), (shift, "bn_b")):
                        sp.dma_start(tile[:, :], columns(name)).then_inc(loaded, 16)

            @block.vector
            def _(dve):
                n = [0]

                def then(ins):
                    n[0] += 1
                    ins.then_inc(step, 1)
                    dve.wait_ge(step, n[0])

                dve.wait_ge(loaded, 16 * 5)
                then(dve.tensor_tensor(bias[:, :], bias[:, :], bias2[:, :], ALU.add))
                then(dve.reciprocal(rden[:, :, :], m.acc[:, :, width:width + HEADS]))
                with dve.Fori(0, NB) as b:
                    dve.wait_ge(product, b + 1)
                    dve.tensor_tensor(flat[:, :].rearrange("p (h c) -> p h c", c=c),
                                      m.acc[:, ds(b, 1), 0:width].rearrange("p o (h c) -> p (o h) c", c=c),
                                      spread(rden[:, ds(b, 1), :].rearrange("p o h -> p (o h)"), c), ALU.mult).then_inc(staged, 1)
                dve.wait_ge(stored, NB + 1)
                for o in range(ot):
                    for i, (at, size) in enumerate(chunks):
                        ins = dve.bn_stats(stats[:, o, i, :], nxt[:, o, at:at + size])
                    then(ins)
                    then(dve.bn_aggr(agg[:, o, :], stats[:, o, :, :].rearrange("p i s -> p (i s)")))
                then(dve.tensor_scalar(std[:, :].unsqueeze(2), agg[:, :, 1:2], 1e-5, None, ALU.add))
                dve.sem_inc(inverted, 1)
                dve.wait_ge(rooted, 1)
                then(dve.reciprocal(std[:, :], std[:, :]))
                then(dve.tensor_tensor(gain[:, :], gain[:, :], std[:, :], ALU.mult))
                then(dve.tensor_tensor(std[:, :].unsqueeze(2), agg[:, :, 0:1], gain[:, :].unsqueeze(2), ALU.mult))
                then(dve.tensor_tensor(shift[:, :], shift[:, :], std[:, :], ALU.subtract))
                dve.sem_inc(inverted, 1)

            @block.scalar
            def _(act):
                act.sem_inc(stored, 1)
                act.wait_ge(step, 2)
                with act.Fori(0, NB) as b:
                    act.wait_ge(product, b + 2)
                    for o in range(ot):
                        ins = act.activation(nxt[:, o, ds(b * P, P)], o_ps[:, o * P:(o + 1) * P], ACT.Identity, bias=bias[:, o:o + 1])
                    ins.then_inc(stored, 1)
                act.wait_ge(inverted, 1)
                act.activation(std[:, :], std[:, :], ACT.Sqrt).then_inc(rooted, 1)
                act.wait_ge(inverted, 2)
                for o in range(ot):
                    act.activation(nxt[:, o, :], nxt[:, o, :], ACT.Silu, bias=shift[:, o:o + 1], scale=gain[:, o:o + 1])

            @block.tensor
            def _(pe):
                pe.sem_inc(product, 1)
                pe.wait_ge(loaded, 16 * 5)
                with pe.Fori(0, NB) as b:
                    pe.wait_ge(staged, b + 1)
                    pe.wait_ge(stored, b + 1)
                    for o in range(ot):
                        pe.matmul(o_ps[:, o * P:(o + 1) * P], flat[:, o * P:(o + 1) * P], m.ident[:, :], start=True, stop=False)
                        for k in range(kt):
                            ins = pe.matmul(o_ps[:, o * P:(o + 1) * P], adj[:, k, o * P:(o + 1) * P], cur[:, k, ds(b * P, P)],
                                            start=False, stop=k == kt - 1)
                    ins.then_inc(product, 1)


def diffusion_out(nc, m, a, cur):
    with Stage(nc, "gat_out") as st:
        loaded, staged, product, stored = st.sem("loaded"), st.sem("staged"), st.sem("product"), st.sem("stored")
        w, bias, flat, y = st.sb("w", [P, DIM]), st.sb("bias", [P, DIM]), st.sb("flat", [P, P]), st.sb("y", [P, NB, DIM])
        o_ps = m.ps[0]
        with nc.Block() as block:
            @block.sync
            def _(sp):
                sp.dma_start(w[:, :], a["L2_gnn_out_w"]).then_inc(loaded, 16)
                sp.dma_start(bias[:, :], a["L2_gnn_out_b"].partition_broadcast(P)).then_inc(loaded, 16)

            @block.scalar
            def _(act):
                with act.Fori(0, NB) as b:
                    act.wait_ge(product, b + 1)
                    act.activation(flat[:, :], cur[:, 0, ds(b * P, P)], ACT.Copy).then_inc(staged, 1)

            @block.vector
            def _(dve):
                dve.sem_inc(stored, 1)
                dve.wait_ge(loaded, 32)
                with dve.Fori(0, NB) as b:
                    dve.wait_ge(product, b + 2)
                    dve.tensor_tensor(y[:, ds(b, 1), :], o_ps[:, 0:DIM].unsqueeze(1), bias[:, :].unsqueeze(1), ALU.add)\
                        .then_inc(stored, 1)

            @block.tensor
            def _(pe):
                pe.sem_inc(product, 1)
                pe.wait_ge(loaded, 32)
                with pe.Fori(0, NB) as b:
                    pe.wait_ge(staged, b + 1)
                    pe.wait_ge(stored, b + 1)
                    pe.matmul(o_ps[:, 0:DIM], flat[:, :], w[:, :], start=True, stop=True).then_inc(product, 1)
        residual_norm(nc, m, y)


def attention_tables(nc, m, a):
    with Stage(nc, "att_tab") as st:
        loaded, staged, turned = st.sem("loaded"), st.sem("staged"), st.sem("turned")
        evacuated, product, stored, written = st.sem("evacuated"), st.sem("product"), st.sem("stored"), st.sem("written")
        w, bias = st.sb("w", [DIM, 3 * DIM]), st.sb("bias", [P, 3 * DIM])
        flat, tall = st.sb("flat", [P, P]), st.sb("tall", [DIM, P])
        pre = st.sb("pre", [P, NB, 2 * DIM])
        x_t, res = m.ps[0], m.ps[1]
        with nc.Block() as block:
            @block.sync
            def _(sp):
                for i, k in enumerate("KVQ"):
                    part = slice(i * DIM, (i + 1) * DIM)
                    sp.dma_start(w[:, part], a[f"L3_gnn_W{k}"]).then_inc(loaded, 16)
                    sp.dma_start(bias[:, part], a[f"L3_gnn_b{k}"].partition_broadcast(P)).then_inc(loaded, 16)
                write_table(sp, m.pre_table, pre, 2 * DIM, stored, 2, written)

            @block.vector
            def _(dve):
                dve.memset(flat[:, :], 0.0).then_inc(stored, 1)
                dve.wait_ge(stored, 1)
                dve.wait_ge(loaded, 96)
                with dve.Fori(0, NB) as b:
                    dve.wait_ge(turned, b + 1)
                    dve.tensor_copy(flat[:, 0:DIM].unsqueeze(1), m.x[:, ds(b, 1), :]).then_inc(staged, 1)
                    dve.wait_ge(product, b + 2)
                    dve.tensor_tensor(pre[:, ds(b, 1), :], res[:, 0:2 * DIM].unsqueeze(1), bias[:, 0:2 * DIM].unsqueeze(1),
                                      ALU.add).then_inc(stored, 1)
                    dve.tensor_tensor(m.q_tab[:, ds(b, 1), :], res[:, 2 * DIM:3 * DIM].unsqueeze(1),
                                      bias[:, 2 * DIM:3 * DIM].unsqueeze(1), ALU.add).then_inc(stored, 1)

            @block.tensor
            def _(pe):
                pe.sem_inc(turned, 1)
                pe.sem_inc(product, 1)
                pe.wait_ge(loaded, 96)
                with pe.Fori(0, NB) as b:
                    pe.wait_ge(staged, b + 1)
                    pe.wait_ge(evacuated, b + 1)
                    pe.transpose(x_t[:, 0:P], flat[:, :], m.ident[:, :]).then_inc(turned, 1)
                    pe.wait_ge(evacuated, b + 2)
                    pe.wait_ge(stored, b * 2 + 1)
                    pe.matmul(res[:, 0:3 * DIM], tall[:, :], w[:, :], start=True, stop=True).then_inc(product, 1)

            @block.scalar
            def _(act):
                act.sem_inc(evacuated, 1)
                with act.Fori(0, NB) as b:
                    act.wait_ge(turned, b + 2)
                    act.wait_ge(product, b + 1)
                    act.activation(tall[:, :], x_t[0:DIM, 0:P], ACT.Copy).then_inc(evacuated, 1)


def attention_pass(nc, m, a):
    d = DIM // HEADS
    scale = float(np.float32(1.0 / np.sqrt(d)))
    TWOS = BATCH // 2
    with Stage(nc, "att") as st:
        g = Gather(nc, m, st, m.pre_table, 2 * DIM)
        w_zeroed, w_loaded, attr_loaded = st.sem("w_zeroed"), st.sem("w_loaded"), st.pair("attr_loaded")
        dst_loaded, dst_far, dst_hot, dst_rows = (st.pair(s) for s in ("dst_loaded", "dst_far", "dst_hot", "dst_rows"))
        turned, evacuated, edge_part = st.pair("turned"), st.pair("evacuated"), st.pair("edge_part")
        eb, kq, kqe, score, scaled, clipped, powered = (st.pair(s) for s in ("eb", "kq", "kqe", "score", "scaled", "clipped", "powered"))
        msg_made, hot_made, summed, added = st.pair("msg"), st.pair("edge_hot"), st.pair("summed"), st.sem("added")
        negated = st.sem("negated")
        w = st.sb("w", [P, P])
        bias = st.sb("bias", [P, DIM])
        minus_row = st.sb("minus_row", [P, 1])
        attr = st.pair_sb("attr", [P, BATCH, DIM])
        attr_t = st.pair_sb("attr_t", [P, TWOS * P])
        dst = st.pair_sb("dst", [P, BATCH * P])
        dhot = st.pair_sb("dhot", [P, BATCH * P])
        hot = st.pair_sb("hot", [P, BATCH, P])
        prod = st.pair_sb("prod", [P, BATCH, DIM])
        edge = st.pair_sb("edge", [P, BATCH, DIM])
        sc = st.pair_sb("sc", [P, BATCH * HEADS])
        e = st.pair_sb("e", [P, BATCH * HEADS])
        msg = st.pair_sb("msg_s", [P, BATCH, DIM])
        turn_ps, edge_ps, row_ps, sum_ps = m.ps[0:2], m.ps[2:4], m.ps[4:6], m.ps[6:8]
        by_item = lambda bank: bank[:, :].rearrange("p (b d) -> p b d", d=DIM)
        with nc.Block() as block:
            @block.gpsimd
            def _(pool):
                g.program(pool, msg_made)

            @block.sync
            def _(sp):
                sp.wait_ge(w_zeroed, 1)
                for i in range(2):
                    part = slice(i * DIM, (i + 1) * DIM)
                    sp.dma_start(w[part, part], a["L3_gnn_WE"]).then_inc(w_loaded, 16)
                sp.dma_start(bias[:, :], a["L3_gnn_bE"].partition_broadcast(P)).then_inc(w_loaded, 16)
                pipeline(sp, (0, lambda n: load_dst(sp, m, n, dst, dst_far, dst_loaded)),
                         (0, lambda n: load_attr(sp, m, n, a["edge_attr_64"], attr, turned, attr_loaded)))

            @block.scalar
            def _(act):
                def keep(n):
                    q = n.q
                    act.wait_ge(turned[q], n.count(1, 2))
                    act.wait_ge(edge_part[q], n.count(1, 1))
                    act.activation(attr_t[q][:, :], turn_ps[q][:, :], ACT.Copy).then_inc(evacuated[q], 1)

                def power(n):
                    q = n.q
                    act.wait_ge(clipped[q], n.count(1, 1))
                    act.wait_ge(msg_made[q], n.count(1, 1))
                    act.activation(e[q][:, :], sc[q][:, :], ACT.Exp).then_inc(powered[q], 1)

                for q in range(2):
                    act.sem_inc(evacuated[q], 1)
                    act.sem_inc(dst_far[q], 1)
                act.wait_ge(negated, 1)
                pipeline(act, (0, keep), (1, power),
                         (0, lambda n: make_dst_hot(act, m, n, dst, minus_row, dst_loaded, dst_rows, dst_far, dst_hot, dhot)))

            @block.vector
            def _(dve):
                def scores(n):
                    q = n.q
                    make_hot(dve, m, n, hot, summed, hot_made)
                    dve.wait_ge(edge_part[q], n.count(1, 2))
                    dve.tensor_tensor(edge[q][:, :, :], by_item(edge_ps[q]), repeat(bias[:, :], BATCH), ALU.add).then_inc(eb[q], 1)
                    dve.wait_ge(dst_rows[q], n.count(1, 2))
                    g.wait(dve, n)
                    dve.tensor_tensor(prod[q][:, :, :], g.rows[q][:, :, 0:DIM], by_item(row_ps[q]), ALU.mult).then_inc(kq[q], 1)
                    dve.wait_ge(eb[q], n.count(1, 2))
                    dve.wait_ge(kq[q], n.count(1, 2))
                    dve.tensor_tensor(prod[q][:, :, :], prod[q][:, :, :], edge[q][:, :, :], ALU.mult).then_inc(kqe[q], 1)
                    dve.wait_ge(kqe[q], n.count(1, 1))
                    dve.tensor_reduce(sc[q][:, :], prod[q][:, :, :].rearrange("p b (h d) -> p (b h) d", d=d), AX.X, ALU.add)\
                        .then_inc(score[q], 1)
                    dve.wait_ge(score[q], n.count(1, 1))
                    dve.tensor_scalar(sc[q][:, :], sc[q][:, :], scale, 5.0, ALU.mult, ALU.min).then_inc(scaled[q], 1)
                    dve.wait_ge(scaled[q], n.count(1, 1))
                    dve.tensor_single_scalar(sc[q][:, :], sc[q][:, :], -5.0, ALU.max).then_inc(clipped[q], 1)

                def messages(n):
                    q = n.q
                    dve.wait_ge(powered[q], n.count(1, 1))
                    dve.tensor_tensor(msg[q][:, :, :].rearrange("p b (h d) -> p (b h) d", d=d),
                                      g.rows[q][:, :, DIM:2 * DIM].rearrange("p b (h d) -> p b h d", d=d),
                                      spread(e[q][:, :], d), ALU.mult).then_inc(msg_made[q], 1)

                def adds(n):
                    dve.wait_ge(summed[n.q], n.count(1, 2))
                    add_groups(dve, m, n, sum_ps[n.q], DIM, added, m.acc)

                dve.memset(w[:, :], 0.0).then_inc(w_zeroed, 1)
                dve.tensor_single_scalar(minus_row[:, :], m.iota_col[:, :], -1.0, ALU.mult).then_inc(negated, 1)
                dve.memset(m.acc[:, :, :], 0.0).then_inc(added, 1)
                dve.sem_inc(added, PAIR)
                for q in range(2):
                    for s in (msg_made, eb, kq):
                        dve.sem_inc(s[q], 1)
                dve.wait_ge(w_loaded, 48)
                pipeline(dve, (1, scores), (3, adds), (1, messages))

            @block.tensor
            def _(pe):
                def turn(n):
                    q = n.q
                    pe.wait_ge(attr_loaded[q], n.count(16 * PAIR, 16 * PAIR))
                    pe.wait_ge(evacuated[q], n.count(1, 1))
                    for i in range(TWOS):
                        ins = pe.transpose(turn_ps[q][:, i * P:(i + 1) * P],
                                           attr[q][:, 2 * i:2 * i + 2, :].rearrange("p b d -> p (b d)"), m.ident[:, :])
                    ins.then_inc(turned[q], 1)

                def edge_products(n):
                    q = n.q
                    pe.wait_ge(evacuated[q], n.count(1, 2))
                    pe.wait_ge(eb[q], n.count(1, 1))
                    for i in range(TWOS):
                        ins = pe.matmul(edge_ps[q][:, i * P:(i + 1) * P], attr_t[q][:, i * P:(i + 1) * P], w[:, :],
                                        start=True, stop=True)
                    ins.then_inc(edge_part[q], 1)

                def rows(n):
                    q = n.q
                    pe.wait_ge(dst_hot[q], n.count(1, 1))
                    pe.wait_ge(kq[q], n.count(1, 1))
                    destination_gather(pe, m, n, dhot[q], m.q_tab, DIM, row_ps[q], dst_rows[q])

                def sums(n):
                    q = n.q
                    pe.wait_ge(hot_made[q], n.count(1, 1))
                    pe.wait_ge(msg_made[q], n.count(1, 2))
                    wait_added(pe, n, added)
                    sum_groups(pe, hot[q], msg[q], sum_ps[q], DIM, summed[q])

                for q in range(2):
                    for s in (turned, dst_rows, edge_part, summed):
                        pe.sem_inc(s[q], 1)
                pe.wait_ge(w_loaded, 48)
                pipeline(pe, (0, turn), (2, sums), (0, edge_products), (0, rows))


_NAMES = ["L0_gnn_rel_emb", "L0_gnn_w_loop", "L0_gnn_w_fwd", "L0_gnn_w_bwd", "x", "edge_attr_32", "edge_attr_64",
          "node_vec", "L1_gnn_msg_w1", "L1_gnn_msg_b1", "L1_gnn_msg_w2", "L1_gnn_msg_b2",
          "L1_gnn_upd_w1", "L1_gnn_upd_b1", "L1_gnn_upd_w2", "L1_gnn_upd_b2",
          "L2_gnn_init_w", "L2_gnn_init_b", "L2_gnn_te_w1", "L2_gnn_te_b1", "L2_gnn_te_w2", "L2_gnn_te_b2",
          "L2_gnn_out_w", "L2_gnn_out_b"]
_NAMES += [f"L2_gnn_{n}{i}" for i in range(3)
           for n in ("gat_w", "att_src", "att_dst", "gat_b", "adj_w", "adj_b", "bn_g", "bn_b")]
_NAMES += [f"L3_gnn_{k}{n}" for n in "QKEV" for k in "Wb"]


def kernel(**inputs):
    import concourse.bacc as bacc
    from concourse.bass_utils import run_bass_kernel_spmd

    nc = bacc.Bacc("TRN2", target_bir_lowering=False, num_devices=1)
    arrays = {n: np.ascontiguousarray(inputs[n]) for n in _NAMES}
    arrays["edges"] = np.stack([np.asarray(inputs["src"]), np.asarray(inputs["dst"]), np.asarray(inputs["edge_type_200"]),
                                np.asarray(inputs["edge_weight"]).view(np.int32)])
    half = P // 2
    freq = np.power(np.float32(1.0 / 10000.0), np.arange(half, dtype=np.float32) / np.float32(half)).astype(np.float32)
    phase = np.repeat(np.array([0.0, np.pi / 2], np.float32), half)
    arrays["freq"] = np.stack([np.concatenate([freq, freq]), phase], axis=1)
    a = {n: nc.dram_tensor(f"in_{n}", v.shape, mybir.dt.from_np(v.dtype), kind="ExternalInput").ap()
         for n, v in arrays.items()}
    out = nc.dram_tensor("out", (N, DIM), F32, kind="ExternalOutput").ap()
    build(nc, a, out)
    r = run_bass_kernel_spmd(nc, [{f"in_{n}": v for n, v in arrays.items()}], core_ids=[0])
    return r.results[0]["out"]
```

```python
from contextlib import ExitStack

import numpy as np
import concourse.bass as bass
from concourse import mybir

F32 = mybir.dt.float32
I32 = mybir.dt.int32
BF16 = mybir.dt.bfloat16
ALU = mybir.AluOpType
ACT = mybir.ActivationFunctionType
AX = mybir.AxisListType

P = 128
N, E, DIM = 3125, 103125, 64
NB = -(-N // P)
NP = NB * P
GROUP = 4
GE = GROUP * P
PAIR = 2
BATCH = PAIR * GROUP
NG = -(-((E + NB * (GE - 1)) // GE) // (2 * PAIR)) * 2 * PAIR
STEPS = NG // PAIR
KG = -(-NG // P)
NGP = KG * P
NIP = NGP * GROUP
ER, EC = 125, E // 125
HALF_REL = 100
HEADS = 8
PARTS = 3
FAR = -1.0e30
CHUNK = 512
ROUND = 5
ds = bass.ds


class Mem:
    pass


def build(nc, a, out):
    m = Mem()
    m.norms = 0
    with ExitStack() as ctx:
        def sb(name, shape, dt=F32):
            return ctx.enter_context(nc.sbuf_tensor(name, shape, dt))

        def dram(name, shape, dt=F32):
            return nc.dram_tensor(name, shape, dt, kind="Internal").ap()

        m.group_first = dram("group_first", [NGP], I32)
        m.group_block = dram("group_block", [NGP], I32)
        m.edge_rows = dram("edge_rows", [4, NGP, GE], I32)
        m.dst_rows = dram("dst_rows", [NGP, GE])
        m.rel_rows = dram("rel_rows", [NGP, GE])
        m.run_rows = dram("run_rows", [NGP, GE])
        m.sorted_edges = dram("sorted_edges", [4, E], I32)
        m.sorted_attr_32 = dram("sorted_attr_32", [E, 32])
        m.sorted_attr_64 = dram("sorted_attr_64", [E, DIM])
        m.node_count = dram("node_count", [NP, 1])
        m.node_start = dram("node_start", [NP, 1])
        m.x_table = dram("x_table", [NP, DIM])
        m.pre_table = dram("pre_table", [NP, 2 * DIM])
        m.xw_table = dram("xw_table", [NP, 264])
        m.xw_table2 = dram("xw_table2", [NP, 136])
        m.al_table = dram("al_table", [NP, HEADS])

        m.ident = sb("ident", [P, P])
        m.iota_row = sb("iota_row", [P, P])
        m.iota_col = sb("iota_col", [P, 1])
        m.ones = sb("ones", [P, P])
        m.src_i = sb("src_i", [P, NIP], I32)
        m.dst_l = sb("dst_l", [P, NIP])
        m.w_fwd = sb("w_fwd", [P, NIP])
        m.w_bwd = sb("w_bwd", [P, NIP])
        m.run_end = sb("run_end", [P, NIP])
        m.unsorted = sb("unsorted", [1, 1], I32)
        m.late = sb("late", [P, KG])
        m.blk_col = sb("blk_col", [P, KG])
        m.first_tab = sb("first_tab", [1, NGP], I32)
        m.block_tab = sb("block_tab", [1, NGP], I32)
        m.x = sb("x", [P, NB, DIM])
        m.acc = sb("acc", [P, NB, 264])
        m.ps = [ctx.enter_context(nc.psum_tensor(f"bank{i}", [P, 512], F32)) for i in range(8)]

        constants(nc, m)
        edge_order(nc, m, a)
        sort_edges(nc, m, a)
        group_tables(nc, m, a)
        edge_columns(nc, m, a)
        load_nodes(nc, m, a)
        with ExitStack() as c:
            m.y = c.enter_context(nc.sbuf_tensor("y", [P, NB, DIM], F32))
            compgcn_pass(nc, m, a, 0, a["x"])
            compgcn_nodes(nc, m, a, 0, m.x, m.y)
            compgcn_pass(nc, m, a, 1, m.x_table)
            compgcn_nodes(nc, m, a, 1, m.y, m.y)
            residual_norm(nc, m, m.y)
        message_tables(nc, m, a)
        message_pass(nc, m, a)
        message_nodes(nc, m, a)
        with ExitStack() as c:
            def cb(name, shape, dt=F32):
                return c.enter_context(nc.sbuf_tensor(name, shape, dt))
            m.ft = cb("ft", [P, 2, NP])
            m.ft2 = cb("ft2", [P, 2, NP])
            m.node_out = cb("node_out", [P, NB, 272])
            m.al_max = cb("al_max", [P, NB, HEADS])
            m.dst_tab = cb("dst_tab", [P, NB, 2 * HEADS])
            m.dst_parts = cb("dst_parts", [P, NB, PARTS * 2 * HEADS], BF16)
            cur, nxt = m.ft, m.ft2
            diffusion_embed(nc, m, a, cur)
            for layer in range(3):
                gat_tables(nc, m, a, layer, cur)
                gat_max_pass(nc, m, layer)
                gat_self_loops(nc, m, layer)
                gat_sum_pass(nc, m, layer)
                gat_nodes(nc, m, a, layer, cur, nxt)
                cur, nxt = nxt, cur
            diffusion_out(nc, m, a, cur)
        with ExitStack() as c:
            m.kvq = c.enter_context(nc.sbuf_tensor("kvq", [P, NB, 3 * DIM], F32))
            attention_tables(nc, m, a)
            attention_pass(nc, m, a)
        residual_norm(nc, m, m.acc[:, :, 0:DIM])
        finish(nc, m, out)


class Stage:

    def __init__(self, nc, name):
        self.nc, self.name, self.stack, self.sems = nc, name, ExitStack(), []

    def sem(self, name):
        s = self.nc.alloc_semaphore(f"{self.name}_{name}")
        self.sems.append(s)
        return s

    def pair(self, name):
        return [self.sem(f"{name}_{q}") for q in range(2)]

    def sb(self, name, shape, dt=F32):
        return self.stack.enter_context(self.nc.sbuf_tensor(f"{self.name}_{name}", shape, dt))

    def pair_sb(self, name, shape, dt=F32):
        return [self.sb(f"{name}_{q}", shape, dt) for q in range(2)]

    def __enter__(self):
        return self

    def __exit__(self, *e):
        if e[0] is None:
            self.nc.clear_and_free_semaphores(self.sems)
            self.nc.all_engine_barrier()
        self.stack.close()


def spread(ap, count):
    return ap.unsqueeze(2).to_broadcast([ap.shape[0], ap.shape[1], count])


def repeat(ap, count):
    return ap.unsqueeze(1).to_broadcast([ap.shape[0], count, ap.shape[1]])


def constants(nc, m):
    with Stage(nc, "const") as st:
        made = st.sem("const_made")
        zeroed = st.sem("ident_zeroed")
        with nc.Block() as block:
            @block.gpsimd
            def _(pool):
                pool.iota(m.iota_row[:, :], [[1, P]], base=0, channel_multiplier=0,
                          allow_small_or_imprecise_dtypes=True).then_inc(made, 1)
                pool.iota(m.iota_col[:, :], [[1, 1]], base=0, channel_multiplier=1,
                          allow_small_or_imprecise_dtypes=True).then_inc(made, 1)
                pool.memset(m.ident[:, :], 0.0).then_inc(zeroed, 1)
                pool.wait_ge(zeroed, 1)
                pool.affine_select(out=m.ident[:, :], in_=m.ident[:, :], compare_op=ALU.not_equal, fill=1.0,
                                   base=0, pattern=[[-1, P]], channel_multiplier=1).then_inc(made, 1)

            @block.vector
            def _(dve):
                dve.memset(m.ones[:, :], 1.0).then_inc(made, 1)


def group_tables(nc, m, a):
    with Stage(nc, "groups") as st:
        loaded, cast, counted, totals = st.sem("dst_loaded"), st.sem("dst_cast"), st.sem("counted"), st.sem("totals")
        step, idx_made, stored, back = st.sem("step"), st.sem("ids_made"), st.sem("tables_stored"), st.sem("tables_back")
        di, df, hit = st.sb("dst_int", [ER, EC], I32), st.sb("dst_f", [ER, EC]), st.sb("below", [ER, EC])
        cnt = st.sb("below_count", [ER, NB + 1])
        first = st.sb("first_edge", [P, NB + 1])
        n_e, n_ii = st.sb("edges_of", [P, NB]), st.sb("groups_int", [P, NB], I32)
        n_i, base = st.sb("groups_of", [P, NB]), st.sb("groups_to", [P, NB + 1])
        lag, dlag = st.sb("lag", [P, NB]), st.sb("dlag", [P, NB])
        ids, blk, e0, past = (st.sb(n, [P, KG]) for n in ("ids", "blk", "nominal", "past"))
        tab_f, tab_b = st.sb("tab_f", [P, KG], I32), st.sb("tab_b", [P, KG], I32)
        clip = st.sb("clipped", [P, KG])
        tot = m.ps[0]
        with nc.Block() as block:
            @block.sync
            def _(sp):
                sp.dma_start(di[:, :], a["edges"][1, :].rearrange("(p c) -> p c", p=ER)).then_inc(loaded, 16)
                sp.wait_ge(stored, 1)
                with nc.allow_non_contiguous_dma(reason="two small tables"):
                    sp.dma_start(m.group_first.rearrange("(k p) -> p k", p=P), tab_f[:, :]).then_inc(back, 16)
                    sp.dma_start(m.group_block.rearrange("(k p) -> p k", p=P), tab_b[:, :]).then_inc(back, 16)
                sp.wait_ge(back, 32)
                sp.dma_start(m.first_tab[:, :], m.group_first.unsqueeze(0)).then_inc(back, 16)
                sp.dma_start(m.block_tab[:, :], m.group_block.unsqueeze(0)).then_inc(back, 16)
                sp.wait_ge(back, 64)

            @block.gpsimd
            def _(pool):
                pool.iota(ids[:, :], [[P, KG]], base=0, channel_multiplier=1,
                          allow_small_or_imprecise_dtypes=True).then_inc(idx_made, 1)

            @block.vector
            def _(dve):
                n = [0]

                def then(ins):
                    n[0] += 1
                    ins.then_inc(step, 1)
                    dve.wait_ge(step, n[0])

                dve.wait_ge(loaded, 16)
                dve.memset(cnt[:, :], 0.0).then_inc(cast, 1)
                dve.tensor_copy(df[:, :], di[:, :]).then_inc(cast, 1)
                dve.wait_ge(cast, 2)
                for b in range(1, NB):
                    then(dve.tensor_scalar(hit[:, :], df[:, :], float(P * b), 0.0, ALU.is_lt, ALU.add,
                                           accum_out=cnt[:, b:b + 1]))
                dve.memset(cnt[:, NB:NB + 1], float(EC)).then_inc(counted, 1)
                dve.wait_ge(totals, 1)
                then(dve.tensor_copy(first[:, :], tot[:, 0:NB + 1]))
                then(dve.tensor_tensor(n_e[:, :], first[:, 1:NB + 1], first[:, 0:NB], ALU.subtract))
                then(dve.tensor_scalar(n_ii[:, :], n_e[:, :], float(GE - 1), None, ALU.add))
                then(dve.tensor_single_scalar(n_ii[:, :], n_ii[:, :], GE.bit_length() - 1, ALU.arith_shift_right))
                then(dve.tensor_copy(n_i[:, :], n_ii[:, :]))
                then(dve.memset(base[:, 0:1], 0.0))
                then(dve.tensor_tensor_scan(base[:, 1:NB + 1], m.ones[:, 0:NB], n_i[:, :], 0.0, ALU.mult, ALU.add))
                then(dve.scalar_tensor_tensor(lag[:, :], base[:, 0:NB], float(-GE), first[:, 0:NB], ALU.mult, ALU.add))
                then(dve.tensor_tensor(dlag[:, 1:NB], lag[:, 1:NB], lag[:, 0:NB - 1], ALU.subtract))
                dve.wait_ge(idx_made, 1)
                then(dve.memset(blk[:, :], 0.0))
                then(dve.tensor_scalar(e0[:, :], ids[:, :], float(GE), lag[:, 0:1], ALU.mult, ALU.add))
                for b in range(1, NB):
                    then(dve.tensor_scalar(past[:, :], ids[:, :], base[:, b:b + 1], None, ALU.is_ge))
                    then(dve.tensor_tensor(blk[:, :], blk[:, :], past[:, :], ALU.add))
                    then(dve.scalar_tensor_tensor(e0[:, :], past[:, :], dlag[:, b:b + 1], e0[:, :], ALU.mult, ALU.add))
                then(dve.tensor_scalar(past[:, :], ids[:, :], base[:, NB:NB + 1], float(E), ALU.is_ge, ALU.mult))
                then(dve.tensor_tensor(e0[:, :], e0[:, :], past[:, :], ALU.add))
                then(dve.tensor_scalar(clip[:, :], e0[:, :], float(E - GE), None, ALU.min))
                then(dve.tensor_tensor(m.late[:, :], e0[:, :], clip[:, :], ALU.subtract))
                then(dve.tensor_copy(m.blk_col[:, :], blk[:, :]))
                then(dve.tensor_copy(tab_f[:, :], clip[:, :]))
                dve.tensor_copy(tab_b[:, :], blk[:, :]).then_inc(stored, 1)

            @block.tensor
            def _(pe):
                pe.wait_ge(counted, 1)
                pe.matmul(tot[:, 0:NB + 1], m.ones[0:ER, :], cnt[:, :], start=True, stop=True).then_inc(totals, 1)


def edge_columns(nc, m, a):
    UN = 4
    with Stage(nc, "cols") as st:
        copied, rowed = [st.sem("rows_copied_sp"), st.sem("rows_copied_act")], st.sem("rows_loaded")
        ready, turned, kept, wrote = st.sem("rows_ready"), st.sem("turned"), st.sem("kept"), st.sem("rows_written")
        step = st.sem("step")
        ri = st.sb("int_rows", [P, KG, 4, GE], I32)
        rw = ri[:, :, 3, :].bitcast(F32)
        src, dst, rel = (st.sb(n, [P, KG, GE]) for n in ("src", "dst", "rel"))
        wf, wb, end, run = (st.sb(n, [P, KG, GE]) for n in ("wf", "wb", "end", "run"))
        tmp = st.sb("tmp", [P, KG, GE])
        count, counted = st.sb("count", [P, GE]), st.sem("counted")

        def copy_rows(eng, odd):
            def loop(edges):
                with eng.Fori(0, NGP // (2 * UN)) as i:
                    for u in range(UN):
                        group = ds(i * (2 * UN) + (2 * u + odd), 1)
                        e = eng.value_load(m.first_tab[0:1, group], min_val=0, max_val=E - GE)
                        eng.dma_start(m.edge_rows[:, group, :], edges[:, ds(e, GE)].unsqueeze(1)).then_inc(copied[odd], 16)

            with eng.If(is_unsorted(eng, m) > 0):
                loop(m.sorted_edges)
            with eng.Else():
                loop(a["edges"])

        with nc.Block() as block:
            @block.sync
            def _(sp):
                copy_rows(sp, 0)
                for odd in range(2):
                    sp.wait_ge(copied[odd], 8 * NGP)
                for k in range(KG):
                    sp.dma_start(ri[:, k, :, :], m.edge_rows[:, k * P:(k + 1) * P, :].rearrange("t p e -> p t e"))\
                      .then_inc(rowed, 16)
                sp.wait_ge(ready, 1)
                for rows, tile in ((m.dst_rows, dst), (m.rel_rows, rel), (m.run_rows, run)):
                    sp.dma_start(rows.rearrange("(k p) e -> p k e", p=P), tile[:, :, :]).then_inc(wrote, 16)
                sp.wait_ge(wrote, 48)

            @block.gpsimd
            def _(pool):
                pool.iota(count[:, :], [[1, GE]], base=0, channel_multiplier=0,
                          allow_small_or_imprecise_dtypes=True).then_inc(counted, 1)

            @block.scalar
            def _(act):
                copy_rows(act, 1)

            @block.vector
            def _(dve):
                n = [0]

                def then(ins):
                    n[0] += 1
                    ins.then_inc(step, 1)
                    dve.wait_ge(step, n[0])

                dve.wait_ge(rowed, 16 * KG)
                dve.wait_ge(counted, 1)
                then(dve.tensor_copy(src[:, :, :], ri[:, :, 0, :]))
                then(dve.tensor_copy(dst[:, :, :], ri[:, :, 1, :]))
                then(dve.tensor_copy(rel[:, :, :], ri[:, :, 2, :]))
                then(dve.scalar_tensor_tensor(dst[:, :, :], spread(m.blk_col[:, :], GE), float(-P), dst[:, :, :],
                                              ALU.mult, ALU.add))
                then(dve.tensor_tensor(tmp[:, :, :], repeat(count[:, :], KG), spread(m.late[:, :], GE), ALU.is_lt))
                then(dve.scalar_tensor_tensor(dst[:, :, :], tmp[:, :, :], float(-4 * NP), dst[:, :, :],
                                              ALU.mult, ALU.add))
                then(dve.tensor_tensor(end[:, :, 0:GE - 1], dst[:, :, 0:GE - 1], dst[:, :, 1:GE], ALU.not_equal))
                for j in range(GROUP):
                    ins = dve.memset(end[:, :, (j + 1) * P - 1:(j + 1) * P], 1.0)
                then(ins)
                then(dve.tensor_single_scalar(run[:, :, 1:GE], end[:, :, 0:GE - 1], FAR, ALU.mult))
                then(dve.memset(run[:, :, 0:1], FAR))
                then(dve.tensor_single_scalar(tmp[:, :, :], rel[:, :, :], float(HALF_REL), ALU.is_ge))
                then(dve.tensor_tensor(wb[:, :, :], rw, tmp[:, :, :], ALU.mult))
                then(dve.tensor_tensor(wf[:, :, :], rw, wb[:, :, :], ALU.subtract))
                then(dve.scalar_tensor_tensor(rel[:, :, :], tmp[:, :, :], float(-HALF_REL), rel[:, :, :],
                                              ALU.mult, ALU.add))
                dve.sem_inc(ready, 1)
                for k in range(KG):
                    dve.wait_ge(turned, k + 1)
                    for i, t in enumerate((m.src_i, m.dst_l, m.w_fwd, m.w_bwd, m.run_end)):
                        ins = dve.tensor_copy(t[:, k * GE:(k + 1) * GE].rearrange("p (g j) -> p j g", j=GROUP),
                                              m.ps[i][:, :].rearrange("p (j g) -> p j g", j=GROUP))
                    ins.then_inc(kept, 1)

            @block.tensor
            def _(pe):
                pe.wait_ge(ready, 1)
                for k in range(KG):
                    if k:
                        pe.wait_ge(kept, k)
                    for i, t in enumerate((src, dst, wf, wb, end)):
                        for j in range(GROUP):
                            ins = pe.transpose(m.ps[i][:, j * P:(j + 1) * P], t[:, k, j * P:(j + 1) * P], m.ident[:, :])
                    ins.then_inc(turned, 1)


def load_nodes(nc, m, a):
    full = N // P
    with Stage(nc, "nodes") as st:
        loaded, zeroed = st.sem("loaded"), st.sem("zeroed")
        with nc.Block() as block:
            @block.vector
            def _(dve):
                dve.memset(m.x[:, full, :], 0.0).then_inc(zeroed, 1)

            @block.sync
            def _(sp):
                sp.dma_start(m.x[:, 0:full, :], a["x"][0:full * P, :].rearrange("(b p) d -> p b d", p=P))\
                  .then_inc(loaded, 16)
                sp.wait_ge(zeroed, 1)
                sp.dma_start(m.x[0:N - full * P, full, :], a["x"][full * P:N, :]).then_inc(loaded, 16)
                sp.wait_ge(loaded, 32)


def finish(nc, m, out):
    full = N // P
    with Stage(nc, "finish") as st:
        stored = st.sem("stored")
        with nc.Block() as block:
            @block.sync
            def _(sp):
                sp.dma_start(out[0:full * P, :].rearrange("(b p) d -> p b d", p=P), m.x[:, 0:full, :])\
                  .then_inc(stored, 16)
                sp.dma_start(out[full * P:N, :], m.x[0:N - full * P, full, :]).then_inc(stored, 16)
                sp.wait_ge(stored, 32)


def edge_order(nc, m, a):
    rows = 127
    cols = (E - 1) // rows
    with Stage(nc, "order") as st:
        loaded, step, counted, totals = st.sem("loaded"), st.sem("step"), st.sem("counted"), st.sem("totals")
        both_i, both = st.sb("both_int", [rows, 2, cols], I32), st.sb("both", [rows, 2, cols])
        falls, count, tot = st.sb("falls", [rows, cols]), st.sb("count", [rows, 1]), m.ps[0]
        flag = st.sb("flag", [1, 1])
        dst = a["edges"][1, :]
        with nc.Block() as block:
            @block.sync
            def _(sp):
                for i in range(2):
                    sp.dma_start(both_i[:, i, :], dst[i:i + E - 1].rearrange("(p c) -> p c", p=rows)).then_inc(loaded, 16)

            @block.vector
            def _(dve):
                n = [0]

                def then(ins):
                    n[0] += 1
                    ins.then_inc(step, 1)
                    dve.wait_ge(step, n[0])

                dve.wait_ge(loaded, 32)
                then(dve.tensor_copy(both[:, :, :], both_i[:, :, :]))
                then(dve.tensor_tensor(falls[:, :], both[:, 1, :], both[:, 0, :], ALU.is_lt))
                dve.tensor_reduce(count[:, :], falls[:, :], AX.X, ALU.add).then_inc(counted, 1)
                dve.wait_ge(totals, 1)
                then(dve.tensor_single_scalar(flag[:, :], tot[0:1, 0:1], 1.0, ALU.min))
                dve.tensor_copy(m.unsorted[:, :], flag[:, :])

            @block.tensor
            def _(pe):
                pe.wait_ge(counted, 1)
                pe.matmul(tot[:, 0:1], m.ones[0:rows, :], count[:, :], start=True, stop=True).then_inc(totals, 1)


def is_unsorted(eng, m):
    return eng.value_load(m.unsorted[0:1, 0:1], min_val=0, max_val=1)


def sort_edges(nc, m, a):
    with Stage(nc, "sort") as st:
        loaded, cast, zeroed, cleared = st.sem("loaded"), st.sem("cast"), st.sem("zeroed"), st.sem("cleared")
        picked, spread_out, row_made, matched, earlier = (st.sem(s) for s in ("picked", "diagonal", "row", "matched", "earlier"))
        ranked, renewed, got, counted, passed = (st.sem(s) for s in ("ranked", "renewed", "got", "counted", "passed"))
        below, degrees, summed, started, starts_out = (st.sem(s) for s in ("below", "degrees", "summed", "starts", "starts_out"))
        recorded, delivered = st.sem("recorded"), st.sem("delivered")
        chosen, placed, found, attr_in = (st.sem(s) for s in ("chosen", "placed", "found", "attr_in"))
        rows_sent, attr_sent = st.sem("rows_sent"), st.sem("attr_sent")
        edges = st.sb("edges", [ER, 4, EC], I32)
        dst = st.sb("dst", [ER, EC])
        rank = st.sb("rank", [ER, EC])
        zeros = st.sb("zeros", [P, NB])
        lower = st.sb("lower", [ER, ER])
        index, col = st.sb("index", [ER, 1], I32), st.sb("col", [ER, 1])
        diag, same, before = st.sb("diag", [ER, ER]), st.sb("same", [ER, ER]), st.sb("before", [ER, ER])
        base, total, within, new = (st.sb(s, [ER, 1]) for s in ("base", "total", "within", "new"))
        degree, ends = st.sb("degree", [1, NP]), st.sb("ends", [1, NP])
        one_row = st.sb("one_row", [1, NP])
        pos, pos_i, value = st.sb("pos", [ER, 4]), st.sb("pos_int", [ER, 4], I32), st.sb("value", [ER, 4], I32)
        at32, at64 = st.sb("at32", [ER, 32]), st.sb("at64", [ER, DIM])
        row_ps = m.ps[0]
        flat_edges = m.sorted_edges.rearrange("r e -> (r e)").unsqueeze(1)
        attr32, attr64 = (a[f"edge_attr_{w}"].rearrange("(p c) d -> p c d", p=ER) for w in (32, 64))
        with nc.Block() as block:
            @block.sync
            def _(sp):
                with sp.If(is_unsorted(sp, m) > 0):
                    sp.dma_start(edges[:, :, :], a["edges"].rearrange("r (p c) -> p r c", p=ER)).then_inc(loaded, 16)
                    sp.wait_ge(zeroed, 1)
                    sp.dma_start(m.node_count.rearrange("(p b) o -> p (b o)", p=P), zeros[:, :]).then_inc(cleared, 16)
                    sp.wait_ge(counted, 16 * EC)
                    sp.dma_start(degree[:, :], m.node_count.rearrange("n o -> o n")).then_inc(degrees, 16)
                    sp.wait_ge(started, 1)
                    sp.dma_start(m.node_start.rearrange("n o -> o n"), ends[:, :]).then_inc(starts_out, 16)
                    with sp.Fori(0, EC) as c:
                        sp.wait_ge(delivered, c + 1)
                        sp.dma_start(at32[:, :].unsqueeze(1), attr32[:, ds(c, 1), :]).then_inc(attr_in, 16)
                        sp.dma_start(at64[:, :].unsqueeze(1), attr64[:, ds(c, 1), :]).then_inc(attr_in, 16)

            @block.gpsimd
            def _(pool):
                def at(index):
                    return bass.IndirectOffsetOnAxis(ap=index, axis=0)

                with pool.If(is_unsorted(pool, m) > 0):
                    pool.memset(lower[:, :], 1.0).then_inc(below, 1)
                    pool.wait_ge(below, 1)
                    pool.affine_select(out=lower[:, :], in_=lower[:, :], compare_op=ALU.is_gt, fill=0.0,
                                       base=0, pattern=[[-1, ER]], channel_multiplier=1).then_inc(below, 1)
                    pool.wait_ge(cleared, 16)
                    pool.sem_inc(recorded, 1)
                    with pool.Fori(0, EC) as c:
                        pool.wait_ge(picked, c * 2 + 2)
                        pool.sem_inc(passed, 1)
                        pool.indirect_dma_start(base[:, :], None, m.node_count, at(index[:, :])).then_inc(got, 16)
                        pool.wait_ge(renewed, c + 1)
                        pool.sem_inc(passed, 1)
                        pool.indirect_dma_start(m.node_count, at(index[:, :]), new[:, :], None).then_inc(counted, 16)
                        pool.wait_ge(counted, c * 16 + 16)
                        pool.sem_inc(recorded, 1)
                    pool.wait_ge(starts_out, 16)
                    pool.sem_inc(delivered, 1)
                    with pool.Fori(0, EC) as c:
                        pool.wait_ge(chosen, c * 2 + 2)
                        pool.sem_inc(passed, 1)
                        pool.indirect_dma_start(base[:, :], None, m.node_start, at(index[:, :])).then_inc(found, 16)
                        pool.wait_ge(placed, c * 3 + 3)
                        pool.wait_ge(attr_in, c * 32 + 32)
                        pool.sem_inc(passed, 1)
                        for r in range(4):
                            pool.indirect_dma_start(flat_edges, at(pos_i[:, r:r + 1]), value[:, r:r + 1], None).then_inc(rows_sent, 16)
                        pool.indirect_dma_start(m.sorted_attr_32, at(pos_i[:, 0:1]), at32[:, :], None).then_inc(attr_sent, 16)
                        pool.indirect_dma_start(m.sorted_attr_64, at(pos_i[:, 0:1]), at64[:, :], None).then_inc(attr_sent, 16)
                        pool.wait_ge(rows_sent, c * 64 + 64)
                        pool.wait_ge(attr_sent, c * 32 + 32)
                        pool.sem_inc(delivered, 1)

            @block.vector
            def _(dve):
                with dve.If(is_unsorted(dve, m) > 0):
                    dve.memset(zeros[:, :], 0.0).then_inc(zeroed, 1)
                    dve.memset(one_row[:, :], 1.0).then_inc(zeroed, 1)
                    dve.wait_ge(loaded, 16)
                    dve.tensor_copy(dst[:, :], edges[:, 1, :]).then_inc(cast, 1)
                    dve.wait_ge(cast, 1)
                    dve.wait_ge(below, 2)
                    dve.sem_inc(matched, 1)
                    with dve.Fori(0, EC) as c:
                        dve.wait_ge(recorded, c + 1)
                        dve.tensor_copy(index[:, :], edges[:, 1, ds(c, 1)]).then_inc(picked, 1)
                        dve.tensor_copy(col[:, :], dst[:, ds(c, 1)]).then_inc(picked, 1)
                        dve.wait_ge(picked, c * 2 + 2)
                        dve.tensor_scalar(diag[:, :], m.ident[0:ER, 0:ER], col[:, 0:1], None, ALU.mult).then_inc(spread_out, 1)
                        dve.wait_ge(row_made, c + 1)
                        dve.tensor_scalar(same[:, :], row_ps[0:ER, 0:ER], col[:, 0:1], None, ALU.is_equal).then_inc(matched, 1)
                        dve.wait_ge(matched, c + 2)
                        dve.tensor_reduce(total[:, :], same[:, :], AX.X, ALU.add).then_inc(earlier, 1)
                        dve.tensor_tensor(before[:, :], same[:, :], lower[:, :], ALU.mult).then_inc(earlier, 1)
                        dve.wait_ge(earlier, c * 3 + 2)
                        dve.tensor_reduce(within[:, :], before[:, :], AX.X, ALU.add).then_inc(earlier, 1)
                        dve.wait_ge(earlier, c * 3 + 3)
                        dve.wait_ge(got, c * 16 + 16)
                        dve.tensor_tensor(rank[:, ds(c, 1)], base[:, :], within[:, :], ALU.add).then_inc(ranked, 1)
                        dve.tensor_tensor(new[:, :], base[:, :], total[:, :], ALU.add).then_inc(renewed, 1)
                    dve.wait_ge(degrees, 16)
                    dve.wait_ge(zeroed, 2)
                    dve.tensor_tensor_scan(ends[:, :], one_row[:, :], degree[:, :], 0.0, ALU.mult, ALU.add).then_inc(summed, 1)
                    dve.wait_ge(summed, 1)
                    dve.tensor_tensor(ends[:, :], ends[:, :], degree[:, :], ALU.subtract).then_inc(started, 1)
                    dve.wait_ge(ranked, EC)
                    with dve.Fori(0, EC) as c:
                        dve.wait_ge(delivered, c + 1)
                        dve.tensor_copy(index[:, :], edges[:, 1, ds(c, 1)]).then_inc(chosen, 1)
                        dve.tensor_copy(value[:, :].unsqueeze(2), edges[:, :, ds(c, 1)]).then_inc(chosen, 1)
                        dve.wait_ge(found, c * 16 + 16)
                        dve.tensor_tensor(pos[:, 0:1], base[:, :], rank[:, ds(c, 1)], ALU.add).then_inc(placed, 1)
                        dve.wait_ge(placed, c * 3 + 1)
                        for r in range(1, 4):
                            ins = dve.tensor_single_scalar(pos[:, r:r + 1], pos[:, 0:1], float(r * E), ALU.add)
                        ins.then_inc(placed, 1)
                        dve.wait_ge(placed, c * 3 + 2)
                        dve.tensor_copy(pos_i[:, :], pos[:, :]).then_inc(placed, 1)

            @block.tensor
            def _(pe):
                with pe.If(is_unsorted(pe, m) > 0):
                    with pe.Fori(0, EC) as c:
                        pe.wait_ge(matched, c + 1)
                        pe.wait_ge(spread_out, c + 1)
                        pe.matmul(row_ps[0:ER, 0:ER], m.ones[0:ER, 0:ER], diag[:, :], start=True, stop=True).then_inc(row_made, 1)


class Step:

    def __init__(self, turn, ahead, q):
        self.turn, self.ahead, self.q = turn, ahead, q

    def count(self, per, plus):
        plus = plus + per * self.ahead
        if self.turn is None:
            return plus
        scaled = self.turn if per == 1 else self.turn * per
        return scaled + plus if plus else scaled

    def items(self):
        return ds(self.count(2 * BATCH, self.q * BATCH), BATCH)

    def group(self, g=0, size=1):
        return ds(self.count(2 * PAIR, self.q * PAIR + g), size)


def pipeline(eng, *parts):
    last = max(lag for lag, _ in parts)
    head = last + last % 2

    def at(times):
        for t in times:
            for lag, part in parts:
                if 0 <= t - lag < STEPS:
                    part(Step(None, (t - lag) // 2, (t - lag) % 2))

    at(range(head))
    with eng.Fori(head // 2, STEPS // 2) as turn:
        for r in range(2):
            for lag, part in parts:
                part(Step(turn, (r - lag) // 2, (r - lag) % 2))
    at(range(STEPS, STEPS + last))


def blocks_by_two(eng, part):
    with eng.Fori(0, NB // 2) as t:
        for q in range(2):
            part(t * 2 + q if q else t * 2, q)
    if NB % 2:
        part(NB - 1, 0)


class Gather:

    def __init__(self, nc, m, st, table, width):
        self.m, self.table = m, table
        self.rows = st.pair_sb("rows", [P, BATCH, width])
        self.index = st.pair_sb("index", [P, BATCH], I32)
        self.index_set = st.pair("index_set")
        self.gathered = st.pair("gathered")
        self.passed = st.sem("passed")

    def program(self, pool, rows_used, per=1):
        def indices(n):
            pool.wait_ge(rows_used[n.q], n.count(per, per))
            pool.tensor_copy(self.index[n.q][:, :], self.m.src_i[:, n.items()]).then_inc(self.index_set[n.q], 1)

        def gather(n, items):
            for j in items:
                pool.indirect_dma_start(self.rows[n.q][:, j, :], None, self.table,
                                        bass.IndirectOffsetOnAxis(ap=self.index[n.q][:, j:j + 1], axis=0))\
                    .then_inc(self.gathered[n.q], 16)

        def most(n):
            pool.wait_ge(self.index_set[n.q], n.count(1, 1))
            pool.sem_inc(self.passed, 1)
            gather(n, range(BATCH - 2))

        def rest(n):
            gather(n, range(BATCH - 2, BATCH))

        pipeline(pool, (1, most), (0, indices), (1, rest))

    def wait(self, eng, n):
        eng.wait_ge(self.gathered[n.q], n.count(16 * BATCH, 16 * BATCH))


def make_hot(dve, m, n, hot, summed, hot_made):
    dve.wait_ge(summed[n.q], n.count(1, 1))
    dve.tensor_tensor(hot[n.q][:, :, :], repeat(m.iota_row[:, :], BATCH), spread(m.dst_l[:, n.items()], P), ALU.is_equal)\
        .then_inc(hot_made[n.q], 1)


def make_dst_hot(act, m, n, dst, minus_row, dst_loaded, dst_rows, dst_far, dst_hot, dhot):
    q = n.q
    act.wait_ge(dst_loaded[q], n.count(16, 16))
    act.wait_ge(dst_rows[q], n.count(1, 1))
    act.activation(dhot[q][:, :], dst[q][:, :], ACT.Abs, bias=minus_row[:, 0:1]).then_inc(dst_far[q], 1)
    act.wait_ge(dst_far[q], n.count(1, 2))
    act.activation(dhot[q][:, :], dhot[q][:, :], ACT.Relu, scale=-1.0, bias=m.ones[:, 0:1]).then_inc(dst_hot[q], 1)


def load_dst(sp, m, n, dst, dst_far, dst_loaded):
    sp.wait_ge(dst_far[n.q], n.count(1, 1))
    sp.dma_start(dst[n.q][:, :], m.dst_rows[n.group(size=PAIR), :].rearrange("g e -> (g e)").partition_broadcast(P))\
      .then_inc(dst_loaded[n.q], 16)


def sum_groups(pe, hot, msg, banks, width, summed):
    for g in range(PAIR):
        for j in range(GROUP):
            ins = pe.matmul(place(banks, g, width), hot[:, g * GROUP + j, :], msg[:, g * GROUP + j, 0:width],
                            start=j == 0, stop=j == GROUP - 1)
    ins.then_inc(summed, 1)


def add_groups(dve, m, n, banks, width, added, acc, op=ALU.add):
    for g in range(PAIR):
        b = dve.value_load(m.block_tab[0:1, n.group(g)], min_val=0, max_val=NB - 1)
        dve.wait_ge(added, n.count(2 * PAIR, n.q * PAIR + g + 1 + PAIR))
        dst = acc[:, ds(b, 1), 0:width]
        dve.tensor_tensor(dst, dst, place(banks, g, width).unsqueeze(1), op).then_inc(added, 1)


def wait_added(eng, n, added):
    eng.wait_ge(added, n.count(2 * PAIR, n.q * PAIR + 1))


def place(banks, g, width):
    if not isinstance(banks, list):
        return banks[:, g * width:(g + 1) * width]
    return banks[g][:, 0:width]


def compgcn_pass(nc, m, a, layer, table):
    with Stage(nc, f"gcn{layer}") as st:
        g = Gather(nc, m, st, table, DIM)
        rel_loaded, ids_loaded = st.sem("rel_loaded"), st.pair("ids_loaded")
        rel_hot, rel_rows = st.pair("rel_hot"), st.pair("rel_rows")
        comp_made, hot_made, msg_made = st.pair("comp"), st.pair("edge_hot"), st.pair("msg")
        summed, added = st.pair("summed"), st.sem("added")
        rel = st.sb("rel", [HALF_REL, DIM])
        ids = st.pair_sb("ids", [HALF_REL, BATCH * P])
        rhot = st.pair_sb("rhot", [HALF_REL, BATCH * P])
        comp = st.pair_sb("comp_s", [P, BATCH, DIM])
        hot = st.pair_sb("hot", [P, BATCH, P])
        msg = st.pair_sb("msg_s", [P, BATCH, 2 * DIM])
        rel_ps, sum_ps = m.ps[0:2], m.ps[2:4]
        with nc.Block() as block:
            @block.gpsimd
            def _(pool):
                g.program(pool, comp_made)

            @block.sync
            def _(sp):
                def load_ids(n):
                    sp.wait_ge(rel_hot[n.q], n.count(1, 1))
                    sp.dma_start(ids[n.q][:, :], m.rel_rows[n.group(size=PAIR), :].rearrange("g e -> (g e)")
                                 .partition_broadcast(HALF_REL)).then_inc(ids_loaded[n.q], 16)

                sp.dma_start(rel[:, :], a["L0_gnn_rel_emb"][layer, 0:HALF_REL, :]).then_inc(rel_loaded, 16)
                pipeline(sp, (0, load_ids))

            @block.vector
            def _(dve):
                def relation_hot(n):
                    q = n.q
                    dve.wait_ge(ids_loaded[q], n.count(16, 16))
                    dve.wait_ge(rel_rows[q], n.count(1, 1))
                    dve.tensor_scalar(rhot[q][:, :], ids[q][:, :], m.iota_col[0:HALF_REL, 0:1], None, ALU.is_equal)\
                        .then_inc(rel_hot[q], 1)

                def messages(n):
                    q = n.q
                    make_hot(dve, m, n, hot, summed, hot_made)
                    dve.wait_ge(rel_rows[q], n.count(1, 2))
                    g.wait(dve, n)
                    dve.tensor_tensor(comp[q][:, :, :], g.rows[q][:, :, :],
                                      rel_ps[q][:, :].rearrange("p (b d) -> p b d", b=BATCH), ALU.mult)\
                        .then_inc(comp_made[q], 1)
                    dve.wait_ge(comp_made[q], n.count(1, 2))
                    for half, w in ((0, m.w_fwd), (1, m.w_bwd)):
                        dve.tensor_tensor(msg[q][:, :, half * DIM:(half + 1) * DIM], comp[q][:, :, :],
                                          spread(w[:, n.items()], DIM), ALU.mult).then_inc(msg_made[q], 1)

                def adds(n):
                    dve.wait_ge(summed[n.q], n.count(1, 2))
                    add_groups(dve, m, n, sum_ps[n.q], 2 * DIM, added, m.acc)

                dve.memset(m.acc[:, :, :], 0.0).then_inc(added, 1)
                dve.sem_inc(added, PAIR)
                for q in range(2):
                    dve.sem_inc(rel_hot[q], 1)
                    dve.sem_inc(comp_made[q], 1)
                pipeline(dve, (0, relation_hot), (1, messages), (3, adds))

            @block.tensor
            def _(pe):
                def relation_rows(n):
                    q = n.q
                    pe.wait_ge(rel_hot[q], n.count(1, 2))
                    pe.wait_ge(comp_made[q], n.count(1, 1))
                    for j in range(BATCH):
                        ins = pe.matmul(rel_ps[q][:, j * DIM:(j + 1) * DIM], rhot[q][:, j * P:(j + 1) * P], rel[:, :],
                                        start=True, stop=True)
                    ins.then_inc(rel_rows[q], 1)

                def sums(n):
                    q = n.q
                    pe.wait_ge(hot_made[q], n.count(1, 1))
                    pe.wait_ge(msg_made[q], n.count(2, 2))
                    wait_added(pe, n, added)
                    sum_groups(pe, hot[q], msg[q], sum_ps[q], 2 * DIM, summed[q])

                for q in range(2):
                    pe.sem_inc(rel_rows[q], 1)
                    pe.sem_inc(summed[q], 1)
                pe.wait_ge(rel_loaded, 16)
                pipeline(pe, (0, relation_rows), (2, sums))


def write_table(sp, table, tile, width, stored, ahead, written):
    with sp.Fori(0, NB) as b:
        sp.wait_ge(stored, b + (1 + ahead))
        sp.dma_start(table[ds(b * P, P), :].unsqueeze(1), tile[:, ds(b, 1), 0:width]).then_inc(written, 16)
    sp.wait_ge(written, 16 * NB)


def compgcn_nodes(nc, m, a, layer, x, y):
    with Stage(nc, f"gcn_nodes{layer}") as st:
        loaded, staged, turned = st.sem("loaded"), st.sem("staged"), st.sem("turned")
        evacuated, product, stored, written = st.sem("evacuated"), st.sem("product"), st.sem("stored"), st.sem("written")
        w_agg, w_loop = st.sb("w_agg", [P, DIM]), st.sb("w_loop", [DIM, DIM])
        first = st.sb("first", [P, 1])
        flat, tall, tall_x = st.sb("flat", [P, 3 * DIM]), st.sb("tall", [P, P]), st.sb("tall_x", [DIM, P])
        agg_t, x_t, res = m.ps[0], m.ps[1], m.ps[2]
        with nc.Block() as block:
            @block.sync
            def _(sp):
                sp.dma_start(w_agg[0:DIM, :], a["L0_gnn_w_fwd"][layer]).then_inc(loaded, 16)
                sp.dma_start(w_agg[DIM:P, :], a["L0_gnn_w_bwd"][layer]).then_inc(loaded, 16)
                sp.dma_start(w_loop[:, :], a["L0_gnn_w_loop"][layer]).then_inc(loaded, 16)
                if layer == 0:
                    write_table(sp, m.x_table, y, DIM, stored, 1, written)

            @block.vector
            def _(dve):
                with dve.Fori(0, NB) as b:
                    dve.wait_ge(turned, b + 1)
                    dve.tensor_copy(flat[:, 0:P].unsqueeze(1), m.acc[:, ds(b, 1), 0:P]).then_inc(staged, 1)
                    dve.tensor_copy(flat[:, P:3 * DIM].unsqueeze(1), x[:, ds(b, 1), :]).then_inc(staged, 1)

            @block.tensor
            def _(pe):
                pe.sem_inc(turned, 1)
                pe.sem_inc(product, 1)
                pe.wait_ge(loaded, 48)
                with pe.Fori(0, NB) as b:
                    pe.wait_ge(staged, b * 2 + 2)
                    pe.wait_ge(evacuated, b * 2 + 1)
                    pe.transpose(agg_t[:, 0:P], flat[:, 0:P], m.ident[:, :])
                    pe.transpose(x_t[0:DIM, 0:P], flat[:, P:3 * DIM], m.ident[:, :]).then_inc(turned, 1)
                    pe.wait_ge(evacuated, b * 2 + 3)
                    pe.wait_ge(stored, b + 1)
                    pe.matmul(res[:, 0:DIM], tall[:, :], w_agg[:, :], start=True, stop=False)
                    pe.matmul(res[:, 0:DIM], tall_x[:, :], w_loop[:, :], start=False, stop=True).then_inc(product, 1)

            @block.scalar
            def _(act):
                act.sem_inc(evacuated, 1)
                act.sem_inc(stored, 1)
                act.activation(first[:, :], m.ones[:, 0:1], ACT.Relu)
                with act.Fori(0, NB) as b:
                    act.wait_ge(turned, b + 2)
                    act.wait_ge(product, b + 1)
                    act.activation(tall[:, :], agg_t[:, 0:P], ACT.Copy).then_inc(evacuated, 1)
                    act.activation(tall_x[:, :], x_t[0:DIM, 0:P], ACT.Copy).then_inc(evacuated, 1)
                    act.wait_ge(product, b + 2)
                    act.activation(y[:, ds(b, 1), :], res[:, 0:DIM].unsqueeze(1), ACT.Relu).then_inc(stored, 1)


def residual_norm(nc, m, y):
    with Stage(nc, f"norm{m.norms}") as st:
        m.norms += 1
        step, rooted = st.sem("step"), st.sem("rooted")
        sq = st.sb("sq", [P, NB, DIM])
        mean, var = st.sb("mean", [P, NB]), st.sb("var", [P, NB])
        x = m.x[:, :, :]
        with nc.Block() as block:
            @block.vector
            def _(dve):
                n = [0]

                def then(ins):
                    n[0] += 1
                    ins.then_inc(step, 1)
                    dve.wait_ge(step, n[0])

                then(dve.tensor_tensor(x, x, y[:, :, :], ALU.add))
                then(dve.tensor_reduce(mean[:, :], x, AX.X, ALU.add))
                then(dve.tensor_single_scalar(mean[:, :], mean[:, :], 1.0 / DIM, ALU.mult))
                then(dve.tensor_tensor(x, x, spread(mean[:, :], DIM), ALU.subtract))
                then(dve.tensor_tensor(sq[:, :, :], x, x, ALU.mult))
                then(dve.tensor_reduce(var[:, :], sq[:, :, :], AX.X, ALU.add))
                then(dve.tensor_scalar(var[:, :], var[:, :], 1.0 / DIM, 1e-5, ALU.mult, ALU.add))
                dve.wait_ge(rooted, 1)
                then(dve.reciprocal(var[:, :], var[:, :]))
                dve.tensor_tensor(x, x, spread(var[:, :], DIM), ALU.mult)

            @block.scalar
            def _(act):
                act.wait_ge(step, 7)
                act.activation(var[:, :], var[:, :], ACT.Sqrt).then_inc(rooted, 1)


def project_nodes(nc, m, name, parts, tile, table, table_width):
    width = len(parts) * DIM
    per = CHUNK // width
    spans = [(i, min(per, ROUND - i)) for i in range(0, ROUND, per)]
    with Stage(nc, name) as st:
        loaded, padded, staged, turned = st.sem("loaded"), st.sem("padded"), st.sem("staged"), st.sem("turned")
        evacuated, product, stored, written = st.sem("evacuated"), st.sem("product"), st.sem("stored"), st.sem("written")
        w, bias = st.sb("w", [DIM, width]), st.sb("bias", [P, width])
        flat, tall = st.sb("flat", [P, ROUND, P]), st.sb("tall", [DIM, ROUND * P])
        turn_ps, res = m.ps[0:2], m.ps[2:2 + len(spans)]
        with nc.Block() as block:
            @block.sync
            def _(sp):
                for i, (weight, shift) in enumerate(parts):
                    part = slice(i * DIM, (i + 1) * DIM)
                    sp.dma_start(w[:, part], weight).then_inc(loaded, 16)
                    sp.dma_start(bias[:, part], shift.partition_broadcast(P)).then_inc(loaded, 16)
                with sp.Fori(0, NB // ROUND) as r:
                    sp.wait_ge(stored, r + 1)
                    sp.dma_start(table[ds(r * (ROUND * P), ROUND * P), :].rearrange("(i p) d -> p i d", p=P),
                                 tile[:, ds(r * ROUND, ROUND), 0:table_width]).then_inc(written, 16)
                sp.wait_ge(written, 16 * (NB // ROUND))

            @block.vector
            def _(dve):
                dve.memset(flat[:, :, :], 0.0).then_inc(padded, 1)
                dve.wait_ge(padded, 1)
                dve.wait_ge(loaded, 32 * len(parts))
                with dve.Fori(0, NB // ROUND) as r:
                    dve.wait_ge(turned, r + 1)
                    dve.tensor_copy(flat[:, :, 0:DIM], m.x[:, ds(r * ROUND, ROUND), :]).then_inc(staged, 1)
                    dve.wait_ge(product, r + 2)
                    for bank, (i, size) in zip(res, spans):
                        ins = dve.tensor_tensor(tile[:, ds(r * ROUND + i, size), :],
                                                bank[:, 0:size * width].rearrange("p (i d) -> p i d", d=width),
                                                repeat(bias[:, :], size), ALU.add)
                    ins.then_inc(stored, 1)

            @block.tensor
            def _(pe):
                pe.sem_inc(turned, 1)
                pe.sem_inc(product, 1)
                pe.wait_ge(loaded, 32 * len(parts))
                with pe.Fori(0, NB // ROUND) as r:
                    pe.wait_ge(staged, r + 1)
                    pe.wait_ge(evacuated, r + 1)
                    for i in range(ROUND):
                        at = (i * P) % CHUNK
                        ins = pe.transpose(turn_ps[i * P // CHUNK][:, at:at + P], flat[:, i, :], m.ident[:, :])
                    ins.then_inc(turned, 1)
                    pe.wait_ge(evacuated, r + 2)
                    for bank, (i, size) in zip(res, spans):
                        for k in range(size):
                            ins = pe.matmul(bank[:, k * width:(k + 1) * width], tall[:, (i + k) * P:(i + k + 1) * P], w[:, :],
                                            start=True, stop=True)
                    ins.then_inc(product, 1)

            @block.scalar
            def _(act):
                act.sem_inc(evacuated, 1)
                with act.Fori(0, NB // ROUND) as r:
                    act.wait_ge(turned, r + 2)
                    act.wait_ge(product, r + 1)
                    act.activation(tall[:, 0:CHUNK], turn_ps[0][0:DIM, :], ACT.Copy)
                    act.activation(tall[:, CHUNK:ROUND * P], turn_ps[1][0:DIM, 0:ROUND * P - CHUNK], ACT.Copy).then_inc(evacuated, 1)


def message_tables(nc, m, a):
    parts = [(a["L1_gnn_msg_w1"][l, 0:DIM, :], a["L1_gnn_msg_b1"][l]) for l in range(2)]
    with Stage(nc, "msg_tab") as st:
        project_nodes(nc, m, "msg_project", parts, st.sb("pre", [P, NB, 2 * DIM]), m.pre_table, 2 * DIM)


def load_attr(sp, m, attr, sorted_attr, tile, turned, loaded, *more):
    def load(source):
        def part(n):
            sp.wait_ge(turned[n.q], n.count(1, 1))
            for g in range(PAIR):
                e = sp.value_load(m.first_tab[0:1, n.group(g)], min_val=0, max_val=E - GE)
                sp.dma_start(tile[n.q][:, g * GROUP:(g + 1) * GROUP, :],
                             source[ds(e, GE), :].rearrange("(j p) d -> p j d", p=P)).then_inc(loaded[n.q], 16)
        return part

    with sp.If(is_unsorted(sp, m) > 0):
        pipeline(sp, *more, (0, load(sorted_attr)))
    with sp.Else():
        pipeline(sp, *more, (0, load(attr)))


def message_pass(nc, m, a):
    HID, ED = 2 * DIM, 32
    with Stage(nc, "msg") as st:
        g = Gather(nc, m, st, m.pre_table, HID)
        w_zeroed, w_loaded, attr_loaded = st.sem("w_zeroed"), st.sem("w_loaded"), st.pair("attr_loaded")
        turned, evacuated, edge_part = st.pair("turned"), st.pair("evacuated"), st.pair("edge_part")
        pre_made, msg_made, hot_made = st.pair("pre"), st.pair("msg"), st.pair("edge_hot")
        summed, added = st.pair("summed"), st.sem("added")
        w = st.sb("w", [P, GROUP * HID])
        attr = st.pair_sb("attr", [P, BATCH, ED])
        attr_t = st.pair_sb("attr_t", [P, PAIR * P])
        pre = st.pair_sb("pre_s", [P, BATCH, HID])
        msg = st.pair_sb("msg_s", [P, BATCH, HID + 1])
        hot = st.pair_sb("hot", [P, BATCH, P])
        turn_ps, edge_ps, sum_ps = m.ps[0:2], [m.ps[2:4], m.ps[4:6]], m.ps[6:8]
        with nc.Block() as block:
            @block.gpsimd
            def _(pool):
                g.program(pool, pre_made, per=PAIR)

            @block.sync
            def _(sp):
                sp.wait_ge(w_zeroed, 1)
                for l in range(2):
                    for j in range(GROUP):
                        col = j * HID + l * DIM
                        sp.dma_start(w[j * ED:(j + 1) * ED, col:col + DIM], a["L1_gnn_msg_w1"][l, DIM:DIM + ED, :])\
                          .then_inc(w_loaded, 16)
                load_attr(sp, m, a["edge_attr_32"], m.sorted_attr_32, attr, turned, attr_loaded)

            @block.scalar
            def _(act):
                def keep(n):
                    q = n.q
                    act.wait_ge(turned[q], n.count(1, 2))
                    act.wait_ge(edge_part[q], n.count(1, 1))
                    act.activation(attr_t[q][:, :], turn_ps[q][:, 0:PAIR * P], ACT.Copy).then_inc(evacuated[q], 1)

                def rectify(n):
                    q = n.q
                    act.wait_ge(pre_made[q], n.count(PAIR, 2 * PAIR))
                    act.wait_ge(summed[q], n.count(1, 1))
                    act.activation(msg[q][:, :, 0:HID], pre[q][:, :, :], ACT.Relu).then_inc(msg_made[q], 1)

                for q in range(2):
                    act.sem_inc(evacuated[q], 1)
                pipeline(act, (0, keep), (1, rectify))

            @block.vector
            def _(dve):
                def preactivations(n):
                    q = n.q
                    make_hot(dve, m, n, hot, summed, hot_made)
                    dve.wait_ge(edge_part[q], n.count(1, 2))
                    dve.wait_ge(msg_made[q], n.count(1, 1))
                    g.wait(dve, n)
                    for i in range(PAIR):
                        part = slice(i * GROUP, (i + 1) * GROUP)
                        dve.tensor_tensor(pre[q][:, part, :], g.rows[q][:, part, :],
                                          edge_ps[q][i][:, :].rearrange("p (j d) -> p j d", j=GROUP), ALU.add)\
                            .then_inc(pre_made[q], 1)

                def adds(n):
                    dve.wait_ge(summed[n.q], n.count(1, 2))
                    add_groups(dve, m, n, sum_ps[n.q], HID + 1, added, m.acc)

                dve.memset(w[:, :], 0.0).then_inc(w_zeroed, 1)
                dve.memset(m.acc[:, :, :], 0.0).then_inc(added, 1)
                dve.sem_inc(added, PAIR)
                for q in range(2):
                    dve.memset(msg[q][:, :, HID:HID + 1], 1.0).then_inc(msg_made[q], 1)
                    dve.sem_inc(pre_made[q], PAIR)
                pipeline(dve, (1, preactivations), (3, adds))

            @block.tensor
            def _(pe):
                def turn(n):
                    q = n.q
                    pe.wait_ge(attr_loaded[q], n.count(16 * PAIR, 16 * PAIR))
                    pe.wait_ge(evacuated[q], n.count(1, 1))
                    for i in range(PAIR):
                        ins = pe.transpose(turn_ps[q][:, i * P:(i + 1) * P],
                                           attr[q][:, i * GROUP:(i + 1) * GROUP, :].rearrange("p j d -> p (j d)"), m.ident[:, :])
                    ins.then_inc(turned[q], 1)

                def edge_products(n):
                    q = n.q
                    pe.wait_ge(evacuated[q], n.count(1, 2))
                    pe.wait_ge(pre_made[q], n.count(PAIR, PAIR))
                    for i in range(PAIR):
                        ins = pe.matmul(edge_ps[q][i][:, :], attr_t[q][:, i * P:(i + 1) * P], w[:, :], start=True, stop=True)
                    ins.then_inc(edge_part[q], 1)

                def sums(n):
                    q = n.q
                    pe.wait_ge(hot_made[q], n.count(1, 1))
                    pe.wait_ge(msg_made[q], n.count(1, 2))
                    wait_added(pe, n, added)
                    sum_groups(pe, hot[q], msg[q], sum_ps[q], HID + 1, summed[q])

                for q in range(2):
                    pe.sem_inc(turned[q], 1)
                    pe.sem_inc(edge_part[q], 1)
                    pe.sem_inc(summed[q], 1)
                pe.wait_ge(w_loaded, 2 * GROUP * 16)
                pipeline(pe, (0, turn), (2, sums), (0, edge_products))


def message_nodes(nc, m, a):
    with Stage(nc, "msg_nodes") as st:
        loaded, biased, rated = st.sem("loaded"), st.sem("biased"), st.sem("rated")
        staged, turned, evac, agged = st.sem("staged"), st.sem("turned"), st.sem("evacuated"), st.sem("agg")
        divided, joined, joined_t = st.sem("divided"), st.sem("joined"), st.sem("joined_t")
        hidden_ps, hidden, updated, stored = st.sem("hidden_ps"), st.sem("hidden"), st.sem("updated"), st.sem("stored")
        w2, w_u1, w_u2 = st.sb("w2", [P, DIM]), st.sb("w_u1", [P, DIM]), st.sb("w_u2", [DIM, DIM])
        b2, b2b, b_u1, b_u2 = st.sb("b2", [P, DIM]), st.sb("b2b", [P, DIM]), st.sb("b_u1", [DIM, 1]), st.sb("b_u2", [P, DIM])
        rate, bias_sum = st.sb("rate", [P, NB]), st.sb("bias_sum", [P, NB, DIM])
        y = st.sb("y", [P, NB, DIM])
        flat, tall, agg_s = st.sb("flat", [P, ROUND, P]), st.sb("tall", [P, ROUND * P]), st.sb("agg_s", [P, ROUND, DIM])
        both, both_t, hid = st.sb("both", [P, ROUND, P]), st.sb("both_t", [P, ROUND * P]), st.sb("hid", [DIM, ROUND * P])
        t_ps, agg_ps, bt_ps, h_ps, u_ps = m.ps[0:2], m.ps[2], m.ps[3:5], m.ps[5:7], m.ps[7]
        deg = m.acc[:, :, 2 * DIM:2 * DIM + 1].rearrange("p b o -> p (b o)")
        spans = [(0, CHUNK), (CHUNK, ROUND * P - CHUNK)]
        by_block = lambda bank: bank[:, 0:ROUND * DIM].rearrange("p (i d) -> p i d", d=DIM)
        with nc.Block() as block:
            @block.sync
            def _(sp):
                sp.dma_start(w2[:, :], a["L1_gnn_msg_w2"].rearrange("l i o -> (l i) o")).then_inc(loaded, 16)
                sp.dma_start(b2[:, :], a["L1_gnn_msg_b2"][0].partition_broadcast(P)).then_inc(loaded, 16)
                sp.dma_start(b2b[:, :], a["L1_gnn_msg_b2"][1].partition_broadcast(P)).then_inc(loaded, 16)
                sp.dma_start(w_u1[:, :], a["L1_gnn_upd_w1"]).then_inc(loaded, 16)
                sp.dma_start(w_u2[:, :], a["L1_gnn_upd_w2"]).then_inc(loaded, 16)
                sp.dma_start(b_u1[:, :], a["L1_gnn_upd_b1"].unsqueeze(1)).then_inc(loaded, 16)
                sp.dma_start(b_u2[:, :], a["L1_gnn_upd_b2"].partition_broadcast(P)).then_inc(loaded, 16)

            @block.vector
            def _(dve):
                dve.wait_ge(loaded, 16 * 7)
                dve.tensor_tensor(b2[:, :], b2[:, :], b2b[:, :], ALU.add).then_inc(biased, 1)
                dve.tensor_single_scalar(rate[:, :], deg, 1e-8, ALU.add).then_inc(rated, 1)
                dve.wait_ge(rated, 1)
                dve.reciprocal(rate[:, :], rate[:, :]).then_inc(rated, 1)
                dve.wait_ge(biased, 1)
                dve.tensor_tensor(bias_sum[:, :, :], spread(deg, DIM), repeat(b2[:, :], NB), ALU.mult).then_inc(biased, 1)
                dve.wait_ge(biased, 2)
                dve.wait_ge(rated, 2)
                with dve.Fori(0, NB // ROUND) as r:
                    blocks = ds(r * ROUND, ROUND)
                    dve.wait_ge(turned, r + 1)
                    dve.tensor_copy(flat[:, :, :], m.acc[:, blocks, 0:P]).then_inc(staged, 1)
                    dve.wait_ge(joined_t, r + 1)
                    dve.tensor_copy(both[:, :, 0:DIM], m.x[:, blocks, :]).then_inc(joined, 1)
                    dve.wait_ge(agged, r + 1)
                    dve.tensor_tensor(agg_s[:, :, :], bias_sum[:, blocks, :], by_block(agg_ps), ALU.add).then_inc(divided, 1)
                    dve.wait_ge(divided, r + 1)
                    dve.tensor_tensor(both[:, :, DIM:P], agg_s[:, :, :], spread(rate[:, blocks], DIM), ALU.mult).then_inc(joined, 1)
                    dve.wait_ge(updated, r + 1)
                    dve.tensor_tensor(y[:, blocks, :], by_block(u_ps), repeat(b_u2[:, :], ROUND), ALU.add).then_inc(stored, 1)

            @block.tensor
            def _(pe):
                def turn(banks, tile):
                    for i in range(ROUND):
                        at = (i * P) % CHUNK
                        ins = pe.transpose(banks[i * P // CHUNK][:, at:at + P], tile[:, i, :], m.ident[:, :])
                    return ins

                pe.sem_inc(turned, 1)
                pe.sem_inc(joined_t, 1)
                pe.wait_ge(loaded, 16 * 7)
                with pe.Fori(0, NB // ROUND) as r:
                    pe.wait_ge(staged, r + 1)
                    turn(t_ps, flat).then_inc(turned, 1)
                    pe.wait_ge(evac, r * 2 + 1)
                    for i in range(ROUND):
                        ins = pe.matmul(agg_ps[:, i * DIM:(i + 1) * DIM], tall[:, i * P:(i + 1) * P], w2[:, :], start=True, stop=True)
                    ins.then_inc(agged, 1)
                    pe.wait_ge(joined, r * 2 + 2)
                    turn(bt_ps, both).then_inc(joined_t, 1)
                    pe.wait_ge(evac, r * 2 + 2)
                    for bank, (at, size) in zip(h_ps, spans):
                        ins = pe.matmul(bank[0:DIM, 0:size], w_u1[:, :], both_t[:, at:at + size], start=True, stop=True)
                    ins.then_inc(hidden_ps, 1)
                    pe.wait_ge(hidden, r + 1)
                    pe.wait_ge(stored, r + 1)
                    for i in range(ROUND):
                        ins = pe.matmul(u_ps[:, i * DIM:(i + 1) * DIM], hid[:, i * P:(i + 1) * P], w_u2[:, :], start=True, stop=True)
                    ins.then_inc(updated, 1)

            @block.scalar
            def _(act):
                act.sem_inc(stored, 1)
                with act.Fori(0, NB // ROUND) as r:
                    act.wait_ge(turned, r + 2)
                    for bank, (at, size) in zip(t_ps, spans):
                        ins = act.activation(tall[:, at:at + size], bank[:, 0:size], ACT.Copy)
                    ins.then_inc(evac, 1)
                    act.wait_ge(joined_t, r + 2)
                    for bank, (at, size) in zip(bt_ps, spans):
                        ins = act.activation(both_t[:, at:at + size], bank[:, 0:size], ACT.Copy)
                    ins.then_inc(evac, 1)
                    act.wait_ge(hidden_ps, r + 1)
                    for bank, (at, size) in zip(h_ps, spans):
                        ins = act.activation(hid[:, at:at + size], bank[0:DIM, 0:size], ACT.Relu, bias=b_u1[:, 0:1])
                    ins.then_inc(hidden, 1)
        residual_norm(nc, m, y)


MAGIC = 12582912.0
TURN = 2.0 * np.pi
TURN_HI = float(np.float32(6.28125))
TURN_MID = float(np.float32(TURN - 6.28125))
TURN_LO = float(np.float32(TURN - 6.28125 - float(np.float32(TURN - 6.28125))))


def diffusion_embed(nc, m, a, cur):
    with Stage(nc, "embed") as st:
        loaded, padded, step, sined = st.sem("loaded"), st.sem("padded"), st.sem("step"), st.sem("sined")
        staged, turned, evac = st.sem("staged"), st.sem("turned"), st.sem("evacuated")
        hidden_ps, hidden, product, stored = st.sem("hidden_ps"), st.sem("hidden"), st.sem("product"), st.sem("stored")
        w_in, w1, w2 = st.sb("w_in", [DIM, P]), st.sb("w1", [P, P]), st.sb("w2", [P, P])
        b_in, b1, b2 = st.sb("b_in", [P, 1]), st.sb("b1", [P, 1]), st.sb("b2", [P, 1])
        freq = st.sb("freq", [P, 2])
        ang, rnd = st.sb("ang", [P, NP]), st.sb("rnd", [P, NP])
        flat, tall, emb = st.sb("flat", [P, P]), st.sb("tall", [DIM, P]), st.sb("emb", [P, P])
        hid = st.sb("hid", [P, P])
        t_ps, h_ps, o_ps = m.ps[0:3]
        with nc.Block() as block:
            @block.sync
            def _(sp):
                sp.wait_ge(padded, 1)
                sp.dma_start(ang[:, 0:N], a["node_vec"].partition_broadcast(P)).then_inc(loaded, 16)
                sp.dma_start(freq[:, :], a["freq"]).then_inc(loaded, 16)
                for tile, name in ((w_in, "init_w"), (w1, "te_w1"), (w2, "te_w2")):
                    sp.dma_start(tile[:, :], a["L2_gnn_" + name]).then_inc(loaded, 16)
                for tile, name in ((b_in, "init_b"), (b1, "te_b1"), (b2, "te_b2")):
                    sp.dma_start(tile[:, :], a["L2_gnn_" + name].unsqueeze(1)).then_inc(loaded, 16)

            @block.vector
            def _(dve):
                n = [0]

                def then(ins):
                    n[0] += 1
                    ins.then_inc(step, 1)
                    dve.wait_ge(step, n[0])

                dve.memset(ang[:, :], 0.0).then_inc(padded, 1)
                dve.memset(flat[:, :], 0.0).then_inc(padded, 1)
                dve.wait_ge(loaded, 16 * 8)
                dve.wait_ge(padded, 2)
                then(dve.tensor_tensor(b_in[:, :], b_in[:, :], b2[:, :], ALU.add))
                then(dve.tensor_single_scalar(ang[:, :], ang[:, :], freq[:, 0:1], ALU.mult))
                then(dve.tensor_scalar(rnd[:, :], ang[:, :], freq[:, 1:2], None, ALU.add))
                then(dve.tensor_scalar(rnd[:, :], rnd[:, :], 1.0 / TURN, MAGIC, ALU.mult, ALU.add))
                then(dve.tensor_single_scalar(rnd[:, :], rnd[:, :], -MAGIC, ALU.add))
                for part in (TURN_HI, TURN_MID, TURN_LO):
                    then(dve.scalar_tensor_tensor(ang[:, :], rnd[:, :], -part, ang[:, :], ALU.mult, ALU.add))
                then(dve.tensor_scalar(ang[:, :], ang[:, :], freq[:, 1:2], None, ALU.add))
                then(dve.tensor_scalar(ang[:, :], ang[:, :], 3.1415925, -3.1415925, ALU.min, ALU.max))
                dve.wait_ge(sined, 1)
                dve.sem_inc(stored, 1)
                with dve.Fori(0, NB) as b:
                    dve.wait_ge(product, b + 1)
                    dve.tensor_copy(flat[:, 0:DIM].unsqueeze(1), m.x[:, ds(b, 1), :]).then_inc(staged, 1)
                    dve.tensor_copy(emb[:, :], rnd[:, ds(b * P, P)]).then_inc(staged, 1)
                    dve.wait_ge(turned, b + 1)
                    dve.tensor_copy(tall[:, :], t_ps[0:DIM, 0:P]).then_inc(evac, 1)
                    dve.wait_ge(product, b + 2)
                    dve.tensor_scalar(cur[:, 0, ds(b * P, P)], o_ps[:, 0:P], b_in[:, 0:1], None, ALU.add).then_inc(stored, 1)

            @block.scalar
            def _(act):
                act.wait_ge(step, 10)
                act.activation(rnd[:, :], ang[:, :], ACT.Sin).then_inc(sined, 1)
                with act.Fori(0, NB) as b:
                    act.wait_ge(hidden_ps, b + 1)
                    act.wait_ge(product, b + 1)
                    act.activation(hid[:, :], h_ps[:, 0:P], ACT.Silu, bias=b1[:, 0:1]).then_inc(hidden, 1)

            @block.tensor
            def _(pe):
                pe.sem_inc(product, 1)
                pe.wait_ge(loaded, 16 * 8)
                with pe.Fori(0, NB) as b:
                    pe.wait_ge(staged, b * 2 + 2)
                    pe.transpose(t_ps[:, 0:P], flat[:, :], m.ident[:, :]).then_inc(turned, 1)
                    pe.matmul(h_ps[:, 0:P], w1[:, :], emb[:, :], start=True, stop=True).then_inc(hidden_ps, 1)
                    pe.wait_ge(evac, b + 1)
                    pe.wait_ge(hidden, b + 1)
                    pe.wait_ge(stored, b + 1)
                    pe.matmul(o_ps[:, 0:P], w_in[:, :], tall[:, :], start=True, stop=False)
                    pe.matmul(o_ps[:, 0:P], w2[:, :], hid[:, :], start=False, stop=True).then_inc(product, 1)


def gat_shape(layer):
    return (1, 2, 2)[layer], (256, 256, 128)[layer]


def gat_tables(nc, m, a, layer, cur):
    kt, width = gat_shape(layer)
    c, full = width // HEADS, width + 2 * HEADS
    with Stage(nc, f"gat_tab{layer}") as st:
        loaded, folded, staged = st.sem("loaded"), st.sem("folded"), st.sem("staged")
        product, stored, kept, written, step = st.sem("product"), st.sem("stored"), st.sem("kept"), st.sem("written"), st.sem("step")
        w = st.sb("w", [P, kt, full])
        att = st.sb("att", [P, 2, width])
        prod = st.sb("prod", [P, width])
        flat = st.pair_sb("flat", [P, kt, P])
        o_ps = m.ps[0:2]
        table = m.xw_table if width == 256 else m.xw_table2
        with nc.Block() as block:
            @block.sync
            def _(sp):
                sp.dma_start(w[:, :, 0:width], a[f"L2_gnn_gat_w{layer}"].rearrange("(k p) o -> p k o", p=P)).then_inc(loaded, 16)
                for i, name in enumerate(("src", "dst")):
                    sp.dma_start(att[:, i, :], a[f"L2_gnn_att_{name}{layer}"].rearrange("h c -> (h c)").partition_broadcast(P))\
                      .then_inc(loaded, 16)
                write_table(sp, table, m.node_out, width + HEADS, stored, 2, written)
                sp.dma_start(m.al_table.rearrange("(b p) d -> p b d", p=P), m.node_out[:, :, width:width + HEADS])\
                  .then_inc(written, 16)
                sp.wait_ge(written, 16 * (NB + 1))

            @block.vector
            def _(dve):
                n = [0]

                def then(ins):
                    n[0] += 1
                    ins.then_inc(step, 1)
                    dve.wait_ge(step, n[0])

                dve.wait_ge(loaded, 48)
                for k in range(kt):
                    for i in range(2):
                        then(dve.tensor_tensor(prod[:, :], w[:, k, 0:width], att[:, i, :], ALU.mult))
                        then(dve.tensor_reduce(w[:, k, width + HEADS * i:width + HEADS * (i + 1)],
                                               prod[:, :].rearrange("p (h c) -> p h c", h=HEADS), AX.X, ALU.add))
                dve.sem_inc(folded, 1)

                def stage(b, q):
                    dve.wait_ge(product, b + 1)
                    dve.tensor_copy(flat[q][:, :, :], cur[:, 0:kt, ds(b * P, P)]).then_inc(staged, 1)

                blocks_by_two(dve, stage)
                dve.wait_ge(stored, NB + 2)
                dve.tensor_copy(m.dst_tab[:, :, 0:HEADS], m.node_out[:, :, width + HEADS:full])

            @block.scalar
            def _(act):
                def keep(b, q):
                    act.wait_ge(product, b + 3)
                    act.activation(m.node_out[:, ds(b, 1), 0:full], o_ps[q][:, 0:full].unsqueeze(1), ACT.Copy).then_inc(stored, 1)

                act.sem_inc(stored, 2)
                blocks_by_two(act, keep)

            @block.tensor
            def _(pe):
                def products(b, q):
                    pe.wait_ge(stored, b + 1)
                    pe.wait_ge(staged, b + 1)
                    for k in range(kt):
                        ins = pe.matmul(o_ps[q][:, 0:full], flat[q][:, k, :], w[:, k, :], start=k == 0, stop=k == kt - 1)
                    ins.then_inc(product, 1)

                pe.sem_inc(product, 2)
                pe.wait_ge(folded, 1)
                blocks_by_two(pe, products)


def gat_max_pass(nc, m, layer):
    with Stage(nc, f"gat_max{layer}") as st:
        g = Gather(nc, m, st, m.al_table, HEADS)
        runs_loaded, turned, scanned, turned_back = (st.pair(s) for s in ("runs_loaded", "turned", "scanned", "turned_back"))
        ends_made, hot_made, picked, penal = (st.pair(s) for s in ("ends", "edge_hot", "picked", "penalty"))
        offered, best, added, passed = st.pair("offered"), st.pair("best"), st.sem("added"), st.sem("turn_passed")
        ROWS = BATCH * HEADS
        runs = st.pair_sb("runs", [ROWS, P])
        run_max = st.pair_sb("run_max", [ROWS, P])
        ends = st.pair_sb("ends_s", [P, BATCH, HEADS + 1])
        hot = st.pair_sb("hot", [P, BATCH, P])
        pen = st.pair_sb("pen", [P, BATCH])
        cand = st.pair_sb("cand", [P, BATCH, HEADS])
        top = st.pair_sb("top", [P, PAIR * HEADS])
        turn_ps, back_ps, pick_ps = m.ps[0:2], m.ps[2:4], m.ps[4:6]
        with nc.Block() as block:
            @block.gpsimd
            def _(pool):
                g.program(pool, turned)

            @block.sync
            def _(sp):
                def load_runs(n):
                    sp.wait_ge(scanned[n.q], n.count(1, 1))
                    sp.dma_start(runs[n.q][:, :], m.run_rows[n.group(size=PAIR), :].rearrange("g (j e) -> (g j) e", e=P)
                                 .unsqueeze(1).to_broadcast([BATCH, HEADS, P])).then_inc(runs_loaded[n.q], 16)

                pipeline(sp, (0, load_runs))

            @block.vector
            def _(dve):
                def scan(n):
                    q = n.q
                    dve.wait_ge(runs_loaded[q], n.count(16, 16))
                    dve.wait_ge(turned_back[q], n.count(1, 1))
                    dve.wait_ge(turned[q], n.count(1, 2))
                    dve.tensor_tensor_scan(run_max[q][:, :], runs[q][:, :], turn_ps[q][0:ROWS, 0:P], FAR, ALU.add, ALU.max)\
                        .then_inc(scanned[q], 1)

                def run_ends(n):
                    q = n.q
                    make_hot(dve, m, n, hot, picked, hot_made)
                    last = m.run_end[:, n.items()]
                    dve.tensor_copy(ends[q][:, :, HEADS:HEADS + 1], last.unsqueeze(2)).then_inc(ends_made[q], 1)
                    dve.wait_ge(turned_back[q], n.count(1, 2))
                    dve.tensor_tensor(ends[q][:, :, 0:HEADS], back_ps[q][:, 0:ROWS].rearrange("p (b h) -> p b h", b=BATCH),
                                      spread(last, HEADS), ALU.mult).then_inc(ends_made[q], 1)

                def maxima(n):
                    q = n.q
                    view = pick_ps[q][:, 0:BATCH * (HEADS + 1)].rearrange("p (b h) -> p b h", b=BATCH)
                    dve.wait_ge(picked[q], n.count(1, 2))
                    dve.tensor_scalar(pen[q][:, :].unsqueeze(2), view[:, :, HEADS:HEADS + 1], -1.0, -FAR, ALU.add, ALU.mult)\
                        .then_inc(penal[q], 1)
                    dve.wait_ge(penal[q], n.count(1, 1))
                    dve.tensor_tensor(cand[q][:, :, :], view[:, :, 0:HEADS], spread(pen[q][:, :], HEADS), ALU.add)\
                        .then_inc(offered[q], 1)
                    dve.wait_ge(offered[q], n.count(1, 2))
                    wait_added(dve, n, added)
                    for i in range(PAIR):
                        dve.tensor_reduce(top[q][:, i * HEADS:(i + 1) * HEADS],
                                          cand[q][:, i * GROUP:(i + 1) * GROUP, :].rearrange("p j h -> p h j"), AX.X, ALU.max)\
                            .then_inc(best[q], 1)
                    dve.wait_ge(best[q], n.count(PAIR, PAIR))
                    add_groups(dve, m, n, top[q], HEADS, added, m.al_max, ALU.max)

                dve.memset(m.al_max[:, :, :], FAR).then_inc(added, 1)
                dve.sem_inc(added, PAIR)
                for q in range(2):
                    dve.sem_inc(scanned[q], 1)
                    dve.sem_inc(ends_made[q], 2)
                    dve.sem_inc(offered[q], 1)
                pipeline(dve, (0, scan), (1, run_ends), (2, maxima))

            @block.tensor
            def _(pe):
                def turn(n):
                    q = n.q
                    pe.wait_ge(scanned[q], n.count(1, 1))
                    g.wait(pe, n)
                    pe.sem_inc(passed, 1)
                    pe.transpose(turn_ps[q][0:ROWS, 0:P], g.rows[q][:, :, :].rearrange("p b h -> p (b h)"),
                                 m.ident[:, :]).then_inc(turned[q], 1)

                def turn_back(n):
                    q = n.q
                    pe.wait_ge(ends_made[q], n.count(2, 2))
                    pe.wait_ge(scanned[q], n.count(1, 2))
                    pe.matmul(back_ps[q][:, 0:ROWS], run_max[q][:, :], m.ident[0:ROWS, 0:ROWS], start=True,
                              stop=True).then_inc(turned_back[q], 1)

                def pick(n):
                    q = n.q
                    pe.wait_ge(hot_made[q], n.count(1, 1))
                    pe.wait_ge(ends_made[q], n.count(2, 4))
                    pe.wait_ge(offered[q], n.count(1, 1))
                    for j in range(BATCH):
                        ins = pe.matmul(pick_ps[q][:, j * (HEADS + 1):(j + 1) * (HEADS + 1)], hot[q][:, j, :], ends[q][:, j, :],
                                        start=True, stop=True)
                    ins.then_inc(picked[q], 1)

                for q in range(2):
                    pe.sem_inc(turned[q], 1)
                    pe.sem_inc(turned_back[q], 1)
                    pe.sem_inc(picked[q], 1)
                pipeline(pe, (0, turn), (1, turn_back), (2, pick))


def gat_self_loops(nc, m, layer):
    _, width = gat_shape(layer)
    with Stage(nc, f"gat_self{layer}") as st:
        step, powered = st.sem("step"), st.sem("powered")
        logit, low = st.sb("logit", [P, NB, HEADS]), st.sb("low", [P, NB, HEADS])
        al_s = m.node_out[:, :, width:width + HEADS]
        al_d, top = m.dst_tab[:, :, 0:HEADS], m.dst_tab[:, :, HEADS:2 * HEADS]
        own = m.acc[:, :, width:width + HEADS]
        rest = st.sb("rest", [P, NB, 2 * HEADS])
        with nc.Block() as block:
            @block.vector
            def _(dve):
                n = [0]

                def then(ins):
                    n[0] += 1
                    ins.then_inc(step, 1)
                    dve.wait_ge(step, n[0])

                then(dve.tensor_tensor(top, m.al_max[:, :, :], al_s, ALU.max))
                then(dve.tensor_tensor(top, top, al_d, ALU.add))
                then(dve.scalar_tensor_tensor(top, top, 0.2, top, ALU.mult, ALU.max))
                then(dve.tensor_tensor(logit[:, :, :], al_s, al_d, ALU.add))
                then(dve.scalar_tensor_tensor(low[:, :, :], logit[:, :, :], 0.2, logit[:, :, :], ALU.mult, ALU.max))
                then(dve.tensor_tensor(low[:, :, :], low[:, :, :], top, ALU.subtract))
                then(dve.tensor_copy(rest[:, :, :], m.dst_tab[:, :, :]))
                for k in range(PARTS):
                    part = m.dst_parts[:, :, k * 2 * HEADS:(k + 1) * 2 * HEADS]
                    then(dve.tensor_copy(part, rest[:, :, :]))
                    if k < PARTS - 1:
                        then(dve.tensor_tensor(rest[:, :, :], rest[:, :, :], part, ALU.subtract))
                dve.wait_ge(powered, 1)
                for h in range(HEADS):
                    c = width // HEADS
                    dve.tensor_tensor(m.acc[:, :, h * c:(h + 1) * c], m.node_out[:, :, h * c:(h + 1) * c],
                                      spread(m.acc[:, :, width + h:width + h + 1].rearrange("p b o -> p (b o)"), c), ALU.mult)

            @block.scalar
            def _(act):
                act.wait_ge(step, 6)
                act.activation(own, low[:, :, :], ACT.Exp).then_inc(powered, 1)


def gat_sum_pass(nc, m, layer):
    _, width = gat_shape(layer)
    c, full = width // HEADS, width + HEADS
    with Stage(nc, f"gat_sum{layer}") as st:
        g = Gather(nc, m, st, m.xw_table if width == 256 else m.xw_table2, full)
        dst_loaded, dst_far, dst_hot, dst_rows = (st.pair(s) for s in ("dst_loaded", "dst_far", "dst_hot", "dst_rows"))
        joined, logit, leaky, shifted, powered = (st.pair(s) for s in ("joined", "logit", "leaky", "shifted", "powered"))
        msg_made, hot_made, summed, added = st.pair("msg"), st.pair("edge_hot"), st.pair("summed"), st.sem("added")
        negated = st.sem("negated")
        minus_row = st.sb("minus_row", [P, 1])
        dst = st.pair_sb("dst", [P, BATCH * P])
        dhot = st.pair_sb("dhot", [P, BATCH * P], BF16)
        drow = st.pair_sb("drow", [P, BATCH, 2 * HEADS])
        hot = st.pair_sb("hot", [P, BATCH, P])
        lg = st.pair_sb("lg", [P, BATCH, HEADS])
        msg = st.pair_sb("msg_s", [P, BATCH, full])
        row_ps, sum_ps = m.ps[0:2], [m.ps[2:4], m.ps[4:6]]
        with nc.Block() as block:
            @block.gpsimd
            def _(pool):
                g.program(pool, msg_made)

            @block.sync
            def _(sp):
                pipeline(sp, (0, lambda n: load_dst(sp, m, n, dst, dst_far, dst_loaded)))

            @block.scalar
            def _(act):
                def power(n):
                    q = n.q
                    act.wait_ge(shifted[q], n.count(1, 2))
                    act.wait_ge(summed[q], n.count(1, 1))
                    act.activation(msg[q][:, :, width:full], lg[q][:, :, :], ACT.Exp).then_inc(powered[q], 1)

                for q in range(2):
                    act.sem_inc(dst_far[q], 1)
                act.wait_ge(negated, 1)
                pipeline(act, (0, lambda n: make_dst_hot(act, m, n, dst, minus_row, dst_loaded, dst_rows, dst_far, dst_hot, dhot)),
                         (1, power))

            @block.vector
            def _(dve):
                def logits(n):
                    q = n.q
                    dve.wait_ge(dst_rows[q], n.count(1, 2))
                    dve.wait_ge(shifted[q], n.count(1, 1))
                    dve.tensor_reduce(drow[q][:, :, :], row_ps[q][:, 0:BATCH * PARTS * 2 * HEADS]
                                      .rearrange("p (b k h) -> p b h k", b=BATCH, k=PARTS), AX.X, ALU.add).then_inc(joined[q], 1)
                    dve.wait_ge(joined[q], n.count(1, 2))
                    g.wait(dve, n)
                    dve.tensor_tensor(lg[q][:, :, :], g.rows[q][:, :, width:full], drow[q][:, :, 0:HEADS], ALU.add)\
                        .then_inc(logit[q], 1)
                    dve.wait_ge(logit[q], n.count(1, 1))
                    dve.scalar_tensor_tensor(lg[q][:, :, :], lg[q][:, :, :], 0.2, lg[q][:, :, :], ALU.mult, ALU.max)\
                        .then_inc(leaky[q], 1)
                    dve.wait_ge(leaky[q], n.count(1, 1))
                    dve.tensor_tensor(lg[q][:, :, :], lg[q][:, :, :], drow[q][:, :, HEADS:2 * HEADS], ALU.subtract)\
                        .then_inc(shifted[q], 1)

                def messages(n):
                    q = n.q
                    make_hot(dve, m, n, hot, summed, hot_made)
                    dve.wait_ge(powered[q], n.count(1, 1))
                    dve.tensor_tensor(msg[q][:, :, 0:width].rearrange("p b (h c) -> p b h c", c=c),
                                      g.rows[q][:, :, 0:width].rearrange("p b (h c) -> p b h c", c=c),
                                      msg[q][:, :, width:full].unsqueeze(3).to_broadcast([P, BATCH, HEADS, c]), ALU.mult)\
                        .then_inc(msg_made[q], 1)

                def adds(n):
                    dve.wait_ge(summed[n.q], n.count(1, 2))
                    add_groups(dve, m, n, sum_ps[n.q], full, added, m.acc)

                dve.tensor_single_scalar(minus_row[:, :], m.iota_col[:, :], -1.0, ALU.mult).then_inc(negated, 1)
                dve.sem_inc(added, 1 + PAIR)
                for q in range(2):
                    dve.sem_inc(msg_made[q], 1)
                    dve.sem_inc(shifted[q], 1)
                    dve.sem_inc(joined[q], 1)
                pipeline(dve, (1, logits), (1, messages), (3, adds))

            @block.tensor
            def _(pe):
                def rows(n):
                    q = n.q
                    pe.wait_ge(dst_hot[q], n.count(1, 1))
                    pe.wait_ge(joined[q], n.count(1, 1))
                    destination_gather(pe, m, n, dhot[q], m.dst_parts, PARTS * 2 * HEADS, row_ps[q], dst_rows[q])

                def sums(n):
                    q = n.q
                    pe.wait_ge(hot_made[q], n.count(1, 1))
                    pe.wait_ge(msg_made[q], n.count(1, 2))
                    wait_added(pe, n, added)
                    sum_groups(pe, hot[q], msg[q], sum_ps[q], full, summed[q])

                for q in range(2):
                    pe.sem_inc(dst_rows[q], 1)
                    pe.sem_inc(summed[q], 1)
                pipeline(pe, (0, rows), (2, sums))


def destination_gather(pe, m, n, dhot, table, width, bank, done):
    for g in range(PAIR):
        b = pe.value_load(m.block_tab[0:1, n.group(g)], min_val=0, max_val=NB - 1)
        for j in range(g * GROUP, (g + 1) * GROUP):
            ins = pe.matmul(bank[:, j * width:(j + 1) * width], dhot[:, j * P:(j + 1) * P],
                            table[:, ds(b, 1), :].rearrange("p o w -> p (o w)"), start=True, stop=True)
    ins.then_inc(done, 1)


def gat_nodes(nc, m, a, layer, cur, nxt):
    kt, width = gat_shape(layer)
    ot, c = width // P, width // HEADS
    chunks = [(i, min(CHUNK, N - i)) for i in range(0, N, CHUNK)]
    with Stage(nc, f"gat_nodes{layer}") as st:
        loaded, step, inverted, staged = st.sem("loaded"), st.sem("step"), st.sem("inverted"), st.sem("staged")
        product, stored, rooted = st.sem("product"), st.sem("stored"), st.sem("rooted")
        adj = st.sb("adj", [P, kt, width])
        bias, bias2, gain, shift = (st.sb(n, [P, ot]) for n in ("bias", "bias2", "gain", "shift"))
        rden = st.sb("rden", [P, NB, HEADS])
        flat = st.pair_sb("flat", [P, width])
        stats, agg = st.sb("stats", [P, ot, len(chunks), 6]), st.sb("agg", [P, ot, 2])
        std = st.sb("std", [P, ot])
        o_ps = m.ps[0:2]
        columns = lambda name: a[f"L2_gnn_{name}{layer}"].rearrange("(k p) -> p k", p=P)
        with nc.Block() as block:
            @block.sync
            def _(sp):
                sp.dma_start(adj[:, :, :], a[f"L2_gnn_adj_w{layer}"].rearrange("(k p) o -> p k o", p=P)).then_inc(loaded, 16)
                with nc.allow_non_contiguous_dma(reason="four short vectors"):
                    for tile, name in ((bias, "gat_b"), (bias2, "adj_b"), (gain, "bn_g"), (shift, "bn_b")):
                        sp.dma_start(tile[:, :], columns(name)).then_inc(loaded, 16)

            @block.vector
            def _(dve):
                n = [0]

                def then(ins):
                    n[0] += 1
                    ins.then_inc(step, 1)
                    dve.wait_ge(step, n[0])

                dve.wait_ge(loaded, 16 * 5)
                then(dve.tensor_tensor(bias[:, :], bias[:, :], bias2[:, :], ALU.add))
                then(dve.reciprocal(rden[:, :, :], m.acc[:, :, width:width + HEADS]))

                def divide(b, q):
                    dve.wait_ge(product, b + 1)
                    dve.tensor_tensor(flat[q][:, :].rearrange("p (h c) -> p h c", c=c),
                                      m.acc[:, ds(b, 1), 0:width].rearrange("p o (h c) -> p (o h) c", c=c),
                                      spread(rden[:, ds(b, 1), :].rearrange("p o h -> p (o h)"), c), ALU.mult).then_inc(staged, 1)

                blocks_by_two(dve, divide)
                dve.wait_ge(stored, NB + 2)
                for o in range(ot):
                    for i, (at, size) in enumerate(chunks):
                        ins = dve.bn_stats(stats[:, o, i, :], nxt[:, o, at:at + size])
                    then(ins)
                    then(dve.bn_aggr(agg[:, o, :], stats[:, o, :, :].rearrange("p i s -> p (i s)")))
                then(dve.tensor_scalar(std[:, :].unsqueeze(2), agg[:, :, 1:2], 1e-5, None, ALU.add))
                dve.sem_inc(inverted, 1)
                dve.wait_ge(rooted, 1)
                then(dve.reciprocal(std[:, :], std[:, :]))
                then(dve.tensor_tensor(gain[:, :], gain[:, :], std[:, :], ALU.mult))
                then(dve.tensor_tensor(std[:, :].unsqueeze(2), agg[:, :, 0:1], gain[:, :].unsqueeze(2), ALU.mult))
                then(dve.tensor_tensor(shift[:, :], shift[:, :], std[:, :], ALU.subtract))
                dve.sem_inc(inverted, 1)

            @block.scalar
            def _(act):
                def keep(b, q):
                    act.wait_ge(product, b + 3)
                    for o in range(ot):
                        ins = act.activation(nxt[:, o, ds(b * P, P)], o_ps[q][:, o * P:(o + 1) * P], ACT.Identity, bias=bias[:, o:o + 1])
                    ins.then_inc(stored, 1)

                act.sem_inc(stored, 2)
                act.wait_ge(step, 2)
                blocks_by_two(act, keep)
                act.wait_ge(inverted, 1)
                act.activation(std[:, :], std[:, :], ACT.Sqrt).then_inc(rooted, 1)
                act.wait_ge(inverted, 2)
                for o in range(ot):
                    act.activation(nxt[:, o, :], nxt[:, o, :], ACT.Silu, bias=shift[:, o:o + 1], scale=gain[:, o:o + 1])

            @block.tensor
            def _(pe):
                def products(b, q):
                    pe.wait_ge(stored, b + 1)
                    pe.wait_ge(staged, b + 1)
                    for o in range(ot):
                        pe.matmul(o_ps[q][:, o * P:(o + 1) * P], flat[q][:, o * P:(o + 1) * P], m.ident[:, :], start=True, stop=False)
                        for k in range(kt):
                            ins = pe.matmul(o_ps[q][:, o * P:(o + 1) * P], adj[:, k, o * P:(o + 1) * P], cur[:, k, ds(b * P, P)],
                                            start=False, stop=k == kt - 1)
                    ins.then_inc(product, 1)

                pe.sem_inc(product, 2)
                pe.wait_ge(loaded, 16 * 5)
                blocks_by_two(pe, products)


def diffusion_out(nc, m, a, cur):
    with Stage(nc, "gat_out") as st:
        loaded, staged, product, stored = st.sem("loaded"), st.sem("staged"), st.sem("product"), st.sem("stored")
        w, bias, flat, y = st.sb("w", [P, DIM]), st.sb("bias", [P, DIM]), st.sb("flat", [P, P]), st.sb("y", [P, NB, DIM])
        o_ps = m.ps[0]
        with nc.Block() as block:
            @block.sync
            def _(sp):
                sp.dma_start(w[:, :], a["L2_gnn_out_w"]).then_inc(loaded, 16)
                sp.dma_start(bias[:, :], a["L2_gnn_out_b"].partition_broadcast(P)).then_inc(loaded, 16)

            @block.scalar
            def _(act):
                with act.Fori(0, NB) as b:
                    act.wait_ge(product, b + 1)
                    act.activation(flat[:, :], cur[:, 0, ds(b * P, P)], ACT.Copy).then_inc(staged, 1)

            @block.vector
            def _(dve):
                dve.sem_inc(stored, 1)
                dve.wait_ge(loaded, 32)
                with dve.Fori(0, NB) as b:
                    dve.wait_ge(product, b + 2)
                    dve.tensor_tensor(y[:, ds(b, 1), :], o_ps[:, 0:DIM].unsqueeze(1), bias[:, :].unsqueeze(1), ALU.add)\
                        .then_inc(stored, 1)

            @block.tensor
            def _(pe):
                pe.sem_inc(product, 1)
                pe.wait_ge(loaded, 32)
                with pe.Fori(0, NB) as b:
                    pe.wait_ge(staged, b + 1)
                    pe.wait_ge(stored, b + 1)
                    pe.matmul(o_ps[:, 0:DIM], flat[:, :], w[:, :], start=True, stop=True).then_inc(product, 1)
        residual_norm(nc, m, y)


def attention_tables(nc, m, a):
    parts = [(a[f"L3_gnn_W{k}"], a[f"L3_gnn_b{k}"]) for k in "KVQ"]
    project_nodes(nc, m, "att_project", parts, m.kvq, m.pre_table, 2 * DIM)


def attention_pass(nc, m, a):
    d = DIM // HEADS
    scale = float(np.float32(1.0 / np.sqrt(d)))
    TWOS = BATCH // 2
    with Stage(nc, "att") as st:
        g = Gather(nc, m, st, m.pre_table, 2 * DIM)
        w_zeroed, w_loaded, attr_loaded = st.sem("w_zeroed"), st.sem("w_loaded"), st.pair("attr_loaded")
        dst_loaded, dst_far, dst_hot, dst_rows = (st.pair(s) for s in ("dst_loaded", "dst_far", "dst_hot", "dst_rows"))
        turned, evacuated, edge_part = st.pair("turned"), st.pair("evacuated"), st.pair("edge_part")
        eb, kq, kqe, score, scaled, clipped, powered = (st.pair(s) for s in ("eb", "kq", "kqe", "score", "scaled", "clipped", "powered"))
        msg_made, hot_made, summed, added = st.pair("msg"), st.pair("edge_hot"), st.pair("summed"), st.sem("added")
        negated = st.sem("negated")
        w = st.sb("w", [P, P])
        bias = st.sb("bias", [P, DIM])
        minus_row = st.sb("minus_row", [P, 1])
        attr = st.pair_sb("attr", [P, BATCH, DIM])
        attr_t = st.pair_sb("attr_t", [P, TWOS * P])
        dst = st.pair_sb("dst", [P, BATCH * P])
        dhot = st.pair_sb("dhot", [P, BATCH * P])
        hot = st.pair_sb("hot", [P, BATCH, P])
        prod = st.pair_sb("prod", [P, BATCH, DIM])
        edge = st.pair_sb("edge", [P, BATCH, DIM])
        sc = st.pair_sb("sc", [P, BATCH * HEADS])
        e = st.pair_sb("e", [P, BATCH * HEADS])
        msg = st.pair_sb("msg_s", [P, BATCH, DIM])
        turn_ps, edge_ps, row_ps, sum_ps = m.ps[0:2], m.ps[2:4], m.ps[4:6], m.ps[6:8]
        by_item = lambda bank: bank[:, :].rearrange("p (b d) -> p b d", d=DIM)
        with nc.Block() as block:
            @block.gpsimd
            def _(pool):
                g.program(pool, msg_made)

            @block.sync
            def _(sp):
                sp.wait_ge(w_zeroed, 1)
                for i in range(2):
                    part = slice(i * DIM, (i + 1) * DIM)
                    sp.dma_start(w[part, part], a["L3_gnn_WE"]).then_inc(w_loaded, 16)
                sp.dma_start(bias[:, :], a["L3_gnn_bE"].partition_broadcast(P)).then_inc(w_loaded, 16)
                load_attr(sp, m, a["edge_attr_64"], m.sorted_attr_64, attr, turned, attr_loaded,
                          (0, lambda n: load_dst(sp, m, n, dst, dst_far, dst_loaded)))

            @block.scalar
            def _(act):
                def keep(n):
                    q = n.q
                    act.wait_ge(turned[q], n.count(1, 2))
                    act.wait_ge(edge_part[q], n.count(1, 1))
                    act.activation(attr_t[q][:, :], turn_ps[q][:, :], ACT.Copy).then_inc(evacuated[q], 1)

                def power(n):
                    q = n.q
                    act.wait_ge(clipped[q], n.count(1, 1))
                    act.wait_ge(msg_made[q], n.count(1, 1))
                    act.activation(e[q][:, :], sc[q][:, :], ACT.Exp).then_inc(powered[q], 1)

                for q in range(2):
                    act.sem_inc(evacuated[q], 1)
                    act.sem_inc(dst_far[q], 1)
                act.wait_ge(negated, 1)
                pipeline(act, (0, keep), (1, power),
                         (0, lambda n: make_dst_hot(act, m, n, dst, minus_row, dst_loaded, dst_rows, dst_far, dst_hot, dhot)))

            @block.vector
            def _(dve):
                def scores(n):
                    q = n.q
                    make_hot(dve, m, n, hot, summed, hot_made)
                    dve.wait_ge(edge_part[q], n.count(1, 2))
                    dve.tensor_tensor(edge[q][:, :, :], by_item(edge_ps[q]), repeat(bias[:, :], BATCH), ALU.add).then_inc(eb[q], 1)
                    dve.wait_ge(dst_rows[q], n.count(1, 2))
                    g.wait(dve, n)
                    dve.tensor_tensor(prod[q][:, :, :], g.rows[q][:, :, 0:DIM], by_item(row_ps[q]), ALU.mult).then_inc(kq[q], 1)
                    dve.wait_ge(eb[q], n.count(1, 2))
                    dve.wait_ge(kq[q], n.count(1, 2))
                    dve.tensor_tensor(prod[q][:, :, :], prod[q][:, :, :], edge[q][:, :, :], ALU.mult).then_inc(kqe[q], 1)
                    dve.wait_ge(kqe[q], n.count(1, 1))
                    dve.tensor_reduce(sc[q][:, :], prod[q][:, :, :].rearrange("p b (h d) -> p (b h) d", d=d), AX.X, ALU.add)\
                        .then_inc(score[q], 1)
                    dve.wait_ge(score[q], n.count(1, 1))
                    dve.tensor_scalar(sc[q][:, :], sc[q][:, :], scale, 5.0, ALU.mult, ALU.min).then_inc(scaled[q], 1)
                    dve.wait_ge(scaled[q], n.count(1, 1))
                    dve.tensor_single_scalar(sc[q][:, :], sc[q][:, :], -5.0, ALU.max).then_inc(clipped[q], 1)

                def messages(n):
                    q = n.q
                    dve.wait_ge(powered[q], n.count(1, 1))
                    dve.tensor_tensor(msg[q][:, :, :].rearrange("p b (h d) -> p (b h) d", d=d),
                                      g.rows[q][:, :, DIM:2 * DIM].rearrange("p b (h d) -> p b h d", d=d),
                                      spread(e[q][:, :], d), ALU.mult).then_inc(msg_made[q], 1)

                def adds(n):
                    dve.wait_ge(summed[n.q], n.count(1, 2))
                    add_groups(dve, m, n, sum_ps[n.q], DIM, added, m.acc)

                dve.memset(w[:, :], 0.0).then_inc(w_zeroed, 1)
                dve.tensor_single_scalar(minus_row[:, :], m.iota_col[:, :], -1.0, ALU.mult).then_inc(negated, 1)
                dve.memset(m.acc[:, :, :], 0.0).then_inc(added, 1)
                dve.sem_inc(added, PAIR)
                for q in range(2):
                    for s in (msg_made, eb, kq):
                        dve.sem_inc(s[q], 1)
                dve.wait_ge(w_loaded, 48)
                pipeline(dve, (1, scores), (3, adds), (1, messages))

            @block.tensor
            def _(pe):
                def turn(n):
                    q = n.q
                    pe.wait_ge(attr_loaded[q], n.count(16 * PAIR, 16 * PAIR))
                    pe.wait_ge(evacuated[q], n.count(1, 1))
                    for i in range(TWOS):
                        ins = pe.transpose(turn_ps[q][:, i * P:(i + 1) * P],
                                           attr[q][:, 2 * i:2 * i + 2, :].rearrange("p b d -> p (b d)"), m.ident[:, :])
                    ins.then_inc(turned[q], 1)

                def edge_products(n):
                    q = n.q
                    pe.wait_ge(evacuated[q], n.count(1, 2))
                    pe.wait_ge(eb[q], n.count(1, 1))
                    for i in range(TWOS):
                        ins = pe.matmul(edge_ps[q][:, i * P:(i + 1) * P], attr_t[q][:, i * P:(i + 1) * P], w[:, :],
                                        start=True, stop=True)
                    ins.then_inc(edge_part[q], 1)

                def rows(n):
                    q = n.q
                    pe.wait_ge(dst_hot[q], n.count(1, 1))
                    pe.wait_ge(kq[q], n.count(1, 1))
                    destination_gather(pe, m, n, dhot[q], m.kvq[:, :, 2 * DIM:3 * DIM], DIM, row_ps[q], dst_rows[q])

                def sums(n):
                    q = n.q
                    pe.wait_ge(hot_made[q], n.count(1, 1))
                    pe.wait_ge(msg_made[q], n.count(1, 2))
                    wait_added(pe, n, added)
                    sum_groups(pe, hot[q], msg[q], sum_ps[q], DIM, summed[q])

                for q in range(2):
                    for s in (turned, dst_rows, edge_part, summed):
                        pe.sem_inc(s[q], 1)
                pe.wait_ge(w_loaded, 48)
                pipeline(pe, (0, turn), (2, sums), (0, edge_products), (0, rows))


_NAMES = ["L0_gnn_rel_emb", "L0_gnn_w_loop", "L0_gnn_w_fwd", "L0_gnn_w_bwd", "x", "edge_attr_32", "edge_attr_64",
          "node_vec", "L1_gnn_msg_w1", "L1_gnn_msg_b1", "L1_gnn_msg_w2", "L1_gnn_msg_b2",
          "L1_gnn_upd_w1", "L1_gnn_upd_b1", "L1_gnn_upd_w2", "L1_gnn_upd_b2",
          "L2_gnn_init_w", "L2_gnn_init_b", "L2_gnn_te_w1", "L2_gnn_te_b1", "L2_gnn_te_w2", "L2_gnn_te_b2",
          "L2_gnn_out_w", "L2_gnn_out_b"]
_NAMES += [f"L2_gnn_{n}{i}" for i in range(3)
           for n in ("gat_w", "att_src", "att_dst", "gat_b", "adj_w", "adj_b", "bn_g", "bn_b")]
_NAMES += [f"L3_gnn_{k}{n}" for n in "QKEV" for k in "Wb"]


def kernel(**inputs):
    import concourse.bacc as bacc
    from concourse.bass_utils import run_bass_kernel_spmd

    nc = bacc.Bacc("TRN2", target_bir_lowering=False, num_devices=1)
    arrays = {n: np.ascontiguousarray(inputs[n]) for n in _NAMES}
    arrays["edges"] = np.stack([np.asarray(inputs["src"]), np.asarray(inputs["dst"]), np.asarray(inputs["edge_type_200"]),
                                np.asarray(inputs["edge_weight"]).view(np.int32)])
    half = P // 2
    freq = np.power(np.float32(1.0 / 10000.0), np.arange(half, dtype=np.float32) / np.float32(half)).astype(np.float32)
    phase = np.repeat(np.array([0.0, np.pi / 2], np.float32), half)
    arrays["freq"] = np.stack([np.concatenate([freq, freq]), phase], axis=1)
    a = {n: nc.dram_tensor(f"in_{n}", v.shape, mybir.dt.from_np(v.dtype), kind="ExternalInput").ap()
         for n, v in arrays.items()}
    out = nc.dram_tensor("out", (N, DIM), F32, kind="ExternalOutput").ap()
    build(nc, a, out)
    r = run_bass_kernel_spmd(nc, [{f"in_{n}": v for n, v in arrays.items()}], core_ids=[0])
    return r.results[0]["out"]
```
